# Optimizing a Trainium2 kernel written in Bass

```python
import numpy as np
import jax
import jax.numpy as jnp

def _softmax(x, axis=-1):
    return jax.nn.softmax(x, axis=axis)

def _gelu(x):
    return jax.nn.gelu(x, approximate=True)

def _silu(x):
    return jax.nn.silu(x)

def _sigmoid(x):
    return jax.nn.sigmoid(x)

def _layernorm(x, axis=-1, eps=1e-05):
    m = jnp.mean(x, axis=axis, keepdims=True)
    v = jnp.var(x, axis=axis, keepdims=True)
    return (x - m) / jnp.sqrt(v + eps)

def _scatter_add(tgt, idx, src, axis=0):
    return tgt.at[idx].add(src)

def _segment_sum(src, seg, n):
    return jax.ops.segment_sum(src, seg, n)
kernel_name = 'mk_flamingo_gated_d2_seqx_r4_bbfdb1'

def setup_inputs(seed: int=0):
    np.random.seed(seed)
    _w = jnp.asarray

    def _rec_inputs():
        import jax
        import jax.numpy as jnp
        _rk = jax.random.key(seed)
        x = -0.0002928 + 1 * jax.random.normal(jax.random.fold_in(_rk, 1), (16, 256, 256), jnp.float32)
        _lenS = 256 - jax.random.randint(jax.random.fold_in(_rk, 7), (16,), 0, max(1, 256 // 4) + 1, jnp.int32)
        _lenS2 = 77 - jax.random.randint(jax.random.fold_in(_rk, 8), (16,), 0, max(1, 77 // 4) + 1, jnp.int32)
        _ctx_1024P = jax.random.normal(jax.random.fold_in(_rk, 11), (16, 16, 256), jnp.float32)
        _ctx_1024c = jax.random.dirichlet(jax.random.fold_in(_rk, 511), 0.3 * jnp.ones((16,), jnp.float32), (16, 77))
        _ctx_1024t = jnp.einsum('bsk,bkd->bsd', _ctx_1024c, _ctx_1024P)
        _ctx_1024t = _ctx_1024t * jax.lax.rsqrt(jnp.mean(jnp.square(_ctx_1024t)) + 1e-12) * 0.953939
        ctx_1024 = -0.000191848 + 0.999787 * (_ctx_1024t + 0.3 * jax.random.normal(jax.random.fold_in(_rk, 611), (16, 77, 256), jnp.float32))
        _g = jax.random.normal(jax.random.fold_in(_rk, 9001), (2, 2), jnp.float32)
        _g = jnp.sign(_g) * jnp.maximum(jnp.abs(_g), 1.0) + (_g == 0) * 1.0
        g_xattn = _g[0]
        g_ffn = _g[1]
        return (x, ctx_1024, g_xattn, g_ffn)
    x, ctx_1024, g_xattn, g_ffn = _rec_inputs()

    def _L0_xattn_setup():
        import jax, jax.numpy as jnp
        import numpy as np
        D_MODEL = 256
        NUM_HEADS = 16
        DEPTH = D_MODEL // NUM_HEADS
        key = jax.random.key(seed)
        ks = jax.random.split(key, 10)
        B, T, C = (2, 512, 768)
        s = 1.0 / np.sqrt(D_MODEL)
        inp = {'x': jax.random.normal(ks[0], (B, T, D_MODEL), dtype=jnp.float32), 'context': jax.random.normal(ks[1], (B, C, D_MODEL), dtype=jnp.float32), 'Wq': jax.random.normal(ks[2], (D_MODEL, D_MODEL), dtype=jnp.float32) * s, 'bq': jnp.zeros((D_MODEL,), dtype=jnp.float32), 'Wk': jax.random.normal(ks[3], (D_MODEL, D_MODEL), dtype=jnp.float32) * s, 'bk': jnp.zeros((D_MODEL,), dtype=jnp.float32), 'Wv': jax.random.normal(ks[4], (D_MODEL, D_MODEL), dtype=jnp.float32) * s, 'bv': jnp.zeros((D_MODEL,), dtype=jnp.float32), 'Wo': jax.random.normal(ks[5], (D_MODEL, D_MODEL), dtype=jnp.float32) * s, 'bo': jnp.zeros((D_MODEL,), dtype=jnp.float32)}
        return inp
    _L0_xattn_all = _L0_xattn_setup()
    _L0_xattn_in = {k: v for k, v in _L0_xattn_all.items() if k in ('Wq', 'bq', 'Wk', 'bk', 'Wv', 'bv', 'Wo', 'bo')}
    del _L0_xattn_all

    def _L0_ffn_setup():
        import jax, jax.numpy as jnp
        import numpy as np
        BLOCK = 32
        W_BITS = 4
        ACT_BITS = 16

        def act_qdq(x):
            qmax = 2.0 ** (ACT_BITS - 1) - 1.0
            scale = jnp.maximum(jnp.max(jnp.abs(x)) / qmax, 1e-12)
            return jnp.clip(jnp.round(x / scale), -qmax - 1.0, qmax) * scale

        def fixed_qdq_u16(x):
            scale = 1.0 / 65536.0
            return jnp.clip(jnp.round(x / scale), 0.0, 65535.0) * scale

        def lpbq_dequant(w):
            O, I = w.shape
            qmax = 2.0 ** (W_BITS - 1) - 1.0
            wb = w.reshape(O, I // BLOCK, BLOCK)
            s = jnp.maximum(jnp.max(jnp.abs(wb), axis=-1, keepdims=True) / qmax, 1e-12)
            wq = jnp.clip(jnp.round(wb / s), -qmax - 1.0, qmax) * s
            return wq.reshape(O, I)
        key = jax.random.key(seed)
        k1, k2, k3, k4 = jax.random.split(key, 4)
        B, S, H, I = (2, 1024, 256, 768)
        x = jax.random.normal(k1, (B, S, H), jnp.float32)
        w_gate = jax.random.normal(k2, (I, H), jnp.float32) * 0.02
        w_up = jax.random.normal(k3, (I, H), jnp.float32) * 0.02
        w_down = jax.random.normal(k4, (H, I), jnp.float32) * 0.02
        return {'x': x, 'w_gate': w_gate, 'w_up': w_up, 'w_down': w_down}
    _L0_ffn_all = _L0_ffn_setup()
    _L0_ffn_in = {k: v for k, v in _L0_ffn_all.items() if k in ('w_gate', 'w_up', 'w_down')}
    del _L0_ffn_all

    def _L1_xattn_setup():
        import jax, jax.numpy as jnp
        import numpy as np
        B, N, M = (2, 512, 512)
        Q_DIM = 256
        HEADS = 8
        DIM_HEAD = 64
        INNER = HEADS * DIM_HEAD
        key = jax.random.key(seed)
        ks = jax.random.split(key, 7)
        s_in = 1.0 / np.sqrt(Q_DIM)
        s_out = 1.0 / np.sqrt(INNER)
        return {'x': jax.random.normal(ks[0], (B, N, Q_DIM), dtype=jnp.float32), 'context': jax.random.normal(ks[1], (B, M, Q_DIM), dtype=jnp.float32), 'Wq': jax.random.normal(ks[2], (Q_DIM, INNER), dtype=jnp.float32) * s_in, 'Wk': jax.random.normal(ks[3], (Q_DIM, INNER), dtype=jnp.float32) * s_in, 'Wv': jax.random.normal(ks[4], (Q_DIM, INNER), dtype=jnp.float32) * s_in, 'Wo': jax.random.normal(ks[5], (INNER, Q_DIM), dtype=jnp.float32) * s_out, 'bo': jax.random.normal(ks[6], (Q_DIM,), dtype=jnp.float32) * 0.01}
    _L1_xattn_all = _L1_xattn_setup()
    _L1_xattn_in = {k: v for k, v in _L1_xattn_all.items() if k in ('Wq', 'Wk', 'Wv', 'Wo', 'bo')}
    del _L1_xattn_all

    def _L1_ffn_setup():
        import jax, jax.numpy as jnp
        import numpy as np
        D_MODEL = 256
        EXPANSION = 4
        D_HIDDEN = D_MODEL * EXPANSION
        NUM_STAGES = int(np.log2(D_HIDDEN))

        def butterfly(y, weights, dim):
            lead = y.shape[:-1]
            for stage in range(weights.shape[0]):
                s = 2 ** stage
                nb = dim // (2 * s)
                yr = y.reshape(*lead, nb, 2, s)
                a = yr[..., 0, :]
                b = yr[..., 1, :]
                w = weights[stage].reshape(nb, s, 2, 2)
                na = w[..., 0, 0] * a + w[..., 0, 1] * b
                nb2 = w[..., 1, 0] * a + w[..., 1, 1] * b
                y = jnp.stack([na, nb2], axis=-2).reshape(*lead, dim)
            return y
        key = jax.random.key(seed)
        ks = jax.random.split(key, 6)
        B, S = (4, 512)
        x = jax.random.normal(ks[0], (B, S, D_MODEL), jnp.float32)
        W_exp = jax.random.normal(ks[1], (D_MODEL, D_HIDDEN), jnp.float32) * 0.02
        b_exp = jnp.zeros((D_HIDDEN,), jnp.float32)
        up_weights = jax.random.normal(ks[2], (NUM_STAGES, D_HIDDEN // 2, 2, 2), jnp.float32) * 0.02
        up_bias = jnp.zeros((D_HIDDEN,), jnp.float32)
        down_weights = jax.random.normal(ks[3], (NUM_STAGES, D_HIDDEN // 2, 2, 2), jnp.float32) * 0.02
        W_con = jax.random.normal(ks[4], (D_HIDDEN, D_MODEL), jnp.float32) * 0.02
        b_con = jnp.zeros((D_MODEL,), jnp.float32)
        down_bias = jnp.zeros((D_MODEL,), jnp.float32)
        return dict(x=x, W_exp=W_exp, b_exp=b_exp, up_weights=up_weights, up_bias=up_bias, down_weights=down_weights, W_con=W_con, b_con=b_con, down_bias=down_bias)
    _L1_ffn_all = _L1_ffn_setup()
    _L1_ffn_in = {k: v for k, v in _L1_ffn_all.items() if k in ('W_exp', 'b_exp', 'up_weights', 'up_bias', 'down_weights', 'W_con', 'b_con', 'down_bias')}
    del _L1_ffn_all
    return {'x': x, 'ctx_1024': ctx_1024, 'g_xattn': g_xattn, 'g_ffn': g_ffn, 'L0_xattn_Wq': _L0_xattn_in['Wq'], 'L0_xattn_bq': _L0_xattn_in['bq'], 'L0_xattn_Wk': _L0_xattn_in['Wk'], 'L0_xattn_bk': _L0_xattn_in['bk'], 'L0_xattn_Wv': _L0_xattn_in['Wv'], 'L0_xattn_bv': _L0_xattn_in['bv'], 'L0_xattn_Wo': _L0_xattn_in['Wo'], 'L0_xattn_bo': _L0_xattn_in['bo'], 'L0_ffn_w_gate': _L0_ffn_in['w_gate'], 'L0_ffn_w_up': _L0_ffn_in['w_up'], 'L0_ffn_w_down': _L0_ffn_in['w_down'], 'L1_xattn_Wq': _L1_xattn_in['Wq'], 'L1_xattn_Wk': _L1_xattn_in['Wk'], 'L1_xattn_Wv': _L1_xattn_in['Wv'], 'L1_xattn_Wo': _L1_xattn_in['Wo'], 'L1_xattn_bo': _L1_xattn_in['bo'], 'L1_ffn_W_exp': _L1_ffn_in['W_exp'], 'L1_ffn_b_exp': _L1_ffn_in['b_exp'], 'L1_ffn_up_weights': _L1_ffn_in['up_weights'], 'L1_ffn_up_bias': _L1_ffn_in['up_bias'], 'L1_ffn_down_weights': _L1_ffn_in['down_weights'], 'L1_ffn_W_con': _L1_ffn_in['W_con'], 'L1_ffn_b_con': _L1_ffn_in['b_con'], 'L1_ffn_down_bias': _L1_ffn_in['down_bias']}

def reference(x, ctx_1024, g_xattn, g_ffn, L0_xattn_Wq, L0_xattn_bq, L0_xattn_Wk, L0_xattn_bk, L0_xattn_Wv, L0_xattn_bv, L0_xattn_Wo, L0_xattn_bo, L0_ffn_w_gate, L0_ffn_w_up, L0_ffn_w_down, L1_xattn_Wq, L1_xattn_Wk, L1_xattn_Wv, L1_xattn_Wo, L1_xattn_bo, L1_ffn_W_exp, L1_ffn_b_exp, L1_ffn_up_weights, L1_ffn_up_bias, L1_ffn_down_weights, L1_ffn_W_con, L1_ffn_b_con, L1_ffn_down_bias):
    import jax
    import jax.numpy as jnp

    def _L0_xattn_ref(x, context, Wq, bq, Wk, bk, Wv, bv, Wo, bo):
        import jax, jax.numpy as jnp
        import numpy as np
        D_MODEL = 256
        NUM_HEADS = 16
        DEPTH = D_MODEL // NUM_HEADS
        B, T, D = x.shape
        C = context.shape[1]
        H, d = (NUM_HEADS, DEPTH)
        q = x @ Wq.T + bq
        k = context @ Wk.T + bk
        v = context @ Wv.T + bv
        q = q.reshape(B, T, H, d).transpose(0, 2, 1, 3)
        k = k.reshape(B, C, H, d).transpose(0, 2, 1, 3)
        v = v.reshape(B, C, H, d).transpose(0, 2, 1, 3)
        scores = jnp.einsum('bhtd,bhcd->bhtc', q, k) / jnp.sqrt(jnp.asarray(d, x.dtype))
        attn = jax.nn.softmax(scores, axis=-1)
        out = jnp.einsum('bhtc,bhcd->bhtd', attn, v)
        out = out.transpose(0, 2, 1, 3).reshape(B, T, D)
        return out @ Wo.T + bo

    def _L0_ffn_ref(x, w_gate, w_up, w_down):
        import jax, jax.numpy as jnp
        import numpy as np
        BLOCK = 32
        W_BITS = 4
        ACT_BITS = 16

        def act_qdq(x):
            qmax = 2.0 ** (ACT_BITS - 1) - 1.0
            scale = jnp.maximum(jnp.max(jnp.abs(x)) / qmax, 1e-12)
            return jnp.clip(jnp.round(x / scale), -qmax - 1.0, qmax) * scale

        def fixed_qdq_u16(x):
            scale = 1.0 / 65536.0
            return jnp.clip(jnp.round(x / scale), 0.0, 65535.0) * scale

        def lpbq_dequant(w):
            O, I = w.shape
            qmax = 2.0 ** (W_BITS - 1) - 1.0
            wb = w.reshape(O, I // BLOCK, BLOCK)
            s = jnp.maximum(jnp.max(jnp.abs(wb), axis=-1, keepdims=True) / qmax, 1e-12)
            wq = jnp.clip(jnp.round(wb / s), -qmax - 1.0, qmax) * s
            return wq.reshape(O, I)
        x = act_qdq(x)
        up = act_qdq(x @ lpbq_dequant(w_up).T)
        gate = act_qdq(x @ lpbq_dequant(w_gate).T)
        sig = fixed_qdq_u16(jax.nn.sigmoid(gate))
        gate = act_qdq(gate * sig)
        o = act_qdq(gate * up)
        return o @ lpbq_dequant(w_down).T

    def _L1_xattn_ref(x, context, Wq, Wk, Wv, Wo, bo):
        import jax, jax.numpy as jnp
        import numpy as np
        B, N, M = (2, 512, 512)
        Q_DIM = 256
        HEADS = 8
        DIM_HEAD = 64
        INNER = HEADS * DIM_HEAD
        scale = DIM_HEAD ** (-0.5)

        def split_heads(t):
            b, n, _ = t.shape
            return t.reshape(b, n, HEADS, DIM_HEAD).transpose(0, 2, 1, 3)
        q = split_heads(x @ Wq)
        k = split_heads(context @ Wk)
        v = split_heads(context @ Wv)
        sim = jnp.einsum('bhid,bhjd->bhij', q, k) * scale
        attn = jax.nn.softmax(sim, axis=-1)
        out = jnp.einsum('bhij,bhjd->bhid', attn, v)
        out = out.transpose(0, 2, 1, 3).reshape(x.shape[0], x.shape[1], INNER)
        return out @ Wo + bo

    def _L1_ffn_ref(x, W_exp, b_exp, up_weights, up_bias, down_weights, W_con, b_con, down_bias):
        import jax, jax.numpy as jnp
        import numpy as np
        D_MODEL = 256
        EXPANSION = 4
        D_HIDDEN = D_MODEL * EXPANSION
        NUM_STAGES = int(np.log2(D_HIDDEN))

        def butterfly(y, weights, dim):
            lead = y.shape[:-1]
            for stage in range(weights.shape[0]):
                s = 2 ** stage
                nb = dim // (2 * s)
                yr = y.reshape(*lead, nb, 2, s)
                a = yr[..., 0, :]
                b = yr[..., 1, :]
                w = weights[stage].reshape(nb, s, 2, 2)
                na = w[..., 0, 0] * a + w[..., 0, 1] * b
                nb2 = w[..., 1, 0] * a + w[..., 1, 1] * b
                y = jnp.stack([na, nb2], axis=-2).reshape(*lead, dim)
            return y
        h = jnp.einsum('bsd,dh->bsh', x, W_exp) + b_exp
        h = butterfly(h, up_weights, D_HIDDEN)
        h = jax.nn.gelu(h + up_bias, approximate=False)
        h = butterfly(h, down_weights, D_HIDDEN)
        y = jnp.einsum('bsh,hd->bsd', h, W_con) + b_con
        return y + down_bias
    x = x + jnp.tanh(g_xattn[0]) * _L0_xattn_ref(_layernorm(x, axis=-1), ctx_1024, L0_xattn_Wq, L0_xattn_bq, L0_xattn_Wk, L0_xattn_bk, L0_xattn_Wv, L0_xattn_bv, L0_xattn_Wo, L0_xattn_bo)
    x = x + jnp.tanh(g_ffn[0]) * _L0_ffn_ref(_layernorm(x, axis=-1), L0_ffn_w_gate, L0_ffn_w_up, L0_ffn_w_down)
    x = x + jnp.tanh(g_xattn[1]) * _L1_xattn_ref(_layernorm(x, axis=-1), ctx_1024, L1_xattn_Wq, L1_xattn_Wk, L1_xattn_Wv, L1_xattn_Wo, L1_xattn_bo)
    x = x + jnp.tanh(g_ffn[1]) * _L1_ffn_ref(_layernorm(x, axis=-1), L1_ffn_W_exp, L1_ffn_b_exp, L1_ffn_up_weights, L1_ffn_up_bias, L1_ffn_down_weights, L1_ffn_W_con, L1_ffn_b_con, L1_ffn_down_bias)
    return x

_drawn_inputs = setup_inputs


def setup_inputs(seed=0):
    import zlib

    import numpy as np

    out = dict(_drawn_inputs(seed))
    spreads = {'g_ffn': (-1.0, 0.6),
     'L0_xattn_bq': (0.0, 0.511),
     'L0_xattn_bk': (0.0, 0.8),
     'L0_xattn_bv': (0.0, 0.1),
     'L0_xattn_bo': (0.0, 0.1),
     'L1_ffn_b_exp': (0.0, 0.1),
     'L1_ffn_up_bias': (0.0, 0.1),
     'L1_ffn_b_con': (0.0, 0.1),
     'L1_ffn_down_bias': (0.0, 0.1)}
    factors = {'L0_ffn_w_gate': 2.923, 'L0_ffn_w_up': 2.786, 'L0_ffn_w_down': 2.779, 'L1_xattn_bo': 7.066}
    for name, (base, spread) in spreads.items():
        noise = np.random.default_rng([zlib.crc32(name.encode()), seed]).standard_normal(out[name].shape)
        drawn = base * np.exp(spread * noise) if base else spread * noise
        out[name] = jnp.asarray(drawn.astype(out[name].dtype))
    for name, factor in factors.items():
        out[name] = (out[name] * factor).astype(out[name].dtype)
    return out
```

```python
from contextlib import ExitStack

import concourse.bass as bass
from concourse import mybir

F32 = mybir.dt.float32
F32R = mybir.dt.float32r
I16 = mybir.dt.int16
U16 = mybir.dt.uint16
ALU = mybir.AluOpType
ACT = mybir.ActivationFunctionType
AX = mybir.AxisListType
RMAX = bass.bass_isa.ReduceOp.max

P = 128
D = 256
DC = D // P
B = 16
T = 256
TT = T // P
S = 77
NT = B * TT
LN_EPS = 1e-5
BLOCK = 32
ACT_MAX = 32767.0
TINY = 1e-12
GT = 512
HID0 = 768
HID1 = 1024


def three_passes(nc, out, w_hi, w_lo, m_hi, m_lo, start, stop):
    nc.tensor.matmul(out, w_hi, m_hi, start=start, stop=False)
    nc.tensor.matmul(out, w_hi, m_lo, start=False, stop=False)
    return nc.tensor.matmul(out, w_lo, m_hi, start=False, stop=stop)


def free_semaphores(nc, sems):
    nc.clear_and_free_semaphores(sems)
    nc.all_engine_barrier()


def attention(nc, env, layer, heads, inner, wqkv, wo, bq, bk, bv, gbias, gate, ctx_t, x_in):
    d = inner // heads
    C = inner // P
    HPC = P // d
    HP = heads // 2
    NP = C // 2
    NG = TT * heads // 4
    DV = d + 1
    SCALE = float(d) ** -0.5
    first = x_in is not None
    xres, banks, ident = env["xres"], env["banks"], env["ident"]
    T0, T1, X0, X1, S0, S1, O0, O1 = banks
    wide = heads * DV > 512
    mx_banks = [X0] if wide else [X0, X1]
    NMX = len(mx_banks)

    def out_of(t, h):
        if wide and h == heads - 1:
            return X1[:, t * DV:(t + 1) * DV]
        return (O0, O1)[t][:, h * DV:(h + 1) * DV]

    sems = []
    ctx = ExitStack()
    with ctx:
        def sb(name, shape, dt=F32):
            return ctx.enter_context(nc.sbuf_tensor(f"a{layer}_{name}", shape, dt))

        def sem(name):
            sems.append(nc.alloc_semaphore(f"a{layer}_{name}"))
            return sems[-1]

        w_hi = sb("w_hi", [P, DC, 3 * inner], F32R)
        w_lo = sb("w_lo", [P, DC, 3 * inner], F32R)
        wo_hi = sb("wo_hi", [P, C, D], F32R)
        wo_lo = sb("wo_lo", [P, C, D], F32R)
        k_hi = sb("k_hi", [P, C, B * S], F32R)
        k_lo = sb("k_lo", [P, C, B * S], F32R)
        values = sb("values", [P, B, heads, DV])
        bqk = sb("bqk", [P, 2, C])
        bv_all = sb("bv_all", [P, inner])
        gb = sb("gb", [P, D])
        tg = sb("tg", [P, 1])
        minus_half = sb("minus_half", [P, TT])
        eps = sb("eps", [P, TT])
        head_mask = sb("head_mask", [P, HPC])
        pick = sb("pick", [P, heads, S + 1], F32R)

        setup = ExitStack()
        with setup:
            def tmp(name, shape, dt=F32):
                return setup.enter_context(nc.sbuf_tensor(f"a{layer}_{name}", shape, dt))

            w_raw = tmp("w_raw", [P, DC, 3 * inner])
            wo_raw = tmp("wo_raw", [P, C, D])
            c_raw = tmp("c_raw", [P, DC, B * S])
            c_hi = tmp("c_hi", [P, DC, B * S], F32R)
            c_lo = tmp("c_lo", [P, DC, B * S], F32R)
            bo_raw = tmp("bo_raw", [P, D])
            gate_raw = tmp("gate_raw", [P, 1])
            pick_raw = tmp("pick_raw", [P, heads, S + 1])
            w_in, c_in, o_in, small_in = sem("w_in"), sem("c_in"), sem("o_in"), sem("small_in")
            w_rounded, c_rounded, o_rounded = sem("w_rounded"), sem("c_rounded"), sem("o_rounded")
            w_split, c_split = sem("w_split"), sem("c_split")
            k_sum, k_rounded, k_done = sem("k_sum"), sem("k_rounded"), sem("k_done")
            v_sum, v_cleared, v_done, g_done = sem("v_sum"), sem("v_cleared"), sem("v_done"), sem("g_done")
            KN = [(0, 412), (412, 410), (822, 410)]
            KJ = [(c, n0, n) for c in range(C) for n0, n in KN]
            N_SMALL = 4 + (3 if first else 0)

            block = setup.enter_context(nc.Block())

            @block.sync
            def _(sp):
                sp.dma_start(w_raw[:], wqkv.rearrange("(c p) n -> p c n", p=P)).then_inc(w_in, 16)
                sp.dma_start(c_raw[:], ctx_t.rearrange("(c p) n -> p c n", p=P)).then_inc(c_in, 16)
                sp.dma_start(wo_raw[:], wo.rearrange("(c p) n -> p c n", p=P)).then_inc(o_in, 16)
                sp.dma_start(bo_raw[:], gbias).then_inc(small_in, 16)
                sp.dma_start(gate_raw[:], gate).then_inc(small_in, 16)
                sp.dma_start(head_mask[:], env[f"mask{layer}"]).then_inc(small_in, 16)
                sp.dma_start(pick_raw[:], env[f"pick{layer}"]).then_inc(small_in, 16)
                if first:
                    sp.dma_start(bqk[:, 0, :], bq).then_inc(small_in, 16)
                    sp.dma_start(bqk[:, 1, :], bk).then_inc(small_in, 16)
                    sp.dma_start(bv_all[:], bv).then_inc(small_in, 16)

            @block.gpsimd
            def _(pool):
                pool.memset(values[:], 0.0).then_inc(v_cleared, 1)
                pool.memset(minus_half[:], -0.5)
                pool.memset(eps[:], LN_EPS)
                pool.wait_ge(v_cleared, 1)
                pool.memset(values[:, :, :, d:DV], 1.0).then_inc(v_cleared, 1)

            @block.scalar
            def _(act):
                act.wait_ge(w_in, 16)
                act.activation(w_hi[:], w_raw[:], ACT.Copy).then_inc(w_rounded, 1)
                act.wait_ge(c_in, 16)
                act.activation(c_hi[:], c_raw[:], ACT.Copy).then_inc(c_rounded, 1)
                act.wait_ge(o_in, 16)
                act.activation(wo_hi[:], wo_raw[:], ACT.Copy).then_inc(o_rounded, 1)
                act.wait_ge(small_in, 16 * N_SMALL)
                act.activation(tg[:], gate_raw[:], ACT.Tanh).then_inc(g_done, 1)
                act.activation(pick[:], pick_raw[:], ACT.Copy)
                for n, (c, n0, nn) in enumerate(KJ):
                    act.wait_ge(k_sum, n + 1)
                    bias = bqk[:, 1, c:c + 1] if first else 0.0
                    act.activation(k_hi[:, c, n0:n0 + nn], (T0, T1)[n % 2][:, 0:nn], ACT.Identity,
                                   bias=bias).then_inc(k_rounded, 1)

            @block.vector
            def _(dve):
                dve.wait_ge(w_rounded, 1)
                dve.tensor_tensor(w_lo[:], w_raw[:], w_hi[:].bitcast(F32), ALU.subtract).then_inc(w_split, 1)
                dve.wait_ge(c_rounded, 1)
                dve.tensor_tensor(c_lo[:], c_raw[:], c_hi[:].bitcast(F32), ALU.subtract).then_inc(c_split, 1)
                dve.wait_ge(o_rounded, 1)
                dve.tensor_tensor(wo_lo[:], wo_raw[:], wo_hi[:].bitcast(F32), ALU.subtract)
                dve.wait_ge(g_done, 1)
                dve.tensor_scalar(gb[:], bo_raw[:], tg[:, 0:1], None, ALU.mult)
                for n, (c, n0, nn) in enumerate(KJ):
                    dve.wait_ge(k_rounded, n + 1)
                    bias = bqk[:, 1, c:c + 1] if first else 0.0
                    dve.scalar_tensor_tensor(
                        out=k_lo[:, c, n0:n0 + nn], in0=(T0, T1)[n % 2][:, 0:nn], scalar=bias,
                        in1=k_hi[:, c, n0:n0 + nn].bitcast(F32), op0=ALU.add, op1=ALU.subtract,
                    ).then_inc(k_done, 1)
                dve.wait_ge(v_cleared, 2)
                for b in range(B):
                    dve.wait_ge(v_sum, b + 1)
                    src = (S0, S1)[b % 2][0:S, 0:inner].rearrange("p (h v) -> p h v", h=heads)
                    dst = values[0:S, b, :, 0:d]
                    if first:
                        dve.tensor_tensor(dst, src, bv_all[0:S, :].rearrange("p (h v) -> p h v", h=heads),
                                          ALU.add).then_inc(v_done, 1)
                    else:
                        dve.tensor_copy(dst, src).then_inc(v_done, 1)

            @block.tensor
            def _(pe):
                pe.wait_ge(w_split, 1)
                pe.wait_ge(c_split, 1)
                for n, (c, n0, nn) in enumerate(KJ):
                    if n >= 2:
                        pe.wait_ge(k_done, n - 1)
                    for kc in range(DC):
                        cols = slice(inner + c * P, inner + (c + 1) * P)
                        last = three_passes(nc, (T0, T1)[n % 2][:, 0:nn], w_hi[:, kc, cols], w_lo[:, kc, cols],
                                            c_hi[:, kc, n0:n0 + nn], c_lo[:, kc, n0:n0 + nn],
                                            kc == 0, kc == DC - 1)
                    last.then_inc(k_sum, 1)
                for b in range(B):
                    if b >= 2:
                        pe.wait_ge(v_done, b - 1)
                    for kc in range(DC):
                        last = three_passes(nc, (S0, S1)[b % 2][0:S, 0:inner],
                                            c_hi[:, kc, b * S:(b + 1) * S], c_lo[:, kc, b * S:(b + 1) * S],
                                            w_hi[:, kc, 2 * inner:3 * inner], w_lo[:, kc, 2 * inner:3 * inner],
                                            kc == 0, kc == DC - 1)
                    last.then_inc(v_sum, 1)

        mv = sb("mv", [P, TT, 2])
        bn = sb("bn", [P, TT, 6])
        var = sb("var", [P, TT])
        rstd = sb("rstd", [P, TT])
        xn = sb("xn", [P, TT, D])
        xt_hi = sb("xt_hi", [P, DC, T], F32R)
        xt_lo = sb("xt_lo", [P, DC, T], F32R)
        q_hi = sb("q_hi", [P, 2, C, T], F32R)
        q_lo = sb("q_lo", [P, 2, C, T], F32R)
        kb_hi = sb("kb_hi", [P, 2, C, HPC, S], F32R)
        kb_lo = sb("kb_lo", [P, 2, C, HPC, S], F32R)
        maxima = sb("maxima", [P, TT, heads])
        mt = sb("mt", [P, 2, T], F32R)
        prob = sb("prob", [P, 2, 2, T])
        rden = sb("rden", [P, TT, heads])
        att = sb("att", [P, TT, inner])
        at_hi = sb("at_hi", [P, C, T], F32R)
        at_lo = sb("at_lo", [P, C, T], F32R)
        mv2 = sb("mv2", [P, TT, 2])
        bn2 = sb("bn2", [P, TT, 6])
        var2 = sb("var2", [P, TT])
        xn2 = sb("xn2", [P, TT, D])

        x_loaded = [sem("x_loaded0"), sem("x_loaded1")]
        cleared = sem("cleared")
        passed = sem("passed")
        ln_bn, ln_stats, ln_eps, ln_rstd, ln_xn, biased = (sem(x) for x in (
            "ln_bn", "ln_stats", "ln_eps", "ln_rstd", "ln_xn", "biased"))
        xt_ready, xt_rounded, xt_split = sem("xt_ready"), sem("xt_rounded"), sem("xt_split")
        q_ready, q_rounded, q_split = sem("q_ready"), sem("q_rounded"), sem("q_split")
        kb_ready = sem("kb_ready")
        mx_scores, mx_taken, mt_ready, mt_copied = (sem(x) for x in (
            "mx_scores", "mx_taken", "mt_ready", "mt_copied"))
        scores, probs, outs = sem("scores"), sem("probs"), sem("outs")
        den_ready, att_ready = sem("den_ready"), sem("att_ready")
        at_ready, at_rounded, at_split = sem("at_ready"), sem("at_rounded"), sem("at_split")
        proj_ready, x_updated = sem("proj_ready"), sem("x_updated")
        n_bn, n_stats, n_eps, n_rstd, n_xn, n_max = (sem(x) for x in (
            "n_bn", "n_stats", "n_eps", "n_rstd", "n_xn", "n_max"))

        if HP == 8:
            SLOT = ("norm s0 xt s1 p0 kb q0 s2 p1 at0 ln s3 p2 mx0 mx1 proj xn s4 p3 mx2 mx3 st1 s5 p4 mx4 mx5 "
                    "s6 p5 mx6 mx7 s7 p6 mt st2 p7").split()
        else:
            SLOT = ("norm s0 xt s1 p0 q0 at0 kb s2 p1 q1 at1 ln mx0 mx1 s3 p2 mx2 mx3 xn proj mt p3").split()
        FRONT = {"kb", "xt", "mt"} | {f"q{n}" for n in range(NP)} | {f"mx{n}" for n in range(NG)}
        BACK = {"norm", "proj", "st1", "st2"} | {f"at{n}" for n in range(NP)}

        def slots(eng, step):
            def slot(b, par, pre=True, front=True, middle=True, back=True):
                for what in SLOT:
                    if what in ("ln", "xn"):
                        if pre:
                            step(what, b + 2, par)
                    elif what in FRONT:
                        if front:
                            step(what, b + 1, 1 - par)
                    elif what in BACK:
                        if back:
                            step(what, b - 1, 1 - par)
                    elif middle:
                        step(what, b, par)

            slot(-2, 0, front=False, middle=False, back=False)
            slot(-1, 1, middle=False, back=False)
            slot(0, 0, back=False)
            with eng.Fori(0, (B - 4) // 2) as j:
                slot(j * 2 + 1, 1)
                slot(j * 2 + 2, 0)
            slot(B - 3, 1)
            slot(B - 2, 0, pre=False)
            slot(B - 1, 1, pre=False, front=False)
            slot(B, 0, pre=False, front=False, middle=False)

        block = ctx.enter_context(nc.Block())

        @block.sync
        def _(sp):
            if first:
                def load(b, par):
                    sp.dma_start(xres[:, bass.ds(b * TT, TT), :],
                                 x_in[bass.ds(b * T, T), :].rearrange("(t p) d -> p t d", p=P),
                                 ).then_inc(x_loaded[par], 16)

                load(0, 0)
                load(1, 1)
                with sp.Fori(1, B // 2) as j:
                    for par in range(2):
                        sp.wait_ge(x_loaded[par], j * 16)
                        load(j * 2 + par, par)

        @block.gpsimd
        def _(pool):
            pool.memset(mt[:].bitcast(F32), 0.0).then_inc(cleared, 1)
            pool.memset(prob[:], 0.0).then_inc(cleared, 1)

            def step(what, b, par):
                if what == "ln":
                    pool.wait_ge(ln_stats, b + 1)
                    pool.tensor_tensor(var[:], mv[:, :, 1], eps[:], ALU.add).then_inc(ln_eps, 1)
                    pool.wait_ge(ln_eps, b + 1)
                    pool.tensor_tensor(rstd[:], var[:], minus_half[:], ALU.pow).then_inc(ln_rstd, 1)
                    pool.wait_ge(ln_xn, b + 1)
                    for t in range(TT):
                        x = xres[:, bass.ds(b * TT + t, 1), :].rearrange("p o d -> p (o d)")
                        last = pool.tensor_tensor(x, x, gb[:], ALU.add)
                    last.then_inc(biased, 1)
                elif what == "st1" and first:
                    pool.wait_ge(n_stats, b + 1)
                    pool.tensor_tensor(var2[:], mv2[:, :, 1], eps[:], ALU.add).then_inc(n_eps, 1)
                    pool.wait_ge(n_eps, b + 1)
                    pool.tensor_tensor(env["rstd_all"][:, bass.ds(b * TT, TT)], var2[:], minus_half[:],
                                       ALU.pow).then_inc(n_rstd, 1)

            slots(pool, step)

        @block.scalar
        def _(act):
            act.wait_ge(cleared, 2)

            def step(what, b, par):
                if what == "xt":
                    act.wait_ge(xt_ready, b + 1)
                    act.activation(xt_hi[:], T0[:, :], ACT.Copy).then_inc(xt_rounded, 1)
                elif what[0] == "q":
                    n = int(what[1])
                    act.wait_ge(q_ready, b * NP + n + 1)
                    src = (T0, X0)[n]
                    for c in range(2):
                        bias = bqk[:, 0, 2 * n + c:2 * n + c + 1] if first else 0.0
                        last = act.activation(q_hi[:, par, 2 * n + c, :], src[:, c * T:(c + 1) * T],
                                              ACT.Identity, bias=bias)
                    last.then_inc(q_rounded, 1)
                elif what == "mt":
                    act.wait_ge(mt_ready, b + 1)
                    act.activation(mt[0:heads, par, :], T0[0:heads, 0:T], ACT.Copy).then_inc(mt_copied, 1)
                elif what[0] == "s" and what[1] != "t":
                    n = int(what[1])
                    act.wait_ge(scores, b * HP + n + 1)
                    if not (isinstance(b, int) and b == 0 and n < 2):
                        act.wait_ge(outs, b * HP + n - 1)
                    act.activation(prob[0:S, n % 2, :, :].rearrange("p a b -> p (a b)"),
                                   (S0, S1)[n % 2][0:S, :], ACT.Exp, scale=SCALE).then_inc(probs, 1)
                elif what[:2] == "at":
                    n = int(what[2])
                    act.wait_ge(at_ready, b * NP + n + 1)
                    act.activation(at_hi[:, 2 * n:2 * n + 2, :].rearrange("p a b -> p (a b)"), T1[:, :],
                                   ACT.Copy).then_inc(at_rounded, 1)

            slots(act, step)

        @block.vector
        def _(dve):
            dve.sem_inc(x_updated, 1)

            def xtile(b, t):
                return xres[:, bass.ds(b * TT + t, 1), :].rearrange("p o d -> p (o d)")

            def step(what, b, par):
                if what == "norm":
                    dve.wait_ge(outs, (b + 1) * HP)
                    for t in range(TT):
                        near = heads - 1 if wide else heads
                        o = (O0, O1)[t][:, 0:near * DV].rearrange("p (h v) -> p h v", v=DV)
                        last = dve.reciprocal(rden[:, t, 0:near], o[:, :, d])
                        if wide:
                            last = dve.reciprocal(rden[:, t, near:heads], out_of(t, near)[:, d:DV])
                    last.then_inc(den_ready, 1)
                    dve.wait_ge(den_ready, b + 1)
                    for t in range(TT):
                        near = heads - 1 if wide else heads
                        o = (O0, O1)[t][:, 0:near * DV].rearrange("p (h v) -> p h v", v=DV)
                        a = att[:, t, :].rearrange("p (h v) -> p h v", v=d)
                        last = dve.tensor_tensor(a[:, 0:near, :], o[:, :, 0:d],
                                                 rden[:, t, 0:near].unsqueeze(2).to_broadcast([P, near, d]),
                                                 ALU.mult)
                        if wide:
                            last = dve.tensor_scalar(a[:, near, :], out_of(t, near)[:, 0:d],
                                                     rden[:, t, near:heads], None, ALU.mult)
                    last.then_inc(att_ready, 1)
                elif what == "ln":
                    if first:
                        if isinstance(b, int):
                            dve.wait_ge(x_loaded[par], 16 * (b // 2 + 1))
                        else:
                            dve.wait_ge(x_loaded[par], (b - par) * 8 + 16)
                            dve.sem_inc(passed, 1)
                    for t in range(TT):
                        last = dve.bn_stats(bn[:, t, :], xtile(b, t))
                    last.then_inc(ln_bn, 1)
                    dve.wait_ge(ln_bn, b + 1)
                    dve.sem_inc(passed, 1)
                    for t in range(TT):
                        last = dve.bn_aggr(mv[:, t, :], bn[:, t, :])
                    last.then_inc(ln_stats, 1)
                elif what == "xn":
                    dve.wait_ge(ln_rstd, b + 1)
                    for t in range(TT):
                        last = dve.tensor_scalar(xn[:, t, :], xtile(b, t), mv[:, t, 0:1], rstd[:, t:t + 1],
                                                 ALU.subtract, ALU.mult)
                    last.then_inc(ln_xn, 1)
                elif what == "kb":
                    for full, masked in ((k_hi, kb_hi), (k_lo, kb_lo)):
                        for c in range(C):
                            src = full[:, c, bass.ds(b * S, S)].bitcast(F32)
                            last = dve.tensor_tensor(masked[:, par, c, :, :],
                                                     src.unsqueeze(1).to_broadcast([P, HPC, S]),
                                                     head_mask[:].unsqueeze(2).to_broadcast([P, HPC, S]),
                                                     ALU.mult)
                    last.then_inc(kb_ready, 1)
                elif what == "xt":
                    dve.wait_ge(xt_rounded, b + 1)
                    dve.tensor_tensor(xt_lo[:].rearrange("p a b -> p (a b)"), T0[:, :],
                                      xt_hi[:].rearrange("p a b -> p (a b)").bitcast(F32),
                                      ALU.subtract).then_inc(xt_split, 1)
                elif what[0] == "q":
                    n = int(what[1])
                    dve.wait_ge(q_rounded, b * NP + n + 1)
                    src = (T0, X0)[n]
                    for c in range(2):
                        bias = bqk[:, 0, 2 * n + c:2 * n + c + 1] if first else 0.0
                        last = dve.scalar_tensor_tensor(
                            out=q_lo[:, par, 2 * n + c, :], in0=src[:, c * T:(c + 1) * T], scalar=bias,
                            in1=q_hi[:, par, 2 * n + c, :].bitcast(F32), op0=ALU.add, op1=ALU.subtract)
                    last.then_inc(q_split, 1)
                elif what[:2] == "mx":
                    g = int(what[2])
                    t, h0 = g // (NG // TT), 4 * (g % (NG // TT))
                    dve.wait_ge(mx_scores, b * NG + g + 1)
                    dve.tensor_reduce(maxima[:, t, h0:h0 + 4],
                                      mx_banks[g % NMX][:, 0:4 * S].rearrange("p (h s) -> p h s", s=S),
                                      AX.X, ALU.max).then_inc(mx_taken, 1)
                elif what[:2] == "at":
                    n = int(what[2])
                    dve.wait_ge(at_rounded, b * NP + n + 1)
                    dve.tensor_tensor(at_lo[:, 2 * n:2 * n + 2, :].rearrange("p a b -> p (a b)"), T1[:, :],
                                      at_hi[:, 2 * n:2 * n + 2, :].rearrange("p a b -> p (a b)").bitcast(F32),
                                      ALU.subtract).then_inc(at_split, 1)
                elif what == "proj":
                    dve.wait_ge(proj_ready, b + 1)
                    dve.wait_ge(biased, b + 1)
                    for t in range(TT):
                        x = xtile(b, t)
                        last = dve.scalar_tensor_tensor(out=x, in0=T1[:, t * D:(t + 1) * D], scalar=tg[:, 0:1],
                                                        in1=x, op0=ALU.mult, op1=ALU.add)
                    last.then_inc(x_updated, 1)
                elif what == "st1" and first:
                    dve.wait_ge(x_updated, b + 2)
                    dve.sem_inc(passed, 1)
                    for t in range(TT):
                        last = dve.bn_stats(bn2[:, t, :], xtile(b, t))
                    last.then_inc(n_bn, 1)
                    dve.wait_ge(n_bn, b + 1)
                    dve.sem_inc(passed, 1)
                    for t in range(TT):
                        last = dve.bn_aggr(mv2[:, t, :], bn2[:, t, :])
                    last.then_inc(n_stats, 1)
                elif what == "st2" and first:
                    dve.wait_ge(n_rstd, b + 1)
                    dve.tensor_copy(env["mean_all"][:, bass.ds(b * TT, TT)], mv2[:, :, 0])
                    for t in range(TT):
                        last = dve.tensor_scalar(xn2[:, t, :], xtile(b, t), mv2[:, t, 0:1],
                                                 env["rstd_all"][:, bass.ds(b * TT + t, 1)],
                                                 ALU.subtract, ALU.mult)
                    last.then_inc(n_xn, 1)
                    dve.wait_ge(n_xn, b + 1)
                    dve.tensor_reduce(env["amax_x"][:, bass.ds(b, 1)],
                                      xn2[:].rearrange("p t d -> p (t d)"), AX.X, ALU.max,
                                      apply_absolute_value=True).then_inc(n_max, 1)

            slots(dve, step)

        @block.tensor
        def _(pe):
            def step(what, b, par):
                if what == "xt":
                    pe.wait_ge(ln_xn, b + 1)
                    pe.wait_ge(mt_copied, b)
                    for c in range(DC):
                        for t in range(TT):
                            last = pe.transpose(T0[:, c * T + t * P:c * T + (t + 1) * P],
                                                xn[:, t, c * P:(c + 1) * P], ident[:])
                    last.then_inc(xt_ready, 1)
                elif what[0] == "q":
                    n = int(what[1])
                    pe.wait_ge(xt_split, b + 1)
                    for c in range(2):
                        cols = slice((2 * n + c) * P, (2 * n + c + 1) * P)
                        for kc in range(DC):
                            last = three_passes(nc, (T0, X0)[n][:, c * T:(c + 1) * T],
                                                w_hi[:, kc, cols], w_lo[:, kc, cols],
                                                xt_hi[:, kc, :], xt_lo[:, kc, :], kc == 0, kc == DC - 1)
                    last.then_inc(q_ready, 1)
                elif what[:2] == "mx":
                    g = int(what[2])
                    t, h0 = g // (NG // TT), 4 * (g % (NG // TT))
                    if g == 0:
                        pe.wait_ge(kb_ready, b + 1)
                        pe.wait_ge(q_split, (b + 1) * NP)
                    if not (isinstance(b, int) and b == 0 and g < NMX):
                        pe.wait_ge(mx_taken, b * NG + g + 1 - NMX)
                    per = min(4, HPC)
                    for h in range(h0, h0 + 4, per):
                        c, r = h // HPC, h % HPC
                        last = pe.matmul(mx_banks[g % NMX][:, (h - h0) * S:(h - h0 + per) * S],
                                         q_hi[:, par, c, t * P:(t + 1) * P],
                                         kb_hi[:, par, c, r:r + per, :].rearrange("p a b -> p (a b)"),
                                         start=True, stop=True)
                    last.then_inc(mx_scores, 1)
                elif what == "mt":
                    pe.wait_ge(mx_taken, (b + 1) * NG)
                    for t in range(TT):
                        last = pe.transpose(T0[0:heads, t * P:(t + 1) * P], maxima[:, t, :], ident[:])
                    last.then_inc(mt_ready, 1)
                elif what[0] == "s" and what[1] != "t":
                    n = int(what[1])
                    if n == 0:
                        pe.wait_ge(mt_copied, b + 1)
                    if not (isinstance(b, int) and b == 0 and n < 2):
                        pe.wait_ge(probs, b * HP + n - 1)
                    for hh in range(2):
                        h = 2 * n + hh
                        c, r = h // HPC, h % HPC
                        out = (S0, S1)[n % 2][0:S, hh * T:(hh + 1) * T]
                        three_passes(nc, out, kb_hi[:, par, c, r, :], kb_lo[:, par, c, r, :],
                                     q_hi[:, par, c, :], q_lo[:, par, c, :], True, False)
                        last = pe.matmul(out, pick[:, h, 0:S], mt[:, par, :], start=False, stop=True)
                    last.then_inc(scores, 1)
                elif what[0] == "p" and what != "proj":
                    n = int(what[1])
                    pe.wait_ge(probs, b * HP + n + 1)
                    if n == 0:
                        pe.wait_ge(att_ready, b)
                    for hh in range(2):
                        h = 2 * n + hh
                        for t in range(TT):
                            v = values[:, bass.ds(b, 1), h, :].rearrange("p o v -> p (o v)")
                            last = pe.matmul(out_of(t, h), prob[:, n % 2, hh, t * P:(t + 1) * P], v,
                                             start=True, stop=True)
                    last.then_inc(outs, 1)
                elif what[:2] == "at":
                    n = int(what[2])
                    pe.wait_ge(att_ready, b + 1)
                    if n == 0:
                        pe.wait_ge(x_updated, b + 1)
                    else:
                        pe.wait_ge(at_split, b * NP + n)
                    for c in range(2):
                        for t in range(TT):
                            cols = slice((2 * n + c) * P, (2 * n + c + 1) * P)
                            last = pe.transpose(T1[:, c * T + t * P:c * T + (t + 1) * P], att[:, t, cols],
                                                ident[:])
                    last.then_inc(at_ready, 1)
                elif what == "proj":
                    pe.wait_ge(at_split, (b + 1) * NP)
                    for t in range(TT):
                        for c in range(C):
                            last = three_passes(nc, T1[:, t * D:(t + 1) * D],
                                                at_hi[:, c, t * P:(t + 1) * P], at_lo[:, c, t * P:(t + 1) * P],
                                                wo_hi[:, c, :], wo_lo[:, c, :], c == 0, c == C - 1)
                    last.then_inc(proj_ready, 1)

            slots(pe, step)

    free_semaphores(nc, sems)


def quantised_ffn(nc, env, w_up, w_gate, w_down, gate):
    xres, banks, ident = env["xres"], env["banks"], env["ident"]
    T0, T1, X0, X1, S0, S1, O0, O1 = banks
    FT = HID0 // P
    G = NT * P // GT
    GTT = GT // P
    sems = []
    ctx = ExitStack()
    with ctx:
        def sb(name, shape, dt=F32):
            return ctx.enter_context(nc.sbuf_tensor(f"f0_{name}", shape, dt))

        def sem(name):
            sems.append(nc.alloc_semaphore(f"f0_{name}"))
            return sems[-1]

        scales = sb("scales", [P, 5])
        codes = sb("codes", [P, 5])
        small = sb("small", [P, 4])
        unit = sb("unit", [P, 5])
        tg = sb("tg", [P, 1])
        amax = sb("amax", [P, 2, G, FT])
        SX, SG, SU, S2, SO = range(5)
        w_hi = sb("w_hi", [P, 2, DC, HID0], F32R)
        w_lo = sb("w_lo", [P, 2, DC, HID0], F32R)
        d_hi = sb("d_hi", [P, FT, D], F32R)
        d_lo = sb("d_lo", [P, FT, D], F32R)

        def scale_steps(dve, k, done, at):
            dve.tensor_scalar(small[:, 2:3], small[:, 0:1], unit[:, k:k + 1], 1.0 / ACT_MAX,
                              ALU.mult, ALU.mult).then_inc(done, 1)
            dve.wait_ge(done, at + 1)
            dve.tensor_scalar(scales[:, k:k + 1], small[:, 2:3], TINY, None, ALU.max).then_inc(done, 1)
            dve.wait_ge(done, at + 2)
            dve.reciprocal(small[:, 3:4], scales[:, k:k + 1]).then_inc(done, 1)
            dve.wait_ge(done, at + 3)
            dve.tensor_tensor(codes[:, k:k + 1], small[:, 3:4], unit[:, k:k + 1], ALU.mult).then_inc(done, 1)
            dve.wait_ge(done, at + 4)

        with ExitStack() as setup:
            W = 3 * FT * D
            NB = W // BLOCK
            raw = setup.enter_context(nc.sbuf_tensor("f0_raw", [P, 3 * FT, D], F32))
            wcode = setup.enter_context(nc.sbuf_tensor("f0_wcode", [P, W], I16))
            wval = setup.enter_context(nc.sbuf_tensor("f0_wval", [P, 3 * FT, D], F32))
            bs = setup.enter_context(nc.sbuf_tensor("f0_bs", [P, 3, NB], F32))
            w_in, q_step, w_quantised = sem("w_in"), sem("q_step"), sem("w_quantised")
            turned, w_rounded, w_split = sem("turned"), sem("w_rounded"), sem("w_split")
            x_max, x_all, x_scale = sem("x_max"), sem("x_all"), sem("x_scale")
            turns = []
            for net in range(2):
                for c in range(DC):
                    for f0 in range(0, FT, 3):
                        turns.append(([(net * FT + f, c * P) for f in range(f0, f0 + 3)],
                                      (w_hi[:, net, c, f0 * P:(f0 + 3) * P], w_lo[:, net, c, f0 * P:(f0 + 3) * P])))
            for f in range(FT):
                turns.append(([(2 * FT + 3 * o + f // 2, (f % 2) * P) for o in range(DC)],
                              (d_hi[:, f, :], d_lo[:, f, :])))
            block = setup.enter_context(nc.Block())

            @block.sync
            def _(sp):
                sp.dma_start(raw[:, 0:FT, :], w_gate.rearrange("(f p) d -> p f d", p=P)).then_inc(w_in, 16)
                sp.dma_start(raw[:, FT:2 * FT, :], w_up.rearrange("(f p) d -> p f d", p=P)).then_inc(w_in, 16)
                for o in range(DC):
                    sp.dma_start(raw[:, 2 * FT + 3 * o:2 * FT + 3 * o + 3, :].rearrange("p f d -> p (f d)"),
                                 w_down[o * P:(o + 1) * P, :]).then_inc(w_in, 16)
                sp.dma_start(tg[:], gate).then_inc(w_in, 16)

            @block.vector
            def _(dve):
                flat = raw[:].rearrange("p f d -> p (f d)").rearrange("p (n k) -> p n k", k=BLOCK)
                dve.wait_ge(w_in, 16 * 5)
                dve.tensor_reduce(bs[:, 0, :], flat, AX.X, ALU.max, apply_absolute_value=True).then_inc(q_step, 1)
                dve.wait_ge(q_step, 1)
                dve.tensor_scalar(bs[:, 1, :], bs[:, 0, :], 1.0 / 7.0, TINY, ALU.mult, ALU.max).then_inc(q_step, 1)
                dve.wait_ge(q_step, 2)
                dve.reciprocal(bs[:, 2, :], bs[:, 1, :]).then_inc(q_step, 1)
                dve.wait_ge(q_step, 3)
                cv = wcode[:].rearrange("p (n k) -> p n k", k=BLOCK)
                dve.tensor_tensor(cv, flat, bs[:, 2, :].unsqueeze(2).to_broadcast([P, NB, BLOCK]),
                                  ALU.mult).then_inc(q_step, 1)
                dve.wait_ge(q_step, 4)
                dve.tensor_scalar(wcode[:], wcode[:], -8.0, 7.0, ALU.max, ALU.min).then_inc(q_step, 1)
                dve.wait_ge(q_step, 5)
                dve.tensor_tensor(wval[:].rearrange("p f d -> p (f d)").rearrange("p (n k) -> p n k", k=BLOCK), cv,
                                  bs[:, 1, :].unsqueeze(2).to_broadcast([P, NB, BLOCK]),
                                  ALU.mult).then_inc(w_quantised, 1)
                for n, (pieces, (hi, lo)) in enumerate(turns):
                    dve.wait_ge(w_rounded, n + 1)
                    dve.tensor_tensor(lo, (T0, T1)[n % 2][:, 0:len(pieces) * P], hi.bitcast(F32),
                                      ALU.subtract).then_inc(w_split, 1)
                dve.memset(unit[:, SX:SX + 1], 1.0)
                dve.tensor_reduce(small[:, 1:2], env["amax_x"][:], AX.X, ALU.max).then_inc(x_max, 1)
                dve.wait_ge(x_all, 1)
                scale_steps(dve, SX, x_scale, 0)

            @block.gpsimd
            def _(pool):
                pool.wait_ge(x_max, 1)
                pool.partition_all_reduce(small[:, 0:1], small[:, 1:2], P, RMAX).then_inc(x_all, 1)

            @block.tensor
            def _(pe):
                pe.wait_ge(w_quantised, 1)
                for n, (pieces, _) in enumerate(turns):
                    if n >= 2:
                        pe.wait_ge(w_split, n - 1)
                    for i, (tile, col) in enumerate(pieces):
                        last = pe.transpose((T0, T1)[n % 2][:, i * P:(i + 1) * P], wval[:, tile, col:col + P],
                                            ident[:])
                    last.then_inc(turned, 1)

            @block.scalar
            def _(act):
                for n, (pieces, (hi, lo)) in enumerate(turns):
                    act.wait_ge(turned, n + 1)
                    act.activation(hi, (T0, T1)[n % 2][:, 0:len(pieces) * P], ACT.Copy).then_inc(w_rounded, 1)
                act.wait_ge(w_in, 16 * 5)
                act.activation(tg[:], tg[:], ACT.Tanh)

        hid = sb("hid", [P, FT, NT * P])
        with ExitStack() as ph:
            def tmp(name, shape, dt=F32):
                return ph.enter_context(nc.sbuf_tensor(f"f0_{name}", shape, dt))

            xn = tmp("xn", [P, GTT, D])
            xcode = tmp("xcode", [P, GTT, D], I16)
            xt_hi = tmp("xt_hi", [P, 2, DC, GT], F32R)
            xt_lo = tmp("xt_lo", [P, 2, DC, GT], F32R)
            NU = 3
            ubuf = tmp("ubuf", [P, NU, GT])
            x_normed, x_coded, x_float, xt_ready, xt_rounded, xt_split = (sem(x) for x in (
                "x_normed", "x_coded", "x_float", "xt_ready", "xt_rounded", "xt_split"))
            prods, stored, maxed = sem("prods"), sem("stored"), sem("maxed")
            u_sent = [sem(f"u_sent{n}") for n in range(NU)]
            mm = [X0, X1, S0, S1, O0, O1]
            M = 2 * FT
            block = ph.enter_context(nc.Block())

            def slots(eng, step):
                def slot(g, par, front=True, back=True):
                    for n in range(M):
                        if front and n == 1:
                            step("ln", 0, g + 1, 1 - par)
                        if front and n == 5:
                            step("x", 0, g + 1, 1 - par)
                        if back:
                            step("m", n, g, par)

                slot(-1, 1, back=False)
                slot(0, 0)
                with eng.Fori(0, (G - 2) // 2) as j:
                    slot(j * 2 + 1, 1)
                    slot(j * 2 + 2, 0)
                slot(G - 1, 1, front=False)

            @block.vector
            def _(dve):
                def step(what, n, g, par):
                    if what == "ln":
                        for t in range(GTT):
                            last = dve.tensor_scalar(
                                xn[:, t, :], xres[:, bass.ds(g * GTT + t, 1), :].rearrange("p o d -> p (o d)"),
                                env["mean_all"][:, bass.ds(g * GTT + t, 1)],
                                env["rstd_all"][:, bass.ds(g * GTT + t, 1)], ALU.subtract, ALU.mult)
                        last.then_inc(x_normed, 1)
                        dve.wait_ge(x_normed, g + 1)
                        dve.tensor_scalar(xcode[:], xn[:], codes[:, SX:SX + 1], None, ALU.mult).then_inc(x_coded, 1)
                        dve.wait_ge(x_coded, g + 1)
                        dve.tensor_copy(xn[:], xcode[:]).then_inc(x_float, 1)
                    elif what == "x":
                        for c in range(DC):
                            dve.wait_ge(xt_rounded, g * DC + c + 1)
                            dve.tensor_tensor(xt_lo[:, par, c, :], (T0, T1)[c][:, :],
                                              xt_hi[:, par, c, :].bitcast(F32), ALU.subtract).then_inc(xt_split, 1)
                    else:
                        dve.wait_ge(stored, g * M + n + 1)
                        dve.tensor_reduce(amax[:, n % 2, bass.ds(g, 1), n // 2], mm[n % 6][:, :], AX.X, ALU.max,
                                          apply_absolute_value=True).then_inc(maxed, 1)

                slots(dve, step)

            @block.tensor
            def _(pe):
                def step(what, n, g, par):
                    if what == "x":
                        pe.wait_ge(x_float, g + 1)
                        for c in range(DC):
                            pe.wait_ge(xt_split, g * DC)
                            for t in range(GTT):
                                last = pe.transpose((T0, T1)[c][:, t * P:(t + 1) * P],
                                                    xn[:, t, c * P:(c + 1) * P], ident[:])
                            last.then_inc(xt_ready, 1)
                    elif what == "m":
                        if n == 0:
                            pe.wait_ge(xt_split, (g + 1) * DC)
                        if not (isinstance(g, int) and g == 0 and n < 6):
                            pe.wait_ge(maxed, g * M + n - 5)
                        f = n // 2
                        for c in range(DC):
                            last = three_passes(nc, mm[n % 6][:, :],
                                                w_hi[:, n % 2, c, f * P:(f + 1) * P],
                                                w_lo[:, n % 2, c, f * P:(f + 1) * P],
                                                xt_hi[:, par, c, :], xt_lo[:, par, c, :], c == 0, c == DC - 1)
                        last.then_inc(prods, 1)

                slots(pe, step)

            @block.scalar
            def _(act):
                def step(what, n, g, par):
                    if what == "x":
                        for c in range(DC):
                            act.wait_ge(xt_ready, g * DC + c + 1)
                            act.activation(xt_hi[:, par, c, :], (T0, T1)[c][:, :], ACT.Copy).then_inc(xt_rounded, 1)
                    if what != "m":
                        return
                    act.wait_ge(prods, g * M + n + 1)
                    f = n // 2
                    if n % 2 == 0:
                        act.activation(hid[:, f, bass.ds(g * GT, GT)], mm[n % 6][:, :], ACT.Copy).then_inc(stored, 1)
                    else:
                        if not (isinstance(g, int) and g == 0 and f < NU):
                            act.wait_ge(u_sent[f % NU], g * 32 + (f // NU) * 16)
                        act.activation(ubuf[:, f % NU, :], mm[n % 6][:, :], ACT.Copy).then_inc(stored, 1)

                slots(act, step)

            @block.sync
            def _(sp):
                with sp.Fori(0, G) as g:
                    for f in range(FT):
                        sp.wait_ge(stored, g * M + 2 * f + 2)
                        sp.dma_start(env["u_dram"][:, f, bass.ds(g * GT, GT)],
                                     ubuf[:, f % NU, :]).then_inc(u_sent[f % NU], 16)
                for k in range(NU):
                    sp.wait_ge(u_sent[k], G * 32)

        NCH = 12
        CW = FT * NT * P // NCH
        flat = hid[:].rearrange("p f t -> p (f t)")
        u_flat = env["u_dram"].rearrange("p f t -> p (f t)")
        cmax = amax[:].rearrange("p n g f -> p (n g f)")

        with ExitStack() as ph:
            gcode = ph.enter_context(nc.sbuf_tensor("f0_gcode", [P, 2, CW], I16))
            sig = ph.enter_context(nc.sbuf_tensor("f0_sig", [P, 2, CW], F32))
            scode = ph.enter_context(nc.sbuf_tensor("f0_scode", [P, CW], U16))
            t_max, t_all, t_scale, s_ready = sem("t_max"), sem("t_all"), sem("t_scale"), sem("s_ready")
            gcoded, sig_ready, scoded, gated, c_maxed = (sem(x) for x in (
                "gcoded", "sig_ready", "scoded", "gated", "c_maxed"))
            block = ph.enter_context(nc.Block())

            @block.gpsimd
            def _(pool):
                for n in range(2):
                    pool.wait_ge(t_max, n + 1)
                    pool.partition_all_reduce(small[:, 0:1], small[:, 1:2], P, RMAX).then_inc(t_all, 1)

            @block.vector
            def _(dve):
                for n, k in enumerate((SG, SU)):
                    dve.tensor_copy(unit[:, k:k + 1], scales[:, SX:SX + 1])
                    dve.tensor_reduce(small[:, 1:2], amax[:, n, :, :].rearrange("p g f -> p (g f)"), AX.X,
                                      ALU.max).then_inc(t_max, 1)
                    dve.wait_ge(t_all, n + 1)
                    scale_steps(dve, k, t_scale, 4 * n)
                dve.tensor_scalar(unit[:, S2:S2 + 1], scales[:, SG:SG + 1], 1.0 / 65536, None,
                                  ALU.mult).then_inc(s_ready, 1)
                with dve.Fori(0, NCH // 2) as j:
                    for par in range(2):
                        i = j * 2 + par
                        part = flat[:, bass.ds(i * CW, CW)]
                        dve.wait_ge(sig_ready, i + 1)
                        dve.tensor_scalar(scode[:], sig[:, par, :], 65536.0, None, ALU.mult).then_inc(scoded, 1)
                        dve.wait_ge(scoded, i + 1)
                        dve.tensor_tensor(part, gcode[:, par, :], scode[:], ALU.mult).then_inc(gated, 1)
                        dve.wait_ge(gated, i + 1)
                        dve.tensor_reduce(cmax[:, bass.ds(i, 1)], part, AX.X, ALU.max,
                                          apply_absolute_value=True).then_inc(c_maxed, 1)

            @block.scalar
            def _(act):
                act.wait_ge(s_ready, 1)

                def chunk(i, par, again):
                    if again:
                        act.wait_ge(gated, i - 1)
                    act.activation(gcode[:, par, :], flat[:, bass.ds(i * CW, CW)], ACT.Identity,
                                   scale=codes[:, SG:SG + 1]).then_inc(gcoded, 1)
                    act.wait_ge(gcoded, i + 1)
                    act.activation(sig[:, par, :], gcode[:, par, :], ACT.Sigmoid,
                                   scale=scales[:, SG:SG + 1]).then_inc(sig_ready, 1)

                chunk(0, 0, False)
                chunk(1, 1, False)
                with act.Fori(1, NCH // 2) as j:
                    chunk(j * 2, 0, True)
                    chunk(j * 2 + 1, 1, True)

        with ExitStack() as ph:
            NR = 3
            ubuf = ph.enter_context(nc.sbuf_tensor("f0_uback", [P, NR, CW], F32))
            ucode = ph.enter_context(nc.sbuf_tensor("f0_ucode", [P, 2, CW], I16))
            gcode = ph.enter_context(nc.sbuf_tensor("f0_g2code", [P, CW], I16))
            d_max, d_all, d_scale = sem("d_max"), sem("d_all"), sem("d_scale")
            u_back = [sem(f"u_back{n}") for n in range(NR)]
            ucoded, g2coded, multiplied, d_maxed = (sem(x) for x in ("ucoded", "g2coded", "multiplied", "d_maxed"))
            block = ph.enter_context(nc.Block())

            @block.sync
            def _(sp):
                def load(j, k):
                    sp.dma_start(ubuf[:, k, :], u_flat[:, bass.ds((j * NR + k) * CW, CW)]).then_inc(u_back[k], 16)

                for k in range(NR):
                    load(0, k)
                with sp.Fori(1, NCH // NR) as j:
                    for k in range(NR):
                        sp.wait_ge(ucoded, (j - 1) * NR + k + 1)
                        load(j, k)

            @block.scalar
            def _(act):
                def chunk(j, k, n):
                    i = j * 6 + n
                    act.wait_ge(u_back[k], (j * 2 + n // NR + 1) * 16)
                    if not (isinstance(j, int) and j == 0 and n < 2):
                        act.wait_ge(multiplied, i - 1)
                    act.activation(ucode[:, n % 2, :], ubuf[:, k, :], ACT.Identity,
                                   scale=codes[:, SU:SU + 1]).then_inc(ucoded, 1)

                for n in range(6):
                    chunk(0, n % NR, n)
                with act.Fori(1, NCH // 6) as j:
                    for n in range(6):
                        chunk(j, n % NR, n)

            @block.gpsimd
            def _(pool):
                pool.wait_ge(d_max, 1)
                pool.partition_all_reduce(small[:, 0:1], small[:, 1:2], P, RMAX).then_inc(d_all, 1)

            @block.vector
            def _(dve):
                dve.tensor_reduce(small[:, 1:2], cmax[:, 0:NCH], AX.X, ALU.max).then_inc(d_max, 1)
                dve.wait_ge(d_all, 1)
                scale_steps(dve, S2, d_scale, 0)
                dve.tensor_tensor(unit[:, SO:SO + 1], scales[:, S2:S2 + 1], scales[:, SU:SU + 1], ALU.mult)
                with dve.Fori(0, NCH // 2) as j:
                    for par in range(2):
                        i = j * 2 + par
                        part = flat[:, bass.ds(i * CW, CW)]
                        dve.tensor_scalar(gcode[:], part, codes[:, S2:S2 + 1], None, ALU.mult).then_inc(g2coded, 1)
                        dve.wait_ge(g2coded, i + 1)
                        dve.wait_ge(ucoded, i + 1)
                        dve.tensor_tensor(part, gcode[:], ucode[:, par, :], ALU.mult).then_inc(multiplied, 1)
                        dve.wait_ge(multiplied, i + 1)
                        dve.tensor_reduce(cmax[:, bass.ds(i, 1)], part, AX.X, ALU.max,
                                          apply_absolute_value=True).then_inc(d_maxed, 1)

        with ExitStack() as ph:
            ocode = ph.enter_context(nc.sbuf_tensor("f0_ocode", [P, FT, T], I16))
            o_hi = ph.enter_context(nc.sbuf_tensor("f0_o_hi", [P, 2, FT, T], F32R))
            o_lo = ph.enter_context(nc.sbuf_tensor("f0_o_lo", [P, 2, FT, T], F32R))
            back = ph.enter_context(nc.sbuf_tensor("f0_back", [P, 1], F32))
            e_max, e_all, e_scale = sem("e_max"), sem("e_all"), sem("e_scale")
            ocoded, o_rounded, o_split, down, e_added = (sem(x) for x in (
                "ocoded", "o_rounded", "o_split", "down", "e_added"))
            block = ph.enter_context(nc.Block())
            ybank = [X0, X1, S0, S1]

            @block.gpsimd
            def _(pool):
                pool.wait_ge(e_max, 1)
                pool.partition_all_reduce(small[:, 0:1], small[:, 1:2], P, RMAX).then_inc(e_all, 1)

            @block.vector
            def _(dve):
                dve.tensor_reduce(small[:, 1:2], cmax[:, 0:NCH], AX.X, ALU.max).then_inc(e_max, 1)
                dve.wait_ge(e_all, 1)
                scale_steps(dve, SO, e_scale, 0)
                dve.tensor_tensor(back[:], scales[:, SO:SO + 1], tg[:, 0:1], ALU.mult).then_inc(e_scale, 1)
                dve.wait_ge(e_scale, 5)

                def code(b, par, again):
                    dve.wait_ge(o_split, b)
                    dve.tensor_scalar(ocode[:], hid[:, :, bass.ds(b * T, T)], codes[:, SO:SO + 1], None,
                                      ALU.mult).then_inc(ocoded, 1)
                    dve.wait_ge(o_rounded, b + 1)
                    if again:
                        dve.wait_ge(down, b - 1)
                    dve.tensor_tensor(o_lo[:, par, :, :], ocode[:], o_hi[:, par, :, :].bitcast(F32),
                                      ALU.subtract).then_inc(o_split, 1)

                def add(b, par):
                    dve.wait_ge(down, b + 1)
                    for t in range(TT):
                        x = xres[:, bass.ds(b * TT + t, 1), :].rearrange("p o d -> p (o d)")
                        last = dve.scalar_tensor_tensor(out=x, in0=ybank[2 * par + t][:, 0:D], scalar=back[:, 0:1],
                                                        in1=x, op0=ALU.mult, op1=ALU.add)
                    last.then_inc(e_added, 1)

                code(0, 0, False)
                code(1, 1, False)
                with dve.Fori(0, B // 2 - 1) as j:
                    add(j * 2, 0)
                    code(j * 2 + 2, 0, True)
                    add(j * 2 + 1, 1)
                    code(j * 2 + 3, 1, True)
                add(B - 2, 0)
                add(B - 1, 1)

            @block.scalar
            def _(act):
                def hi(b, par, again):
                    act.wait_ge(ocoded, b + 1)
                    if again:
                        act.wait_ge(down, b - 1)
                    act.activation(o_hi[:, par, :, :], ocode[:], ACT.Copy).then_inc(o_rounded, 1)

                hi(0, 0, False)
                hi(1, 1, False)
                with act.Fori(1, B // 2) as j:
                    hi(j * 2, 0, True)
                    hi(j * 2 + 1, 1, True)

            @block.tensor
            def _(pe):
                def prod(b, par, again):
                    pe.wait_ge(o_split, b + 1)
                    if again:
                        pe.wait_ge(e_added, b - 1)
                    for t in range(TT):
                        for f in range(FT):
                            last = three_passes(nc, ybank[2 * par + t][:, 0:D],
                                                o_hi[:, par, f, t * P:(t + 1) * P],
                                                o_lo[:, par, f, t * P:(t + 1) * P],
                                                d_hi[:, f, :], d_lo[:, f, :], f == 0, f == FT - 1)
                    last.then_inc(down, 1)

                prod(0, 0, False)
                prod(1, 1, False)
                with pe.Fori(1, B // 2) as j:
                    prod(j * 2, 0, True)
                    prod(j * 2 + 1, 1, True)

    free_semaphores(nc, sems)


def butterfly_ffn(nc, env, w_exp, b_exp, up_coef, up_bias, down_coef, w_con_t, out_bias, gate, out):
    xres, banks, ident = env["xres"], env["banks"], env["ident"]
    T0, T1, X0, X1, S0, S1, O0, O1 = banks
    HT = HID1 // P
    STAGES = HID1.bit_length() - 1
    G = NT * P // GT
    GTT = GT // P
    sems = []
    ctx = ExitStack()
    with ctx:
        def sb(name, shape, dt=F32):
            return ctx.enter_context(nc.sbuf_tensor(f"f1_{name}", shape, dt))

        def sem(name):
            sems.append(nc.alloc_semaphore(f"f1_{name}"))
            return sems[-1]

        w1_hi = sb("w1_hi", [P, DC, HID1], F32R)
        w1_lo = sb("w1_lo", [P, DC, HID1], F32R)
        w2_hi = sb("w2_hi", [P, HT, D], F32R)
        w2_lo = sb("w2_lo", [P, HT, D], F32R)
        b1 = sb("b1", [P, HT])
        gb = sb("gb", [P, D])
        tg = sb("tg", [P, 1])
        minus_half = sb("minus_half", [P, GTT])
        eps = sb("eps", [P, GTT])

        with ExitStack() as setup:
            def tmp(name, shape, dt=F32):
                return setup.enter_context(nc.sbuf_tensor(f"f1_{name}", shape, dt))

            u = tmp("u", [P, DC + 1, HID1])
            v = tmp("v", [P, DC, HID1])
            ucoef = tmp("ucoef", [P, 2, 2, HID1])
            vcoef = tmp("vcoef", [P, 2, 2, HID1])
            u_own = tmp("u_own", [P, DC + 1, HID1])
            u_pair = tmp("u_pair", [P, DC + 1, HID1])
            v_own = tmp("v_own", [P, DC, HID1])
            v_pair = tmp("v_pair", [P, DC, HID1])
            ub = tmp("ub", [P, HT])
            ob = tmp("ob", [P, 2, D])
            row_clear, w_in, uc_in, vc_in = sem("row_clear"), sem("w_in"), [sem("uc0"), sem("uc1")], [sem("vc0"), sem("vc1")]
            u_mul, u_add, v_mul, v_add = sem("u_mul"), sem("u_add"), sem("v_mul"), sem("v_add")
            bias_turned, b_done, turned, rounded, w2_split, g_done, ob_sum, w1_rounded = (sem(x) for x in (
                "bias_turned", "b_done", "turned", "rounded", "w2_split", "g_done", "ob_sum", "w1_rounded"))
            block = setup.enter_context(nc.Block())

            @block.sync
            def _(sp):
                for i in range(STAGES):
                    if i >= 2:
                        sp.wait_ge(u_mul, i - 1)
                    sp.dma_start(ucoef[:, i % 2, :, :], up_coef[i:i + 1].to_broadcast([P, 2, HID1]),
                                 ).then_inc(uc_in[i % 2], 16)
                    if i == 0:
                        sp.dma_start(u[:, 0:DC, :], w_exp.rearrange("(c p) n -> p c n", p=P)).then_inc(w_in, 16)
                        sp.dma_start(v[:], w_con_t.rearrange("(c p) n -> p c n", p=P)).then_inc(w_in, 16)
                        sp.wait_ge(row_clear, 1)
                        sp.dma_start(u[0:1, DC, :], b_exp).then_inc(w_in, 16)
                        sp.dma_start(ub[:], up_bias).then_inc(w_in, 16)
                        sp.dma_start(ob[:], out_bias).then_inc(w_in, 16)
                        sp.dma_start(tg[:], gate).then_inc(w_in, 16)
                    if i >= 2:
                        sp.wait_ge(v_mul, i - 1)
                    sp.dma_start(vcoef[:, i % 2, :, :], down_coef[i:i + 1].to_broadcast([P, 2, HID1]),
                                 ).then_inc(vc_in[i % 2], 16)

            def stages(eng, y, coef, own, pair, n, stride_of, arrived, mul, add):
                for i in range(STAGES):
                    s = stride_of(i)
                    eng.wait_ge(arrived[i % 2], (i // 2 + 1) * 16)
                    for c in range(n):
                        eng.tensor_tensor(own[:, c, :], y[:, c, :], coef[:, i % 2, 0, :], ALU.mult)
                        yv = y[:, c, :].rearrange("p (k two s) -> p k two s", two=2, s=s)
                        pv = pair[:, c, :].rearrange("p (k two s) -> p k two s", two=2, s=s)
                        cv = coef[:, i % 2, 1, :].rearrange("p (k two s) -> p k two s", two=2, s=s)
                        for half in range(2):
                            last = eng.tensor_tensor(pv[:, :, half, :], yv[:, :, 1 - half, :], cv[:, :, half, :],
                                                     ALU.mult)
                    last.then_inc(mul, 1)
                    eng.wait_ge(mul, i + 1)
                    eng.tensor_tensor(y[:], own[:], pair[:], ALU.add).then_inc(add, 1)
                    eng.wait_ge(add, i + 1)

            @block.vector
            def _(dve):
                dve.memset(u[:, DC, :], 0.0).then_inc(row_clear, 1)
                dve.wait_ge(w_in, 96)
                stages(dve, u, ucoef, u_own, u_pair, DC + 1, lambda i: 1 << i, uc_in, u_mul, u_add)
                dve.wait_ge(w1_rounded, 1)
                dve.tensor_tensor(w1_lo[:], u[:, 0:DC, :], w1_hi[:].bitcast(F32), ALU.subtract)
                dve.wait_ge(bias_turned, 1)
                dve.tensor_tensor(b1[:], X0[:, 0:HT], ub[:], ALU.add).then_inc(b_done, 1)
                dve.tensor_tensor(gb[:], ob[:, 0, :], ob[:, 1, :], ALU.add).then_inc(ob_sum, 1)
                dve.wait_ge(g_done, 1)
                dve.wait_ge(ob_sum, 1)
                dve.tensor_scalar(gb[:], gb[:], tg[:, 0:1], None, ALU.mult)
                for n in range(HT // 2):
                    dve.wait_ge(rounded, n + 1)
                    dve.tensor_tensor(w2_lo[:, 2 * n:2 * n + 2, :].rearrange("p a b -> p (a b)"), (T0, T1)[n % 2][:, :],
                                      w2_hi[:, 2 * n:2 * n + 2, :].rearrange("p a b -> p (a b)").bitcast(F32),
                                      ALU.subtract).then_inc(w2_split, 1)

            @block.gpsimd
            def _(pool):
                pool.memset(minus_half[:], -0.5)
                pool.memset(eps[:], LN_EPS)
                pool.wait_ge(w_in, 96)
                stages(pool, v, vcoef, v_own, v_pair, DC, lambda i: 1 << (STAGES - 1 - i), vc_in, v_mul, v_add)

            @block.tensor
            def _(pe):
                pe.wait_ge(u_add, STAGES)
                for m in range(HT):
                    last = pe.transpose(X0[:, m:m + 1], u[0:1, DC, m * P:(m + 1) * P], ident[0:1, 0:1])
                last.then_inc(bias_turned, 1)
                pe.wait_ge(v_add, STAGES)
                for n in range(HT // 2):
                    if n >= 2:
                        pe.wait_ge(w2_split, n - 1)
                    for a in range(2):
                        for c in range(DC):
                            m = 2 * n + a
                            last = pe.transpose((T0, T1)[n % 2][:, a * D + c * P:a * D + (c + 1) * P],
                                                v[:, c, m * P:(m + 1) * P], ident[:])
                    last.then_inc(turned, 1)

            @block.scalar
            def _(act):
                act.wait_ge(w_in, 96)
                act.activation(tg[:], tg[:], ACT.Tanh).then_inc(g_done, 1)
                act.wait_ge(u_add, STAGES)
                act.activation(w1_hi[:], u[:, 0:DC, :], ACT.Copy).then_inc(w1_rounded, 1)
                for n in range(HT // 2):
                    act.wait_ge(turned, n + 1)
                    act.activation(w2_hi[:, 2 * n:2 * n + 2, :].rearrange("p a b -> p (a b)"), (T0, T1)[n % 2][:, :],
                                   ACT.Copy).then_inc(rounded, 1)

        mv = sb("mv", [P, GTT, 2])
        bn = sb("bn", [P, GTT, 6])
        var = sb("var", [P, GTT])
        rstd = sb("rstd", [P, GTT])
        xn = sb("xn", [P, GTT, D])
        xt_hi = sb("xt_hi", [P, 2, DC, GT], F32R)
        xt_lo = sb("xt_lo", [P, 2, DC, GT], F32R)
        h = sb("h", [P, 2, GT])
        h_hi = sb("h_hi", [P, 2, HT, GT], F32R)
        h_lo = sb("h_lo", [P, 2, HT, GT], F32R)
        ln_bn, ln_stats, ln_eps, ln_rstd, ln_xn, biased = (sem(x) for x in (
            "ln_bn", "ln_stats", "ln_eps", "ln_rstd", "ln_xn", "biased"))
        xt_ready, xt_rounded, xt_split = sem("xt_ready"), sem("xt_rounded"), sem("xt_split")
        h_sum, h_ready, h_rounded, h_split = sem("h_sum"), sem("h_ready"), sem("h_rounded"), sem("h_split")
        passed = sem("passed")
        y_sum, y_added, y_sent = sem("y_sum"), sem("y_added"), sem("y_sent")
        hbank = [X0, X1, S0, S1]
        ybank = [O0, O1]

        def slots(eng, step):
            def slot(g, par, front=True, middle=True, back=True):
                for m in range(HT):
                    if front and m == 1:
                        step("ln", 0, g + 2, par)
                    if front and m == 6:
                        step("x", 0, g + 2, par)
                    if middle:
                        step("h", m, g + 1, 1 - par)
                for t in range(GTT):
                    if back:
                        step("y", t, g, par)

            slot(-2, 0, middle=False, back=False)
            slot(-1, 1, back=False)
            slot(0, 0)
            slot(1, 1)
            with eng.Fori(1, (G - 2) // 2) as j:
                slot(j * 2, 0)
                slot(j * 2 + 1, 1)
            slot(G - 2, 0, front=False)
            slot(G - 1, 1, front=False, middle=False)

        block = ctx.enter_context(nc.Block())

        @block.vector
        def _(dve):
            def xtile(g, t):
                return xres[:, bass.ds(g * GTT + t, 1), :].rearrange("p o d -> p (o d)")

            def step(what, n, g, par):
                if what == "ln":
                    for t in range(GTT):
                        last = dve.bn_stats(bn[:, t, :], xtile(g, t))
                    last.then_inc(ln_bn, 1)
                    dve.wait_ge(ln_bn, g + 1)
                    dve.sem_inc(passed, 1)
                    for t in range(GTT):
                        last = dve.bn_aggr(mv[:, t, :], bn[:, t, :])
                    last.then_inc(ln_stats, 1)
                    dve.wait_ge(ln_rstd, g + 1)
                    for t in range(GTT):
                        last = dve.tensor_scalar(xn[:, t, :], xtile(g, t), mv[:, t, 0:1], rstd[:, t:t + 1],
                                                 ALU.subtract, ALU.mult)
                    last.then_inc(ln_xn, 1)
                elif what == "x":
                    for c in range(DC):
                        dve.wait_ge(xt_rounded, g * DC + c + 1)
                        dve.tensor_tensor(xt_lo[:, par, c, :], (T0, T1)[c][:, :],
                                          xt_hi[:, par, c, :].bitcast(F32), ALU.subtract).then_inc(xt_split, 1)
                elif what == "h":
                    dve.wait_ge(h_ready, g * HT + n + 1)
                    dve.tensor_copy(h_hi[:, par, n, :], h[:, n % 2, :]).then_inc(h_rounded, 1)
                    dve.wait_ge(h_rounded, g * HT + n + 1)
                    dve.tensor_tensor(h_lo[:, par, n, :], h[:, n % 2, :], h_hi[:, par, n, :].bitcast(F32),
                                      ALU.subtract).then_inc(h_split, 1)
                elif what == "y":
                    dve.wait_ge(y_sum, g * GTT + n + 1)
                    dve.wait_ge(biased, g + 1)
                    x = xtile(g, n)
                    dve.scalar_tensor_tensor(out=x, in0=ybank[n % 2][:, 0:D], scalar=tg[:, 0:1], in1=x,
                                             op0=ALU.mult, op1=ALU.add).then_inc(y_added, 1)

            slots(dve, step)

        @block.gpsimd
        def _(pool):
            with pool.Fori(0, G) as g:
                pool.wait_ge(ln_stats, g + 1)
                pool.tensor_tensor(var[:], mv[:, :, 1], eps[:], ALU.add).then_inc(ln_eps, 1)
                pool.wait_ge(ln_eps, g + 1)
                pool.tensor_tensor(rstd[:], var[:], minus_half[:], ALU.pow).then_inc(ln_rstd, 1)
                pool.wait_ge(ln_xn, g + 1)
                for t in range(GTT):
                    x = xres[:, bass.ds(g * GTT + t, 1), :].rearrange("p o d -> p (o d)")
                    last = pool.tensor_tensor(x, x, gb[:], ALU.add)
                last.then_inc(biased, 1)

        @block.scalar
        def _(act):
            def step(what, n, g, par):
                if what == "x":
                    for c in range(DC):
                        act.wait_ge(xt_ready, g * DC + c + 1)
                        act.activation(xt_hi[:, par, c, :], (T0, T1)[c][:, :], ACT.Copy).then_inc(xt_rounded, 1)
                elif what == "h":
                    act.wait_ge(h_sum, g * HT + n + 1)
                    if not (isinstance(g, int) and g == 0 and n < 2):
                        act.wait_ge(h_split, g * HT + n - 1)
                    act.activation(h[:, n % 2, :], hbank[n % 4][:, :], ACT.Gelu,
                                   bias=b1[:, n:n + 1]).then_inc(h_ready, 1)

            slots(act, step)

        @block.tensor
        def _(pe):
            def step(what, n, g, par):
                if what == "x":
                    pe.wait_ge(ln_xn, g + 1)
                    pe.wait_ge(xt_split, g * DC)
                    for c in range(DC):
                        for t in range(GTT):
                            last = pe.transpose((T0, T1)[c][:, t * P:(t + 1) * P], xn[:, t, c * P:(c + 1) * P],
                                                ident[:])
                        last.then_inc(xt_ready, 1)
                elif what == "h":
                    if n == 0:
                        pe.wait_ge(xt_split, (g + 1) * DC)
                    if not (isinstance(g, int) and g == 0 and n < 4):
                        pe.wait_ge(h_ready, g * HT + n - 3)
                    for c in range(DC):
                        last = three_passes(nc, hbank[n % 4][:, :], w1_hi[:, c, n * P:(n + 1) * P],
                                            w1_lo[:, c, n * P:(n + 1) * P], xt_hi[:, par, c, :],
                                            xt_lo[:, par, c, :], c == 0, c == DC - 1)
                    last.then_inc(h_sum, 1)
                elif what == "y":
                    if n == 0:
                        pe.wait_ge(h_split, (g + 1) * HT)
                    if not (isinstance(g, int) and g == 0 and n < 2):
                        pe.wait_ge(y_added, g * GTT + n - 1)
                    for m in range(HT):
                        last = three_passes(nc, ybank[n % 2][:, 0:D], h_hi[:, par, m, n * P:(n + 1) * P],
                                            h_lo[:, par, m, n * P:(n + 1) * P], w2_hi[:, m, :], w2_lo[:, m, :],
                                            m == 0, m == HT - 1)
                    last.then_inc(y_sum, 1)

            slots(pe, step)

        @block.sync
        def _(sp):
            with sp.Fori(0, G) as g:
                sp.wait_ge(y_added, (g + 1) * GTT)
                sp.dma_start(out[bass.ds(g * GT, GT), :].rearrange("(t p) d -> p t d", p=P),
                             xres[:, bass.ds(g * GTT, GTT), :]).then_inc(y_sent, 16)
            sp.wait_ge(y_sent, G * 16)


def build(nc, a, out):
    with ExitStack() as ctx:
        env = {"banks": [ctx.enter_context(nc.psum_tensor(f"bank{n}", [P, 512], F32)) for n in range(8)],
               "u_dram": nc.dram_tensor("u_spill", (P, HID0 // P, NT * P), F32, kind="Internal").ap()}
        for name, shape in (("xres", [P, NT, D]), ("ident", [P, P]), ("mean_all", [P, NT]),
                            ("rstd_all", [P, NT]), ("amax_x", [P, B])):
            env[name] = ctx.enter_context(nc.sbuf_tensor(name, shape, F32))
        for layer in range(2):
            env[f"mask{layer}"], env[f"pick{layer}"] = a[f"mask{layer}"], a[f"pick{layer}"]
        ident_in = ctx.enter_context(nc.semaphore("ident_in"))
        with nc.Block() as block:
            @block.sync
            def _(sp):
                sp.dma_start(env["ident"][:], a["ident"]).then_inc(ident_in, 16)
                sp.wait_ge(ident_in, 16)

        attention(nc, env, 0, 16, 256, a["wqkv0"], a["wo0"], a["bq0"], a["bk0"], a["bv0"], a["bo0"],
                  a["gx0"], a["ctx_t"], a["x"])
        quantised_ffn(nc, env, a["w_up"], a["w_gate"], a["w_down"], a["gf0"])
        attention(nc, env, 1, 8, 512, a["wqkv1"], a["wo1"], None, None, None, a["bo1"], a["gx1"],
                  a["ctx_t"], None)
        butterfly_ffn(nc, env, a["w_exp"], a["b_exp"], a["up_coef"], a["up_bias"], a["down_coef"],
                      a["w_con_t"], a["out_bias"], a["gf1"], out)


def kernel(**inputs):
    import numpy as np
    import concourse.bacc as bacc
    from concourse.bass_utils import run_bass_kernel_spmd

    v = {k: np.asarray(x) for k, x in inputs.items()}

    def rows(vec):
        return np.ascontiguousarray(np.broadcast_to(vec.reshape(1, -1), (P, vec.size)))

    def columns(vec):
        return np.ascontiguousarray(vec.reshape(-1, P).T)

    def stage_coefs(w, transposed):
        n = np.arange(HID1)
        got = []
        for stage in range(w.shape[0]):
            s = 1 << stage
            pair, hi = (n // (2 * s)) * s + n % s, (n // s) % 2
            other = w[stage, pair, 1 - hi, hi] if transposed else w[stage, pair, hi, 1 - hi]
            got.append(np.stack([w[stage, pair, hi, hi], other]))
        return np.ascontiguousarray(np.stack(got[::-1] if transposed else got))

    def mask(d):
        return np.ascontiguousarray((np.arange(P)[:, None] // d == np.arange(P // d)[None, :]).astype(np.float32))

    def pick(heads):
        m = np.zeros((P, heads, S + 1), np.float32)
        for h in range(heads):
            m[h, h, :] = -1.0
        return m

    t = np.transpose
    arrays = {
        "x": v["x"].reshape(NT * P, D),
        "ctx_t": np.ascontiguousarray(v["ctx_1024"].reshape(B * S, D).T),
        "ident": np.eye(P, dtype=np.float32),
        "mask0": mask(16), "mask1": mask(64), "pick0": pick(16), "pick1": pick(8),
        "wqkv0": np.ascontiguousarray(np.concatenate([t(v["L0_xattn_Wq"]), t(v["L0_xattn_Wk"]), t(v["L0_xattn_Wv"])], 1)),
        "wo0": np.ascontiguousarray(t(v["L0_xattn_Wo"])),
        "bq0": columns(v["L0_xattn_bq"]), "bk0": columns(v["L0_xattn_bk"]),
        "bv0": rows(v["L0_xattn_bv"]), "bo0": rows(v["L0_xattn_bo"]),
        "wqkv1": np.ascontiguousarray(np.concatenate([v["L1_xattn_Wq"], v["L1_xattn_Wk"], v["L1_xattn_Wv"]], 1)),
        "wo1": v["L1_xattn_Wo"], "bo1": rows(v["L1_xattn_bo"]),
        "gx0": rows(v["g_xattn"][0:1]), "gx1": rows(v["g_xattn"][1:2]),
        "gf0": rows(v["g_ffn"][0:1]), "gf1": rows(v["g_ffn"][1:2]),
        "w_up": v["L0_ffn_w_up"], "w_gate": v["L0_ffn_w_gate"], "w_down": v["L0_ffn_w_down"],
        "w_exp": v["L1_ffn_W_exp"], "b_exp": v["L1_ffn_b_exp"].reshape(1, HID1),
        "up_coef": stage_coefs(v["L1_ffn_up_weights"], False), "up_bias": columns(v["L1_ffn_up_bias"]),
        "down_coef": stage_coefs(v["L1_ffn_down_weights"], True),
        "w_con_t": np.ascontiguousarray(t(v["L1_ffn_W_con"])),
        "out_bias": np.ascontiguousarray(np.stack([rows(v["L1_ffn_b_con"]), rows(v["L1_ffn_down_bias"])], 1)),
    }
    nc = bacc.Bacc("TRN2", target_bir_lowering=False, num_devices=1)
    feed, args = {}, {}
    for name, x in arrays.items():
        feed[f"in_{name}"] = np.ascontiguousarray(x)
        args[name] = nc.dram_tensor(f"in_{name}", x.shape, mybir.dt.from_np(x.dtype), kind="ExternalInput").ap()
    out = nc.dram_tensor("out_x", (NT * P, D), F32, kind="ExternalOutput").ap()
    build(nc, args, out)
    r = run_bass_kernel_spmd(nc, [feed], core_ids=[0])
    return r.results[0]["out_x"].reshape(B, T, D)
```

```python
from contextlib import ExitStack

import concourse.bass as bass
from concourse import mybir

F32 = mybir.dt.float32
F32R = mybir.dt.float32r
I16 = mybir.dt.int16
U16 = mybir.dt.uint16
ALU = mybir.AluOpType
ACT = mybir.ActivationFunctionType
AX = mybir.AxisListType
RMAX = bass.bass_isa.ReduceOp.max

P = 128
D = 256
DC = D // P
B = 16
T = 256
TT = T // P
S = 77
NT = B * TT
LN_EPS = 1e-5
BLOCK = 32
ACT_MAX = 32767.0
TINY = 1e-12
GT = 512
HID0 = 768
HID1 = 1024


def three_passes(nc, out, w_hi, w_lo, m_hi, m_lo, start, stop):
    nc.tensor.matmul(out, w_hi, m_hi, start=start, stop=False)
    nc.tensor.matmul(out, w_hi, m_lo, start=False, stop=False)
    return nc.tensor.matmul(out, w_lo, m_hi, start=False, stop=stop)


def free_semaphores(nc, sems):
    nc.clear_and_free_semaphores(sems)
    nc.all_engine_barrier()


def attention(nc, env, layer, heads, inner, wqkv, wo, bq, bk, bv, gbias, gate, ctx_t, x_in):
    d = inner // heads
    C = inner // P
    HPC = P // d
    HP = heads // 2
    NP = C // 2
    NG = TT * heads // 4
    DV = d + 1
    SCALE = float(d) ** -0.5
    first = x_in is not None
    xres, banks, ident = env["xres"], env["banks"], env["ident"]
    T0, T1, X0, X1, S0, S1, O0, O1 = banks
    wide = heads * DV > 512
    mx_banks = [X0] if wide else [X0, X1]
    NMX = len(mx_banks)

    def out_of(t, h):
        if wide and h == heads - 1:
            return X1[:, t * DV:(t + 1) * DV]
        return (O0, O1)[t][:, h * DV:(h + 1) * DV]

    sems = []
    ctx = ExitStack()
    with ctx:
        def sb(name, shape, dt=F32):
            return ctx.enter_context(nc.sbuf_tensor(f"a{layer}_{name}", shape, dt))

        def sem(name):
            sems.append(nc.alloc_semaphore(f"a{layer}_{name}"))
            return sems[-1]

        w_hi = sb("w_hi", [P, DC, 3 * inner], F32R)
        w_lo = sb("w_lo", [P, DC, 3 * inner], F32R)
        wo_hi = sb("wo_hi", [P, C, D], F32R)
        wo_lo = sb("wo_lo", [P, C, D], F32R)
        k_hi = sb("k_hi", [P, C, B * S], F32R)
        k_lo = sb("k_lo", [P, C, B * S], F32R)
        values = sb("values", [P, B, heads, DV])
        bqk = sb("bqk", [P, 2, C])
        bv_all = sb("bv_all", [P, inner])
        gb = sb("gb", [P, D])
        tg = sb("tg", [P, 1])
        minus_half = sb("minus_half", [P, TT])
        eps = sb("eps", [P, TT])
        head_mask = sb("head_mask", [P, HPC])
        pick = sb("pick", [P, heads, S + 1], F32R)

        setup = ExitStack()
        with setup:
            def tmp(name, shape, dt=F32):
                return setup.enter_context(nc.sbuf_tensor(f"a{layer}_{name}", shape, dt))

            w_raw = tmp("w_raw", [P, DC, 3 * inner])
            wo_raw = tmp("wo_raw", [P, C, D])
            c_raw = tmp("c_raw", [P, DC, B * S])
            c_hi = tmp("c_hi", [P, DC, B * S], F32R)
            c_lo = tmp("c_lo", [P, DC, B * S], F32R)
            bo_raw = tmp("bo_raw", [P, D])
            gate_raw = tmp("gate_raw", [P, 1])
            pick_raw = tmp("pick_raw", [P, heads, S + 1])
            w_in, c_in, o_in, small_in = sem("w_in"), sem("c_in"), sem("o_in"), sem("small_in")
            w_rounded, c_rounded, o_rounded = sem("w_rounded"), sem("c_rounded"), sem("o_rounded")
            w_split, c_split = sem("w_split"), sem("c_split")
            k_sum, k_rounded, k_done = sem("k_sum"), sem("k_rounded"), sem("k_done")
            v_sum, v_cleared, v_done, g_done = sem("v_sum"), sem("v_cleared"), sem("v_done"), sem("g_done")
            KN = [(0, 412), (412, 410), (822, 410)]
            KJ = [(c, n0, n) for c in range(C) for n0, n in KN]
            N_SMALL = 4 + (3 if first else 0)

            block = setup.enter_context(nc.Block())

            @block.sync
            def _(sp):
                sp.dma_start(w_raw[:], wqkv.rearrange("(c p) n -> p c n", p=P)).then_inc(w_in, 16)
                sp.dma_start(c_raw[:], ctx_t.rearrange("(c p) n -> p c n", p=P)).then_inc(c_in, 16)
                sp.dma_start(wo_raw[:], wo.rearrange("(c p) n -> p c n", p=P)).then_inc(o_in, 16)
                sp.dma_start(bo_raw[:], gbias).then_inc(small_in, 16)
                sp.dma_start(gate_raw[:], gate).then_inc(small_in, 16)
                sp.dma_start(head_mask[:], env[f"mask{layer}"]).then_inc(small_in, 16)
                sp.dma_start(pick_raw[:], env[f"pick{layer}"]).then_inc(small_in, 16)
                if first:
                    sp.dma_start(bqk[:, 0, :], bq).then_inc(small_in, 16)
                    sp.dma_start(bqk[:, 1, :], bk).then_inc(small_in, 16)
                    sp.dma_start(bv_all[:], bv).then_inc(small_in, 16)

            @block.gpsimd
            def _(pool):
                pool.memset(values[:], 0.0).then_inc(v_cleared, 1)
                pool.memset(minus_half[:], -0.5)
                pool.memset(eps[:], LN_EPS)
                pool.wait_ge(v_cleared, 1)
                pool.memset(values[:, :, :, d:DV], 1.0).then_inc(v_cleared, 1)

            @block.scalar
            def _(act):
                act.wait_ge(w_in, 16)
                act.activation(w_hi[:], w_raw[:], ACT.Copy).then_inc(w_rounded, 1)
                act.wait_ge(c_in, 16)
                act.activation(c_hi[:], c_raw[:], ACT.Copy).then_inc(c_rounded, 1)
                act.wait_ge(o_in, 16)
                act.activation(wo_hi[:], wo_raw[:], ACT.Copy).then_inc(o_rounded, 1)
                act.wait_ge(small_in, 16 * N_SMALL)
                act.activation(tg[:], gate_raw[:], ACT.Tanh).then_inc(g_done, 1)
                act.activation(pick[:], pick_raw[:], ACT.Copy)
                for n, (c, n0, nn) in enumerate(KJ):
                    act.wait_ge(k_sum, n + 1)
                    bias = bqk[:, 1, c:c + 1] if first else 0.0
                    act.activation(k_hi[:, c, n0:n0 + nn], (T0, T1)[n % 2][:, 0:nn], ACT.Identity,
                                   bias=bias).then_inc(k_rounded, 1)

            @block.vector
            def _(dve):
                dve.wait_ge(w_rounded, 1)
                dve.tensor_tensor(w_lo[:], w_raw[:], w_hi[:].bitcast(F32), ALU.subtract).then_inc(w_split, 1)
                dve.wait_ge(c_rounded, 1)
                dve.tensor_tensor(c_lo[:], c_raw[:], c_hi[:].bitcast(F32), ALU.subtract).then_inc(c_split, 1)
                dve.wait_ge(o_rounded, 1)
                dve.tensor_tensor(wo_lo[:], wo_raw[:], wo_hi[:].bitcast(F32), ALU.subtract)
                dve.wait_ge(g_done, 1)
                dve.tensor_scalar(gb[:], bo_raw[:], tg[:, 0:1], None, ALU.mult)
                for n, (c, n0, nn) in enumerate(KJ):
                    dve.wait_ge(k_rounded, n + 1)
                    bias = bqk[:, 1, c:c + 1] if first else 0.0
                    dve.scalar_tensor_tensor(
                        out=k_lo[:, c, n0:n0 + nn], in0=(T0, T1)[n % 2][:, 0:nn], scalar=bias,
                        in1=k_hi[:, c, n0:n0 + nn].bitcast(F32), op0=ALU.add, op1=ALU.subtract,
                    ).then_inc(k_done, 1)
                dve.wait_ge(v_cleared, 2)
                for b in range(B):
                    dve.wait_ge(v_sum, b + 1)
                    src = (S0, S1)[b % 2][0:S, 0:inner].rearrange("p (h v) -> p h v", h=heads)
                    dst = values[0:S, b, :, 0:d]
                    if first:
                        dve.tensor_tensor(dst, src, bv_all[0:S, :].rearrange("p (h v) -> p h v", h=heads),
                                          ALU.add).then_inc(v_done, 1)
                    else:
                        dve.tensor_copy(dst, src).then_inc(v_done, 1)

            @block.tensor
            def _(pe):
                pe.wait_ge(w_split, 1)
                pe.wait_ge(c_split, 1)
                for n, (c, n0, nn) in enumerate(KJ):
                    if n >= 2:
                        pe.wait_ge(k_done, n - 1)
                    for kc in range(DC):
                        cols = slice(inner + c * P, inner + (c + 1) * P)
                        last = three_passes(nc, (T0, T1)[n % 2][:, 0:nn], w_hi[:, kc, cols], w_lo[:, kc, cols],
                                            c_hi[:, kc, n0:n0 + nn], c_lo[:, kc, n0:n0 + nn],
                                            kc == 0, kc == DC - 1)
                    last.then_inc(k_sum, 1)
                for b in range(B):
                    if b >= 2:
                        pe.wait_ge(v_done, b - 1)
                    for kc in range(DC):
                        last = three_passes(nc, (S0, S1)[b % 2][0:S, 0:inner],
                                            c_hi[:, kc, b * S:(b + 1) * S], c_lo[:, kc, b * S:(b + 1) * S],
                                            w_hi[:, kc, 2 * inner:3 * inner], w_lo[:, kc, 2 * inner:3 * inner],
                                            kc == 0, kc == DC - 1)
                    last.then_inc(v_sum, 1)

        mv = sb("mv", [P, TT, 2])
        bn = sb("bn", [P, TT, 6])
        var = sb("var", [P, TT])
        rstd = sb("rstd", [P, TT])
        xn = sb("xn", [P, TT, D])
        xt_hi = sb("xt_hi", [P, DC, T], F32R)
        xt_lo = sb("xt_lo", [P, DC, T], F32R)
        q_hi = sb("q_hi", [P, 2, C, T], F32R)
        q_lo = sb("q_lo", [P, 2, C, T], F32R)
        kb_hi = sb("kb_hi", [P, 2, C, HPC, S], F32R)
        kb_lo = sb("kb_lo", [P, 2, C, HPC, S], F32R)
        maxima = sb("maxima", [P, TT, heads])
        mt = sb("mt", [P, 2, T], F32R)
        prob = sb("prob", [P, 2, 2, T])
        rden = sb("rden", [P, TT, heads])
        att = sb("att", [P, TT, inner])
        at_hi = sb("at_hi", [P, C, T], F32R)
        at_lo = sb("at_lo", [P, C, T], F32R)
        mv2 = sb("mv2", [P, TT, 2])
        bn2 = sb("bn2", [P, TT, 6])
        var2 = sb("var2", [P, TT])
        xn2 = sb("xn2", [P, TT, D])

        x_loaded = [sem("x_loaded0"), sem("x_loaded1")]
        cleared = sem("cleared")
        passed = sem("passed")
        ln_bn, ln_stats, ln_eps, ln_rstd, ln_xn, biased = (sem(x) for x in (
            "ln_bn", "ln_stats", "ln_eps", "ln_rstd", "ln_xn", "biased"))
        xt_ready, xt_rounded, xt_split = sem("xt_ready"), sem("xt_rounded"), sem("xt_split")
        q_ready, q_rounded, q_split = sem("q_ready"), sem("q_rounded"), sem("q_split")
        kb_ready = sem("kb_ready")
        mx_scores, mx_taken, mt_ready, mt_copied = (sem(x) for x in (
            "mx_scores", "mx_taken", "mt_ready", "mt_copied"))
        scores, probs, outs = sem("scores"), sem("probs"), sem("outs")
        den_ready, att_ready = sem("den_ready"), sem("att_ready")
        at_ready, at_rounded, at_split = sem("at_ready"), sem("at_rounded"), sem("at_split")
        proj_ready, x_updated = sem("proj_ready"), sem("x_updated")
        n_bn, n_stats, n_eps, n_rstd, n_xn, n_max = (sem(x) for x in (
            "n_bn", "n_stats", "n_eps", "n_rstd", "n_xn", "n_max"))

        if HP == 8:
            SLOT = ("s0 xt kb s1 p0 q0 s2 p1 at0 s3 p2 mx0 mx1 pr0 pr1 st1 s4 p3 mx2 mx3 ln s5 p4 mx4 mx5 xn "
                    "s6 p5 mx6 mx7 st2 s7 p6 mt p7 norm").split()
        else:
            SLOT = ("s0 xt kb s1 p0 q0 at0 q1 s2 p1 at1 mx0 s3 mx1 p2 mx2 p3 mx3 ln pr0 norm mt xn pr1").split()
        FRONT = {"kb", "xt", "mt"} | {f"q{n}" for n in range(NP)} | {f"mx{n}" for n in range(NG)}
        BACK = {"pr0", "pr1", "st1", "st2"} | {f"at{n}" for n in range(NP)}

        def slots(eng, step):
            def slot(b, par, pre=True, front=True, middle=True, back=True):
                for what in SLOT:
                    if what in ("ln", "xn"):
                        if pre:
                            step(what, b + 2, par)
                    elif what in FRONT:
                        if front:
                            step(what, b + 1, 1 - par)
                    elif what in BACK:
                        if back:
                            step(what, b - 1, 1 - par)
                    elif middle:
                        step(what, b, par)

            slot(-2, 0, front=False, middle=False, back=False)
            slot(-1, 1, middle=False, back=False)
            slot(0, 0, back=False)
            with eng.Fori(0, (B - 4) // 2) as j:
                slot(j * 2 + 1, 1)
                slot(j * 2 + 2, 0)
            slot(B - 3, 1)
            slot(B - 2, 0, pre=False)
            slot(B - 1, 1, pre=False, front=False)
            slot(B, 0, pre=False, front=False, middle=False)

        block = ctx.enter_context(nc.Block())

        @block.sync
        def _(sp):
            if first:
                def load(b, par):
                    sp.dma_start(xres[:, bass.ds(b * TT, TT), :],
                                 x_in[bass.ds(b * T, T), :].rearrange("(t p) d -> p t d", p=P),
                                 ).then_inc(x_loaded[par], 16)

                load(0, 0)
                load(1, 1)
                with sp.Fori(1, B // 2) as j:
                    for par in range(2):
                        sp.wait_ge(x_loaded[par], j * 16)
                        load(j * 2 + par, par)

        @block.gpsimd
        def _(pool):
            pool.memset(mt[:].bitcast(F32), 0.0).then_inc(cleared, 1)
            pool.memset(prob[:], 0.0).then_inc(cleared, 1)

            def step(what, b, par):
                if what == "ln":
                    pool.wait_ge(ln_stats, b + 1)
                    pool.tensor_tensor(var[:], mv[:, :, 1], eps[:], ALU.add).then_inc(ln_eps, 1)
                    pool.wait_ge(ln_eps, b + 1)
                    pool.tensor_tensor(rstd[:], var[:], minus_half[:], ALU.pow).then_inc(ln_rstd, 1)
                    pool.wait_ge(ln_xn, b + 1)
                    for t in range(TT):
                        x = xres[:, bass.ds(b * TT + t, 1), :].rearrange("p o d -> p (o d)")
                        last = pool.tensor_tensor(x, x, gb[:], ALU.add)
                    last.then_inc(biased, 1)
                elif what == "st1" and first:
                    pool.wait_ge(n_stats, b + 1)
                    pool.tensor_tensor(var2[:], mv2[:, :, 1], eps[:], ALU.add).then_inc(n_eps, 1)
                    pool.wait_ge(n_eps, b + 1)
                    pool.tensor_tensor(env["rstd_all"][:, bass.ds(b * TT, TT)], var2[:], minus_half[:],
                                       ALU.pow).then_inc(n_rstd, 1)

            slots(pool, step)

        @block.scalar
        def _(act):
            act.wait_ge(cleared, 2)

            def step(what, b, par):
                if what == "xt":
                    act.wait_ge(xt_ready, b + 1)
                    act.activation(xt_hi[:], T0[:, :], ACT.Copy).then_inc(xt_rounded, 1)
                elif what[0] == "q":
                    n = int(what[1])
                    act.wait_ge(q_ready, b * NP + n + 1)
                    src = (T0, X0)[n]
                    for c in range(2):
                        bias = bqk[:, 0, 2 * n + c:2 * n + c + 1] if first else 0.0
                        last = act.activation(q_hi[:, par, 2 * n + c, :], src[:, c * T:(c + 1) * T],
                                              ACT.Identity, bias=bias)
                    last.then_inc(q_rounded, 1)
                elif what == "mt":
                    act.wait_ge(mt_ready, b + 1)
                    act.activation(mt[0:heads, par, :], T0[0:heads, 0:T], ACT.Copy).then_inc(mt_copied, 1)
                elif what[0] == "s" and what[1] != "t":
                    n = int(what[1])
                    act.wait_ge(scores, b * HP + n + 1)
                    if not (isinstance(b, int) and b == 0 and n < 2):
                        act.wait_ge(outs, b * HP + n - 1)
                    act.activation(prob[0:S, n % 2, :, :].rearrange("p a b -> p (a b)"),
                                   (S0, S1)[n % 2][0:S, :], ACT.Exp, scale=SCALE).then_inc(probs, 1)
                elif what[:2] == "at":
                    n = int(what[2])
                    act.wait_ge(at_ready, b * NP + n + 1)
                    act.activation(at_hi[:, 2 * n:2 * n + 2, :].rearrange("p a b -> p (a b)"), T1[:, :],
                                   ACT.Copy).then_inc(at_rounded, 1)

            slots(act, step)

        @block.vector
        def _(dve):
            dve.sem_inc(x_updated, 1)

            def xtile(b, t):
                return xres[:, bass.ds(b * TT + t, 1), :].rearrange("p o d -> p (o d)")

            def step(what, b, par):
                if what == "norm":
                    dve.wait_ge(outs, (b + 1) * HP)
                    for t in range(TT):
                        near = heads - 1 if wide else heads
                        o = (O0, O1)[t][:, 0:near * DV].rearrange("p (h v) -> p h v", v=DV)
                        last = dve.reciprocal(rden[:, t, 0:near], o[:, :, d])
                        if wide:
                            last = dve.reciprocal(rden[:, t, near:heads], out_of(t, near)[:, d:DV])
                    last.then_inc(den_ready, 1)
                    dve.wait_ge(den_ready, b + 1)
                    for t in range(TT):
                        near = heads - 1 if wide else heads
                        o = (O0, O1)[t][:, 0:near * DV].rearrange("p (h v) -> p h v", v=DV)
                        a = att[:, t, :].rearrange("p (h v) -> p h v", v=d)
                        last = dve.tensor_tensor(a[:, 0:near, :], o[:, :, 0:d],
                                                 rden[:, t, 0:near].unsqueeze(2).to_broadcast([P, near, d]),
                                                 ALU.mult)
                        if wide:
                            last = dve.tensor_scalar(a[:, near, :], out_of(t, near)[:, 0:d],
                                                     rden[:, t, near:heads], None, ALU.mult)
                    last.then_inc(att_ready, 1)
                elif what == "ln":
                    if first:
                        if isinstance(b, int):
                            dve.wait_ge(x_loaded[par], 16 * (b // 2 + 1))
                        else:
                            dve.wait_ge(x_loaded[par], (b - par) * 8 + 16)
                            dve.sem_inc(passed, 1)
                    for t in range(TT):
                        last = dve.bn_stats(bn[:, t, :], xtile(b, t))
                    last.then_inc(ln_bn, 1)
                    dve.wait_ge(ln_bn, b + 1)
                    dve.sem_inc(passed, 1)
                    for t in range(TT):
                        last = dve.bn_aggr(mv[:, t, :], bn[:, t, :])
                    last.then_inc(ln_stats, 1)
                elif what == "xn":
                    dve.wait_ge(ln_rstd, b + 1)
                    for t in range(TT):
                        last = dve.tensor_scalar(xn[:, t, :], xtile(b, t), mv[:, t, 0:1], rstd[:, t:t + 1],
                                                 ALU.subtract, ALU.mult)
                    last.then_inc(ln_xn, 1)
                elif what == "kb":
                    for full, masked in ((k_hi, kb_hi), (k_lo, kb_lo)):
                        for c in range(C):
                            src = full[:, c, bass.ds(b * S, S)].bitcast(F32)
                            last = dve.tensor_tensor(masked[:, par, c, :, :],
                                                     src.unsqueeze(1).to_broadcast([P, HPC, S]),
                                                     head_mask[:].unsqueeze(2).to_broadcast([P, HPC, S]),
                                                     ALU.mult)
                    last.then_inc(kb_ready, 1)
                elif what == "xt":
                    dve.wait_ge(xt_rounded, b + 1)
                    dve.tensor_tensor(xt_lo[:].rearrange("p a b -> p (a b)"), T0[:, :],
                                      xt_hi[:].rearrange("p a b -> p (a b)").bitcast(F32),
                                      ALU.subtract).then_inc(xt_split, 1)
                elif what[0] == "q":
                    n = int(what[1])
                    dve.wait_ge(q_rounded, b * NP + n + 1)
                    src = (T0, X0)[n]
                    for c in range(2):
                        bias = bqk[:, 0, 2 * n + c:2 * n + c + 1] if first else 0.0
                        last = dve.scalar_tensor_tensor(
                            out=q_lo[:, par, 2 * n + c, :], in0=src[:, c * T:(c + 1) * T], scalar=bias,
                            in1=q_hi[:, par, 2 * n + c, :].bitcast(F32), op0=ALU.add, op1=ALU.subtract)
                    last.then_inc(q_split, 1)
                elif what[:2] == "mx":
                    g = int(what[2])
                    t, h0 = g // (NG // TT), 4 * (g % (NG // TT))
                    dve.wait_ge(mx_scores, b * NG + g + 1)
                    dve.tensor_reduce(maxima[:, t, h0:h0 + 4],
                                      mx_banks[g % NMX][:, 0:4 * S].rearrange("p (h s) -> p h s", s=S),
                                      AX.X, ALU.max).then_inc(mx_taken, 1)
                elif what[:2] == "at":
                    n = int(what[2])
                    dve.wait_ge(at_rounded, b * NP + n + 1)
                    dve.tensor_tensor(at_lo[:, 2 * n:2 * n + 2, :].rearrange("p a b -> p (a b)"), T1[:, :],
                                      at_hi[:, 2 * n:2 * n + 2, :].rearrange("p a b -> p (a b)").bitcast(F32),
                                      ALU.subtract).then_inc(at_split, 1)
                elif what == "pr1":
                    dve.wait_ge(proj_ready, b + 1)
                    dve.wait_ge(biased, b + 1)
                    for t in range(TT):
                        x = xtile(b, t)
                        last = dve.scalar_tensor_tensor(out=x, in0=T1[:, t * D:(t + 1) * D], scalar=tg[:, 0:1],
                                                        in1=x, op0=ALU.mult, op1=ALU.add)
                    last.then_inc(x_updated, 1)
                elif what == "st1" and first:
                    dve.wait_ge(x_updated, b + 2)
                    dve.sem_inc(passed, 1)
                    for t in range(TT):
                        last = dve.bn_stats(bn2[:, t, :], xtile(b, t))
                    last.then_inc(n_bn, 1)
                    dve.wait_ge(n_bn, b + 1)
                    dve.sem_inc(passed, 1)
                    for t in range(TT):
                        last = dve.bn_aggr(mv2[:, t, :], bn2[:, t, :])
                    last.then_inc(n_stats, 1)
                elif what == "st2" and first:
                    dve.wait_ge(n_rstd, b + 1)
                    dve.tensor_copy(env["mean_all"][:, bass.ds(b * TT, TT)], mv2[:, :, 0])
                    for t in range(TT):
                        last = dve.tensor_scalar(xn2[:, t, :], xtile(b, t), mv2[:, t, 0:1],
                                                 env["rstd_all"][:, bass.ds(b * TT + t, 1)],
                                                 ALU.subtract, ALU.mult)
                    last.then_inc(n_xn, 1)
                    dve.wait_ge(n_xn, b + 1)
                    dve.tensor_reduce(env["amax_x"][:, bass.ds(b, 1)],
                                      xn2[:].rearrange("p t d -> p (t d)"), AX.X, ALU.max,
                                      apply_absolute_value=True).then_inc(n_max, 1)

            slots(dve, step)

        @block.tensor
        def _(pe):
            def step(what, b, par):
                if what == "xt":
                    pe.wait_ge(ln_xn, b + 1)
                    pe.wait_ge(mt_copied, b)
                    for c in range(DC):
                        for t in range(TT):
                            last = pe.transpose(T0[:, c * T + t * P:c * T + (t + 1) * P],
                                                xn[:, t, c * P:(c + 1) * P], ident[:])
                    last.then_inc(xt_ready, 1)
                elif what[0] == "q":
                    n = int(what[1])
                    pe.wait_ge(xt_split, b + 1)
                    for c in range(2):
                        cols = slice((2 * n + c) * P, (2 * n + c + 1) * P)
                        for kc in range(DC):
                            last = three_passes(nc, (T0, X0)[n][:, c * T:(c + 1) * T],
                                                w_hi[:, kc, cols], w_lo[:, kc, cols],
                                                xt_hi[:, kc, :], xt_lo[:, kc, :], kc == 0, kc == DC - 1)
                    last.then_inc(q_ready, 1)
                elif what[:2] == "mx":
                    g = int(what[2])
                    t, h0 = g // (NG // TT), 4 * (g % (NG // TT))
                    if g == 0:
                        pe.wait_ge(kb_ready, b + 1)
                        pe.wait_ge(q_split, (b + 1) * NP)
                    if not (isinstance(b, int) and b == 0 and g < NMX):
                        pe.wait_ge(mx_taken, b * NG + g + 1 - NMX)
                    per = min(4, HPC)
                    for h in range(h0, h0 + 4, per):
                        c, r = h // HPC, h % HPC
                        last = pe.matmul(mx_banks[g % NMX][:, (h - h0) * S:(h - h0 + per) * S],
                                         q_hi[:, par, c, t * P:(t + 1) * P],
                                         kb_hi[:, par, c, r:r + per, :].rearrange("p a b -> p (a b)"),
                                         start=True, stop=True)
                    last.then_inc(mx_scores, 1)
                elif what == "mt":
                    pe.wait_ge(mx_taken, (b + 1) * NG)
                    for t in range(TT):
                        last = pe.transpose(T0[0:heads, t * P:(t + 1) * P], maxima[:, t, :], ident[:])
                    last.then_inc(mt_ready, 1)
                elif what[0] == "s" and what[1] != "t":
                    n = int(what[1])
                    if n == 0:
                        pe.wait_ge(mt_copied, b + 1)
                    if not (isinstance(b, int) and b == 0 and n < 2):
                        pe.wait_ge(probs, b * HP + n - 1)
                    for hh in range(2):
                        h = 2 * n + hh
                        c, r = h // HPC, h % HPC
                        out = (S0, S1)[n % 2][0:S, hh * T:(hh + 1) * T]
                        three_passes(nc, out, kb_hi[:, par, c, r, :], kb_lo[:, par, c, r, :],
                                     q_hi[:, par, c, :], q_lo[:, par, c, :], True, False)
                        last = pe.matmul(out, pick[:, h, 0:S], mt[:, par, :], start=False, stop=True)
                    last.then_inc(scores, 1)
                elif what[0] == "p" and what[1] != "r":
                    n = int(what[1])
                    pe.wait_ge(probs, b * HP + n + 1)
                    if n == 0:
                        pe.wait_ge(att_ready, b)
                    for hh in range(2):
                        h = 2 * n + hh
                        for t in range(TT):
                            v = values[:, bass.ds(b, 1), h, :].rearrange("p o v -> p (o v)")
                            last = pe.matmul(out_of(t, h), prob[:, n % 2, hh, t * P:(t + 1) * P], v,
                                             start=True, stop=True)
                    last.then_inc(outs, 1)
                elif what[:2] == "at":
                    n = int(what[2])
                    pe.wait_ge(att_ready, b + 1)
                    if n == 0:
                        pe.wait_ge(x_updated, b + 1)
                    else:
                        pe.wait_ge(at_split, b * NP + n)
                    for c in range(2):
                        for t in range(TT):
                            cols = slice((2 * n + c) * P, (2 * n + c + 1) * P)
                            last = pe.transpose(T1[:, c * T + t * P:c * T + (t + 1) * P], att[:, t, cols],
                                                ident[:])
                    last.then_inc(at_ready, 1)
                elif what[:2] == "pr":
                    t = int(what[2])
                    if t == 0:
                        pe.wait_ge(at_split, (b + 1) * NP)
                    for c in range(C):
                        last = three_passes(nc, T1[:, t * D:(t + 1) * D],
                                            at_hi[:, c, t * P:(t + 1) * P], at_lo[:, c, t * P:(t + 1) * P],
                                            wo_hi[:, c, :], wo_lo[:, c, :], c == 0, c == C - 1)
                    if t == TT - 1:
                        last.then_inc(proj_ready, 1)

            slots(pe, step)

    free_semaphores(nc, sems)


def quantised_ffn(nc, env, w_up, w_gate, w_down, gate, butterfly):
    bf = butterfly
    xres, banks, ident = env["xres"], env["banks"], env["ident"]
    T0, T1, X0, X1, S0, S1, O0, O1 = banks
    FT = HID0 // P
    G = NT * P // GT
    GTT = GT // P
    sems = []
    ctx = ExitStack()
    with ctx:
        def sb(name, shape, dt=F32):
            return ctx.enter_context(nc.sbuf_tensor(f"f0_{name}", shape, dt))

        def sem(name):
            sems.append(nc.alloc_semaphore(f"f0_{name}"))
            return sems[-1]

        scales = sb("scales", [P, 5])
        codes = sb("codes", [P, 5])
        small = sb("small", [P, 4])
        unit = sb("unit", [P, 5])
        tg = sb("tg", [P, 1])
        amax = sb("amax", [P, 2, G, FT])
        SX, SG, SU, S2, SO = range(5)
        d_hi = sb("d_hi", [P, FT, D], F32R)
        d_lo = sb("d_lo", [P, FT, D], F32R)
        hid = sb("hid", [P, FT, NT * P])
        HT = HID1 // P
        TOP = HT.bit_length() - 1
        LOW = P.bit_length() - 1
        top_coef = sb("top_coef", [P, 2, TOP, 2, HT])
        low_coef = sb("low_coef", [P, 2, LOW, 2, HT])
        wide = ExitStack()
        w_hi = wide.enter_context(nc.sbuf_tensor("f0_w_hi", [P, 2, DC, HID0], F32R))
        w_lo = wide.enter_context(nc.sbuf_tensor("f0_w_lo", [P, 2, DC, HID0], F32R))

        def scale_steps(dve, k, done, at):
            dve.tensor_scalar(small[:, 2:3], small[:, 0:1], unit[:, k:k + 1], 1.0 / ACT_MAX,
                              ALU.mult, ALU.mult).then_inc(done, 1)
            dve.wait_ge(done, at + 1)
            dve.tensor_scalar(scales[:, k:k + 1], small[:, 2:3], TINY, None, ALU.max).then_inc(done, 1)
            dve.wait_ge(done, at + 2)
            dve.reciprocal(small[:, 3:4], scales[:, k:k + 1]).then_inc(done, 1)
            dve.wait_ge(done, at + 3)
            dve.tensor_tensor(codes[:, k:k + 1], small[:, 3:4], unit[:, k:k + 1], ALU.mult).then_inc(done, 1)
            dve.wait_ge(done, at + 4)

        def top_stage(pool, y, own, pair, net, i, multiplied, added, at):
            n = y.shape[2]
            r = 1 << i if net == 0 else HT >> (i + 1)
            pool.tensor_tensor(own, y, top_coef[:, net, i, 0, :].unsqueeze(2).to_broadcast([P, HT, n]), ALU.mult)
            yv, pv, cv = (x.rearrange("p (k two s) d -> p k two s d", two=2, s=r) for x in (
                y, pair, top_coef[:, net, i, 1, :].unsqueeze(2).to_broadcast([P, HT, n])))
            for half in range(2):
                for k in range(HT // (2 * r)):
                    last = pool.tensor_tensor(pv[:, k, half, :, :], yv[:, k, 1 - half, :, :], cv[:, k, half, :, :],
                                              ALU.mult)
            last.then_inc(multiplied, 1)
            pool.wait_ge(multiplied, at + 1)
            pool.tensor_tensor(y, own, pair, ALU.add).then_inc(added, 1)
            pool.wait_ge(added, at + 1)

        with ExitStack() as setup:
            W = 3 * FT * D
            NB = W // BLOCK
            raw = setup.enter_context(nc.sbuf_tensor("f0_raw", [P, 3 * FT, D], F32))
            wcode = setup.enter_context(nc.sbuf_tensor("f0_wcode", [P, W], I16))
            wval = raw
            bs = setup.enter_context(nc.sbuf_tensor("f0_bs", [P, 3, NB], F32))
            w_in, q_step, w_quantised = sem("w_in"), sem("q_step"), sem("w_quantised")
            turned, w_rounded, w_split = sem("turned"), sem("w_rounded"), sem("w_split")
            x_max, x_all, x_scale = sem("x_max"), sem("x_all"), sem("x_scale")
            turns = []
            for net in range(2):
                for c in range(DC):
                    for f0 in range(0, FT, 3):
                        turns.append(([(net * FT + f, c * P) for f in range(f0, f0 + 3)],
                                      (w_hi[:, net, c, f0 * P:(f0 + 3) * P], w_lo[:, net, c, f0 * P:(f0 + 3) * P])))
            for f in range(FT):
                turns.append(([(2 * FT + 3 * o + f // 2, (f % 2) * P) for o in range(DC)],
                              (d_hi[:, f, :], d_lo[:, f, :])))
            block = setup.enter_context(nc.Block())

            @block.sync
            def _(sp):
                sp.dma_start(raw[:, 0:FT, :], w_gate.rearrange("(f p) d -> p f d", p=P)).then_inc(w_in, 16)
                sp.dma_start(raw[:, FT:2 * FT, :], w_up.rearrange("(f p) d -> p f d", p=P)).then_inc(w_in, 16)
                for o in range(DC):
                    sp.dma_start(raw[:, 2 * FT + 3 * o:2 * FT + 3 * o + 3, :].rearrange("p f d -> p (f d)"),
                                 w_down[o * P:(o + 1) * P, :]).then_inc(w_in, 16)
                sp.dma_start(tg[:], gate).then_inc(w_in, 16)

            @block.vector
            def _(dve):
                flat = raw[:].rearrange("p f d -> p (f d)").rearrange("p (n k) -> p n k", k=BLOCK)
                dve.wait_ge(w_in, 16 * 5)
                dve.tensor_reduce(bs[:, 0, :], flat, AX.X, ALU.max, apply_absolute_value=True).then_inc(q_step, 1)
                dve.wait_ge(q_step, 1)
                dve.tensor_scalar(bs[:, 1, :], bs[:, 0, :], 1.0 / 7.0, TINY, ALU.mult, ALU.max).then_inc(q_step, 1)
                dve.wait_ge(q_step, 2)
                dve.reciprocal(bs[:, 2, :], bs[:, 1, :]).then_inc(q_step, 1)
                dve.wait_ge(q_step, 3)
                cv = wcode[:].rearrange("p (n k) -> p n k", k=BLOCK)
                dve.tensor_tensor(cv, flat, bs[:, 2, :].unsqueeze(2).to_broadcast([P, NB, BLOCK]),
                                  ALU.mult).then_inc(q_step, 1)
                dve.wait_ge(q_step, 4)
                dve.tensor_scalar(wcode[:], wcode[:], -8.0, 7.0, ALU.max, ALU.min).then_inc(q_step, 1)
                dve.wait_ge(q_step, 5)
                dve.tensor_tensor(wval[:].rearrange("p f d -> p (f d)").rearrange("p (n k) -> p n k", k=BLOCK), cv,
                                  bs[:, 1, :].unsqueeze(2).to_broadcast([P, NB, BLOCK]),
                                  ALU.mult).then_inc(w_quantised, 1)
                for n, (pieces, (hi, lo)) in enumerate(turns):
                    dve.wait_ge(w_rounded, n + 1)
                    dve.tensor_tensor(lo, (T0, T1)[n % 2][:, 0:len(pieces) * P], hi.bitcast(F32),
                                      ALU.subtract).then_inc(w_split, 1)
                dve.memset(unit[:, SX:SX + 1], 1.0)
                dve.tensor_reduce(small[:, 1:2], env["amax_x"][:], AX.X, ALU.max).then_inc(x_max, 1)
                dve.wait_ge(x_all, 1)
                scale_steps(dve, SX, x_scale, 0)

            @block.gpsimd
            def _(pool):
                pool.wait_ge(x_max, 1)
                pool.partition_all_reduce(small[:, 0:1], small[:, 1:2], P, RMAX).then_inc(x_all, 1)

            @block.tensor
            def _(pe):
                pe.wait_ge(w_quantised, 1)
                for n, (pieces, _) in enumerate(turns):
                    if n >= 2:
                        pe.wait_ge(w_split, n - 1)
                    for i, (tile, col) in enumerate(pieces):
                        last = pe.transpose((T0, T1)[n % 2][:, i * P:(i + 1) * P], wval[:, tile, col:col + P],
                                            ident[:])
                    last.then_inc(turned, 1)

            @block.scalar
            def _(act):
                for n, (pieces, (hi, lo)) in enumerate(turns):
                    act.wait_ge(turned, n + 1)
                    act.activation(hi, (T0, T1)[n % 2][:, 0:len(pieces) * P], ACT.Copy).then_inc(w_rounded, 1)
                act.wait_ge(w_in, 16 * 5)
                act.activation(tg[:], tg[:], ACT.Tanh)

        with wide, ExitStack() as ph:
            def tmp(name, shape, dt=F32):
                return ph.enter_context(nc.sbuf_tensor(f"f0_{name}", shape, dt))

            xn = tmp("xn", [P, GTT, D])
            xcode = tmp("xcode", [P, GTT, D], I16)
            xt_hi = tmp("xt_hi", [P, 2, DC, GT], F32R)
            xt_lo = tmp("xt_lo", [P, 2, DC, GT], F32R)
            NU = 3
            ubuf = tmp("ubuf", [P, NU, GT])
            x_normed, x_coded, x_float, xt_ready, xt_rounded, xt_split = (sem(x) for x in (
                "x_normed", "x_coded", "x_float", "xt_ready", "xt_rounded", "xt_split"))
            prods, stored, maxed = sem("prods"), sem("stored"), sem("maxed")
            u_sent = [sem(f"u_sent{n}") for n in range(NU)]
            mm = [X0, X1, S0, S1, O0, O1]
            M = 2 * FT
            HW = D // 2
            z = tmp("z", [P, HT, HW])
            z_own = tmp("z_own", [P, HT, HW])
            z_pair = tmp("z_pair", [P, HT, HW])
            coef_in, z_in, z_mul, z_add, z_sent = (sem(x) for x in ("coef_in", "z_in", "z_mul", "z_add", "z_sent"))
            block = ph.enter_context(nc.Block())

            def slots(eng, step):
                def slot(g, par, front=True, back=True):
                    for n in range(M):
                        if front and n == 1:
                            step("ln", 0, g + 1, 1 - par)
                        if front and n == 5:
                            step("x", 0, g + 1, 1 - par)
                        if back:
                            step("m", n, g, par)

                slot(-1, 1, back=False)
                slot(0, 0)
                with eng.Fori(0, (G - 2) // 2) as j:
                    slot(j * 2 + 1, 1)
                    slot(j * 2 + 2, 0)
                slot(G - 1, 1, front=False)

            @block.vector
            def _(dve):
                def step(what, n, g, par):
                    if what == "ln":
                        for t in range(GTT):
                            last = dve.tensor_scalar(
                                xn[:, t, :], xres[:, bass.ds(g * GTT + t, 1), :].rearrange("p o d -> p (o d)"),
                                env["mean_all"][:, bass.ds(g * GTT + t, 1)],
                                env["rstd_all"][:, bass.ds(g * GTT + t, 1)], ALU.subtract, ALU.mult)
                        last.then_inc(x_normed, 1)
                        dve.wait_ge(x_normed, g + 1)
                        dve.tensor_scalar(xcode[:], xn[:], codes[:, SX:SX + 1], None, ALU.mult).then_inc(x_coded, 1)
                        dve.wait_ge(x_coded, g + 1)
                        dve.tensor_copy(xn[:], xcode[:]).then_inc(x_float, 1)
                    elif what == "x":
                        for c in range(DC):
                            dve.wait_ge(xt_rounded, g * DC + c + 1)
                            dve.tensor_tensor(xt_lo[:, par, c, :], (T0, T1)[c][:, :],
                                              xt_hi[:, par, c, :].bitcast(F32), ALU.subtract).then_inc(xt_split, 1)
                    else:
                        dve.wait_ge(stored, g * M + n + 1)
                        dve.tensor_reduce(amax[:, n % 2, bass.ds(g, 1), n // 2], mm[n % 6][:, :], AX.X, ALU.max,
                                          apply_absolute_value=True).then_inc(maxed, 1)

                slots(dve, step)

            @block.tensor
            def _(pe):
                def step(what, n, g, par):
                    if what == "x":
                        pe.wait_ge(x_float, g + 1)
                        for c in range(DC):
                            pe.wait_ge(xt_split, g * DC)
                            for t in range(GTT):
                                last = pe.transpose((T0, T1)[c][:, t * P:(t + 1) * P],
                                                    xn[:, t, c * P:(c + 1) * P], ident[:])
                            last.then_inc(xt_ready, 1)
                    elif what == "m":
                        if n == 0:
                            pe.wait_ge(xt_split, (g + 1) * DC)
                        if not (isinstance(g, int) and g == 0 and n < 6):
                            pe.wait_ge(maxed, g * M + n - 5)
                        f = n // 2
                        for c in range(DC):
                            last = three_passes(nc, mm[n % 6][:, :],
                                                w_hi[:, n % 2, c, f * P:(f + 1) * P],
                                                w_lo[:, n % 2, c, f * P:(f + 1) * P],
                                                xt_hi[:, par, c, :], xt_lo[:, par, c, :], c == 0, c == DC - 1)
                        last.then_inc(prods, 1)

                slots(pe, step)

            @block.scalar
            def _(act):
                def step(what, n, g, par):
                    if what == "x":
                        for c in range(DC):
                            act.wait_ge(xt_ready, g * DC + c + 1)
                            act.activation(xt_hi[:, par, c, :], (T0, T1)[c][:, :], ACT.Copy).then_inc(xt_rounded, 1)
                    if what != "m":
                        return
                    act.wait_ge(prods, g * M + n + 1)
                    f = n // 2
                    if n % 2 == 0:
                        act.activation(hid[:, f, bass.ds(g * GT, GT)], mm[n % 6][:, :], ACT.Copy).then_inc(stored, 1)
                    else:
                        if not (isinstance(g, int) and g == 0 and f < NU):
                            act.wait_ge(u_sent[f % NU], g * 32 + (f // NU) * 16)
                        act.activation(ubuf[:, f % NU, :], mm[n % 6][:, :], ACT.Copy).then_inc(stored, 1)

                slots(act, step)

            @block.sync
            def _(sp):
                with sp.Fori(0, G) as g:
                    for f in range(FT):
                        sp.wait_ge(stored, g * M + 2 * f + 2)
                        sp.dma_start(env["u_dram"][:, f, bass.ds(g * GT, GT)],
                                     ubuf[:, f % NU, :]).then_inc(u_sent[f % NU], 16)
                for k in range(NU):
                    sp.wait_ge(u_sent[k], G * 32)

            @block.gpsimd
            def _(pool):
                pool.dma_start(top_coef[:], bf["top_coef"]).then_inc(coef_in, 16)
                pool.dma_start(low_coef[:], bf["low_coef"]).then_inc(coef_in, 16)
                pool.wait_ge(coef_in, 32)
                for half in range(2):
                    cols = slice(half * HW, (half + 1) * HW)
                    if half:
                        pool.wait_ge(z_sent, 16)
                    pool.dma_start(z[:], bf["w_con"][:, cols].rearrange("(t p) d -> p t d", p=P)).then_inc(z_in, 16)
                    pool.wait_ge(z_in, 16 * (half + 1))
                    for i in range(TOP):
                        top_stage(pool, z[:], z_own[:], z_pair[:], 1, i, z_mul, z_add, half * TOP + i)
                    pool.dma_start(bf["w2_dram"][:, :, cols], z[:]).then_inc(z_sent, 16)
                pool.wait_ge(z_sent, 32)

        NCH = 12
        CW = FT * NT * P // NCH
        flat = hid[:].rearrange("p f t -> p (f t)")
        u_flat = env["u_dram"].rearrange("p f t -> p (f t)")
        cmax = amax[:].rearrange("p n g f -> p (n g f)")

        blocks = sb("blocks", [P, 2, HT, P])
        NR = 3
        u_back = [sem(f"u_back{n}") for n in range(NR)]
        first_u = sb("first_u", [P, CW])

        with ExitStack() as ph:
            b_own = ph.enter_context(nc.sbuf_tensor("f0_b_own", [P, 2, HT, P], F32))
            b_cross = ph.enter_context(nc.sbuf_tensor("f0_b_cross", [P, 2, HT, P], F32))
            flip = ph.enter_context(nc.sbuf_tensor("f0_flip", [P, 2, P], F32))
            first_flip = ph.enter_context(nc.sbuf_tensor("f0_first_flip", [P, 2, P], F32))
            flips_in, b_cleared = sem("flips_in"), [sem("b_cleared0"), sem("b_cleared1")]
            flip_in = [sem(f"flip_in{net}") for net in range(2)]
            b_scaled, b_summed, b_ready = ([sem(f"{x}{net}") for net in range(2)] for x in (
                "b_scaled", "b_summed", "b_ready"))
            bank_of = [[X0, X1], [S0, S1]]

            def per_row(net, i, k):
                return low_coef[:, net, bass.ds(i, 1), k, :].rearrange("p o t -> p (o t)").unsqueeze(
                    2).to_broadcast([P, HT, P])

            def first_step(eng, net):
                eng.wait_ge(flips_in, 16)
                eng.tensor_tensor(b_own[:, net], ident[:].unsqueeze(1).to_broadcast([P, HT, P]),
                                  per_row(net, 0, 0), ALU.mult)
                eng.tensor_tensor(b_cross[:, net], first_flip[:, net, :].unsqueeze(1).to_broadcast([P, HT, P]),
                                  per_row(net, 0, 1), ALU.mult).then_inc(b_cleared[net], 1)
                eng.wait_ge(b_cleared[net], 1)
                eng.tensor_tensor(blocks[:, net], b_own[:, net], b_cross[:, net], ALU.add).then_inc(b_ready[net], 1)

            gcode = ph.enter_context(nc.sbuf_tensor("f0_gcode", [P, 2, CW], I16))
            sig = ph.enter_context(nc.sbuf_tensor("f0_sig", [P, 2, CW], F32))
            scode = ph.enter_context(nc.sbuf_tensor("f0_scode", [P, CW], U16))
            t_max, t_all, t_scale, s_ready = sem("t_max"), sem("t_all"), sem("t_scale"), sem("s_ready")
            gcoded, sig_ready, scoded, gated, c_maxed = (sem(x) for x in (
                "gcoded", "sig_ready", "scoded", "gated", "c_maxed"))
            block = ph.enter_context(nc.Block())

            @block.gpsimd
            def _(pool):
                for n in range(2):
                    pool.wait_ge(t_max, n + 1)
                    pool.partition_all_reduce(small[:, 0:1], small[:, 1:2], P, RMAX).then_inc(t_all, 1)

                first_step(pool, 0)
                with pool.Fori(1, LOW) as i:
                    for net in range(2):
                        pool.wait_ge(b_ready[net], i)
                        pool.tensor_tensor(b_own[:, net], blocks[:, net], per_row(net, i, 0), ALU.mult)
                        pool.tensor_tensor(b_cross[:, net], blocks[:, net], per_row(net, i, 1),
                                           ALU.mult).then_inc(b_scaled[net], 1)

            @block.sync
            def _(sp):
                sp.dma_start(first_u[:], u_flat[:, 0:CW]).then_inc(u_back[0], 16)
                sp.dma_start(first_flip[:], bf["flips"][:, :, 0, :]).then_inc(flips_in, 16)
                for net in range(2):
                    sp.dma_start(flip[:, net, :], bf["flips"][:, net, 1, :]).then_inc(flip_in[net], 16)
                with sp.Fori(2, LOW) as i:
                    for net in range(2):
                        sp.wait_ge(b_summed[net], i - 1)
                        sp.dma_start(flip[:, net, :], bf["flips"][:, net, bass.ds(i, 1), :].rearrange(
                            "p o m -> p (o m)")).then_inc(flip_in[net], 16)

            @block.tensor
            def _(pe):
                with pe.Fori(1, LOW) as i:
                    for net in range(2):
                        pe.wait_ge(b_scaled[net], i)
                        pe.wait_ge(flip_in[net], i * 16)
                        for k in range(2):
                            tiles = slice(k * HT // 2, (k + 1) * HT // 2)
                            pe.matmul(bank_of[net][k][:, :], ident[:],
                                      b_own[:, net, tiles, :].rearrange("p t m -> p (t m)"), start=True, stop=False)
                            last = pe.matmul(bank_of[net][k][:, :],
                                             flip[:, net, :],
                                             b_cross[:, net, tiles, :].rearrange("p t m -> p (t m)"),
                                             start=False, stop=True)
                        last.then_inc(b_summed[net], 1)

            @block.vector
            def _(dve):
                for n, k in enumerate((SG, SU)):
                    dve.tensor_copy(unit[:, k:k + 1], scales[:, SX:SX + 1])
                    dve.tensor_reduce(small[:, 1:2], amax[:, n, :, :].rearrange("p g f -> p (g f)"), AX.X,
                                      ALU.max).then_inc(t_max, 1)
                    dve.wait_ge(t_all, n + 1)
                    scale_steps(dve, k, t_scale, 4 * n)
                dve.tensor_scalar(unit[:, S2:S2 + 1], scales[:, SG:SG + 1], 1.0 / 65536, None,
                                  ALU.mult).then_inc(s_ready, 1)
                first_step(dve, 1)
                with dve.Fori(0, NCH // 2) as j:
                    for par in range(2):
                        i = j * 2 + par
                        part = flat[:, bass.ds(i * CW, CW)]
                        dve.wait_ge(sig_ready, i + 1)
                        dve.tensor_scalar(scode[:], sig[:, par, :], 65536.0, None, ALU.mult).then_inc(scoded, 1)
                        dve.wait_ge(scoded, i + 1)
                        dve.tensor_tensor(part, gcode[:, par, :], scode[:], ALU.mult).then_inc(gated, 1)
                        dve.wait_ge(gated, i + 1)
                        dve.tensor_reduce(cmax[:, bass.ds(i, 1)], part, AX.X, ALU.max,
                                          apply_absolute_value=True).then_inc(c_maxed, 1)

            @block.scalar
            def _(act):
                act.wait_ge(s_ready, 1)

                def chunk(i, par, again):
                    if again:
                        act.wait_ge(gated, i - 1)
                    act.activation(gcode[:, par, :], flat[:, bass.ds(i * CW, CW)], ACT.Identity,
                                   scale=codes[:, SG:SG + 1]).then_inc(gcoded, 1)
                    act.wait_ge(gcoded, i + 1)
                    act.activation(sig[:, par, :], gcode[:, par, :], ACT.Sigmoid,
                                   scale=scales[:, SG:SG + 1]).then_inc(sig_ready, 1)

                def composed(i, net):
                    act.wait_ge(b_summed[net], i)
                    for k in range(2):
                        last = act.activation(
                            blocks[:, net, k * HT // 2:(k + 1) * HT // 2, :].rearrange("p t m -> p (t m)"),
                            bank_of[net][k][:, :], ACT.Copy)
                    last.then_inc(b_ready[net], 1)

                chunk(0, 0, False)
                chunk(1, 1, False)
                with act.Fori(1, NCH // 2) as j:
                    composed(j, 0)
                    chunk(j * 2, 0, True)
                    composed(j, 1)
                    chunk(j * 2 + 1, 1, True)
                composed(LOW - 1, 0)
                composed(LOW - 1, 1)

        with ExitStack() as ph:
            ubuf = [first_u] + [ph.enter_context(nc.sbuf_tensor(f"f0_uback{n}", [P, CW], F32)) for n in range(1, NR)]
            ucode = ph.enter_context(nc.sbuf_tensor("f0_ucode", [P, 2, CW], I16))
            gcode = ph.enter_context(nc.sbuf_tensor("f0_g2code", [P, 2, CW], I16))
            d_max, d_all, d_scale = sem("d_max"), sem("d_all"), sem("d_scale")
            ucoded, g2coded, multiplied, d_maxed = (sem(x) for x in ("ucoded", "g2coded", "multiplied", "d_maxed"))
            y = ph.enter_context(nc.sbuf_tensor("f0_y", [P, HT, D + 1], F32))
            z = ph.enter_context(nc.sbuf_tensor("f0_z2", [P, HT * (D + 1)], F32))
            z_tiles = z[:, 0:HT * D].rearrange("p (t d) -> p t d", d=D)
            y_own = z[:].rearrange("p (t d) -> p t d", d=D + 1)
            HWB = D // 2 + 1
            y_pair = blocks[:].rearrange("p n t m -> p (n t m)")[:, 0:HT * HWB].rearrange("p (t d) -> p t d", d=HWB)
            y_in, z_back, y_prod, z_prod, bias_prod, y_out, z_out, bias_out, z_stored, y_mul, y_add, y_stored = (
                sem(x) for x in ("y_in", "z_back", "y_prod", "z_prod", "bias_prod", "y_out", "z_out", "bias_out",
                                 "z_stored", "y_mul", "y_add", "y_stored"))
            y_banks, z_banks = [X0, X1, S0, S1], [O0, O1, T0, T1]
            block = ph.enter_context(nc.Block())

            @block.sync
            def _(sp):
                def load(j, k):
                    sp.dma_start(ubuf[k][:], u_flat[:, bass.ds((j * NR + k) * CW, CW)]).then_inc(u_back[k], 16)

                load(0, 1)
                sp.dma_start(z_tiles, bf["w2_dram"]).then_inc(z_back, 16)
                sp.dma_start(y[:], bf["w_exp_t"].rearrange("(t p) d -> p t d", p=P)).then_inc(y_in, 16)
                load(0, 2)
                sp.wait_ge(z_out, 1)
                sp.dma_start(bf["w2_dram"], z_tiles).then_inc(z_stored, 16)
                with sp.Fori(1, NCH // NR) as j:
                    for k in range(NR):
                        sp.wait_ge(ucoded, (j - 1) * NR + k + 1)
                        load(j, k)
                sp.wait_ge(y_add, 2 * TOP)
                sp.dma_start(bf["w1_dram"], y[:]).then_inc(y_stored, 16)
                sp.wait_ge(y_stored, 16)
                sp.wait_ge(z_stored, 16)

            @block.tensor
            def _(pe):
                pe.wait_ge(z_back, 16)
                for t in range(HT):
                    last = pe.matmul(z_banks[t // 2][:, (t % 2) * D:(t % 2 + 1) * D], blocks[:, 1, t, :],
                                     z_tiles[:, t, :], start=True, stop=True)
                last.then_inc(z_prod, 1)
                pe.wait_ge(y_in, 16)
                for t in range(HT):
                    last = pe.matmul(y_banks[t // 2][:, (t % 2) * D:(t % 2 + 1) * D], blocks[:, 0, t, :],
                                     y[:, t, 0:D], start=True, stop=True)
                last.then_inc(y_prod, 1)
                pe.wait_ge(z_out, 1)
                for t in range(HT):
                    last = pe.matmul(T0[:, t:t + 1], blocks[:, 0, t, :], y[:, t, D:D + 1], start=True, stop=True)
                last.then_inc(bias_prod, 1)

            @block.scalar
            def _(act):
                def chunk(j, k, n):
                    i = j * 6 + n
                    act.wait_ge(u_back[k], (j * 2 + n // NR + 1) * 16)
                    if not (isinstance(j, int) and j == 0 and n < 2):
                        act.wait_ge(multiplied, i - 1)
                    act.activation(ucode[:, n % 2, :], ubuf[k][:], ACT.Identity,
                                   scale=codes[:, SU:SU + 1]).then_inc(ucoded, 1)
                    act.activation(gcode[:, n % 2, :], flat[:, bass.ds(i * CW, CW)], ACT.Identity,
                                   scale=codes[:, S2:S2 + 1]).then_inc(g2coded, 1)

                def tiles_out(banks_, dst, done):
                    for k, bank in enumerate(banks_):
                        last = act.activation(dst[:, 2 * k:2 * k + 2, :],
                                              bank[:, :].rearrange("p (t d) -> p t d", d=D), ACT.Copy)
                    last.then_inc(done, 1)

                act.wait_ge(d_scale, 5)
                chunk(0, 0, 0)
                chunk(0, 1, 1)
                act.wait_ge(z_prod, 1)
                tiles_out(z_banks, z_tiles, z_out)
                chunk(0, 2, 2)
                act.wait_ge(y_prod, 1)
                tiles_out(y_banks, y[:, :, 0:D], y_out)
                act.wait_ge(bias_prod, 1)
                act.activation(y[:, :, D], T0[:, 0:HT], ACT.Copy).then_inc(bias_out, 1)
                for n in range(3, 6):
                    chunk(0, n % NR, n)
                with act.Fori(1, NCH // 6) as j:
                    for n in range(6):
                        chunk(j, n % NR, n)

            @block.gpsimd
            def _(pool):
                pool.wait_ge(d_max, 1)
                pool.partition_all_reduce(small[:, 0:1], small[:, 1:2], P, RMAX).then_inc(d_all, 1)
                pool.wait_ge(bias_out, 1)
                pool.wait_ge(z_stored, 16)
                for n, (c0, c1) in enumerate(((0, D // 2), (D // 2, D + 1))):
                    for i in range(TOP):
                        top_stage(pool, y[:, :, c0:c1], y_own[:, :, c0:c1], y_pair[:, :, 0:c1 - c0], 0, i,
                                  y_mul, y_add, n * TOP + i)

            @block.vector
            def _(dve):
                dve.tensor_reduce(small[:, 1:2], cmax[:, 0:NCH], AX.X, ALU.max).then_inc(d_max, 1)
                dve.wait_ge(d_all, 1)
                scale_steps(dve, S2, d_scale, 0)
                dve.tensor_tensor(unit[:, SO:SO + 1], scales[:, S2:S2 + 1], scales[:, SU:SU + 1],
                                  ALU.mult).then_inc(d_scale, 1)
                with dve.Fori(0, NCH // 2) as j:
                    for par in range(2):
                        i = j * 2 + par
                        part = flat[:, bass.ds(i * CW, CW)]
                        dve.wait_ge(g2coded, i + 1)
                        dve.tensor_tensor(part, gcode[:, par, :], ucode[:, par, :], ALU.mult).then_inc(multiplied, 1)
                        dve.wait_ge(multiplied, i + 1)
                        dve.tensor_reduce(cmax[:, bass.ds(i, 1)], part, AX.X, ALU.max,
                                          apply_absolute_value=True).then_inc(d_maxed, 1)

        with ExitStack() as ph:
            ocode = ph.enter_context(nc.sbuf_tensor("f0_ocode", [P, 2, FT, T], I16))
            o_hi = ph.enter_context(nc.sbuf_tensor("f0_o_hi", [P, 2, FT, T], F32R))
            o_lo = ph.enter_context(nc.sbuf_tensor("f0_o_lo", [P, 2, FT, T], F32R))
            back = ph.enter_context(nc.sbuf_tensor("f0_back", [P, 1], F32))
            e_max, e_all, e_scale = sem("e_max"), sem("e_all"), sem("e_scale")
            ocoded, o_rounded, o_split, down, e_added = (sem(x) for x in (
                "ocoded", "o_rounded", "o_split", "down", "e_added"))
            block = ph.enter_context(nc.Block())
            ybank = [X0, X1, S0, S1]

            @block.gpsimd
            def _(pool):
                pool.wait_ge(e_max, 1)
                pool.partition_all_reduce(small[:, 0:1], small[:, 1:2], P, RMAX).then_inc(e_all, 1)

            @block.vector
            def _(dve):
                dve.tensor_reduce(small[:, 1:2], cmax[:, 0:NCH], AX.X, ALU.max).then_inc(e_max, 1)
                dve.wait_ge(e_all, 1)
                scale_steps(dve, SO, e_scale, 0)
                dve.tensor_tensor(back[:], scales[:, SO:SO + 1], tg[:, 0:1], ALU.mult).then_inc(e_scale, 1)
                dve.wait_ge(e_scale, 5)

                def code(b, par, again):
                    if again:
                        dve.wait_ge(o_split, b - 1)
                    dve.tensor_scalar(ocode[:, par, :, :], hid[:, :, bass.ds(b * T, T)], codes[:, SO:SO + 1], None,
                                      ALU.mult).then_inc(ocoded, 1)

                def split(b, par):
                    dve.wait_ge(o_rounded, b + 1)
                    dve.tensor_tensor(o_lo[:, par, :, :], ocode[:, par, :, :], o_hi[:, par, :, :].bitcast(F32),
                                      ALU.subtract).then_inc(o_split, 1)

                def add(b, par):
                    dve.wait_ge(down, b + 1)
                    for t in range(TT):
                        x = xres[:, bass.ds(b * TT + t, 1), :].rearrange("p o d -> p (o d)")
                        last = dve.scalar_tensor_tensor(out=x, in0=ybank[2 * par + t][:, 0:D], scalar=back[:, 0:1],
                                                        in1=x, op0=ALU.mult, op1=ALU.add)
                    last.then_inc(e_added, 1)

                code(0, 0, False)
                code(1, 1, False)
                split(0, 0)
                code(2, 0, True)
                split(1, 1)
                code(3, 1, True)
                with dve.Fori(0, B // 2 - 2) as j:
                    add(j * 2, 0)
                    split(j * 2 + 2, 0)
                    code(j * 2 + 4, 0, True)
                    add(j * 2 + 1, 1)
                    split(j * 2 + 3, 1)
                    code(j * 2 + 5, 1, True)
                for b in range(B - 4, B):
                    add(b, b % 2)
                    if b < B - 2:
                        split(b + 2, b % 2)

            @block.scalar
            def _(act):
                def hi(b, par, again):
                    act.wait_ge(ocoded, b + 1)
                    if again:
                        act.wait_ge(down, b - 1)
                    act.activation(o_hi[:, par, :, :], ocode[:, par, :, :], ACT.Copy).then_inc(o_rounded, 1)

                hi(0, 0, False)
                hi(1, 1, False)
                with act.Fori(1, B // 2) as j:
                    hi(j * 2, 0, True)
                    hi(j * 2 + 1, 1, True)

            @block.tensor
            def _(pe):
                def prod(b, par, again):
                    pe.wait_ge(o_split, b + 1)
                    if again:
                        pe.wait_ge(e_added, b - 1)
                    for t in range(TT):
                        for f in range(FT):
                            last = three_passes(nc, ybank[2 * par + t][:, 0:D],
                                                o_hi[:, par, f, t * P:(t + 1) * P],
                                                o_lo[:, par, f, t * P:(t + 1) * P],
                                                d_hi[:, f, :], d_lo[:, f, :], f == 0, f == FT - 1)
                    last.then_inc(down, 1)

                prod(0, 0, False)
                prod(1, 1, False)
                with pe.Fori(1, B // 2) as j:
                    prod(j * 2, 0, True)
                    prod(j * 2 + 1, 1, True)

    free_semaphores(nc, sems)


def butterfly_ffn(nc, env, w1_dram, w2_dram, up_bias, out_bias, gate, out):
    xres, banks, ident = env["xres"], env["banks"], env["ident"]
    T0, T1, X0, X1, S0, S1, O0, O1 = banks
    HT = HID1 // P
    G = NT * P // GT
    GTT = GT // P
    sems = []
    ctx = ExitStack()
    with ctx:
        def sb(name, shape, dt=F32):
            return ctx.enter_context(nc.sbuf_tensor(f"f1_{name}", shape, dt))

        def sem(name):
            sems.append(nc.alloc_semaphore(f"f1_{name}"))
            return sems[-1]

        w1_hi = sb("w1_hi", [P, DC, HID1], F32R)
        w1_lo = sb("w1_lo", [P, DC, HID1], F32R)
        w2_hi = sb("w2_hi", [P, HT, D], F32R)
        w2_lo = sb("w2_lo", [P, HT, D], F32R)
        b1 = sb("b1", [P, HT])
        gb = sb("gb", [P, D])
        tg = sb("tg", [P, 1])
        minus_half = sb("minus_half", [P, GTT])
        eps = sb("eps", [P, GTT])

        with ExitStack() as setup:
            def tmp(name, shape, dt=F32):
                return setup.enter_context(nc.sbuf_tensor(f"f1_{name}", shape, dt))

            u = tmp("u", [P, HT, D + 1])
            v = tmp("v", [P, HT, D])
            ub = tmp("ub", [P, HT])
            ob = tmp("ob", [P, 2, D])
            u_in, v_in, small_in, turned, w1_rounded, w1_split, v_rounded, g_done, ob_sum = (sem(x) for x in (
                "u_in", "v_in", "small_in", "turned", "w1_rounded", "w1_split", "v_rounded", "g_done", "ob_sum"))
            TURNS = [(c, t0) for c in range(DC) for t0 in range(0, HT, 4)]
            block = setup.enter_context(nc.Block())

            @block.sync
            def _(sp):
                sp.dma_start(u[:], w1_dram).then_inc(u_in, 16)
                sp.dma_start(v[:], w2_dram).then_inc(v_in, 16)
                sp.dma_start(ub[:], up_bias).then_inc(small_in, 16)
                sp.dma_start(ob[:], out_bias).then_inc(small_in, 16)
                sp.dma_start(tg[:], gate).then_inc(small_in, 16)

            @block.gpsimd
            def _(pool):
                pool.memset(minus_half[:], -0.5)
                pool.memset(eps[:], LN_EPS)

            @block.tensor
            def _(pe):
                pe.wait_ge(u_in, 16)
                for n, (c, t0) in enumerate(TURNS):
                    for k in range(4):
                        last = pe.transpose(banks[n][:, k * P:(k + 1) * P], u[:, t0 + k, c * P:(c + 1) * P], ident[:])
                    last.then_inc(turned, 1)

            @block.scalar
            def _(act):
                for n, (c, t0) in enumerate(TURNS):
                    act.wait_ge(turned, n + 1)
                    act.activation(w1_hi[:, c, t0 * P:(t0 + 4) * P], banks[n][:, :], ACT.Copy).then_inc(w1_rounded, 1)
                act.wait_ge(v_in, 16)
                act.activation(w2_hi[:], v[:], ACT.Copy).then_inc(v_rounded, 1)
                act.wait_ge(small_in, 48)
                act.activation(tg[:], tg[:], ACT.Tanh).then_inc(g_done, 1)

            @block.vector
            def _(dve):
                for n, (c, t0) in enumerate(TURNS):
                    dve.wait_ge(w1_rounded, n + 1)
                    cols = slice(t0 * P, (t0 + 4) * P)
                    dve.tensor_tensor(w1_lo[:, c, cols], banks[n][:, :], w1_hi[:, c, cols].bitcast(F32), ALU.subtract)
                dve.wait_ge(v_rounded, 1)
                dve.tensor_tensor(w2_lo[:], v[:], w2_hi[:].bitcast(F32), ALU.subtract)
                dve.wait_ge(small_in, 48)
                dve.tensor_tensor(b1[:], u[:, :, D], ub[:], ALU.add)
                dve.tensor_tensor(gb[:], ob[:, 0, :], ob[:, 1, :], ALU.add).then_inc(ob_sum, 1)
                dve.wait_ge(g_done, 1)
                dve.wait_ge(ob_sum, 1)
                dve.tensor_scalar(gb[:], gb[:], tg[:, 0:1], None, ALU.mult)

        mv = sb("mv", [P, GTT, 2])
        bn = sb("bn", [P, GTT, 6])
        var = sb("var", [P, GTT])
        rstd = sb("rstd", [P, GTT])
        xn = sb("xn", [P, GTT, D])
        xt_hi = sb("xt_hi", [P, 2, DC, GT], F32R)
        xt_lo = sb("xt_lo", [P, 2, DC, GT], F32R)
        h = sb("h", [P, 2, GT])
        h_hi = sb("h_hi", [P, 2, HT, GT], F32R)
        h_lo = sb("h_lo", [P, 2, HT, GT], F32R)
        ln_bn, ln_stats, ln_eps, ln_rstd, ln_xn, biased = (sem(x) for x in (
            "ln_bn", "ln_stats", "ln_eps", "ln_rstd", "ln_xn", "biased"))
        xt_ready, xt_rounded, xt_split = sem("xt_ready"), sem("xt_rounded"), sem("xt_split")
        h_sum, h_ready, h_rounded, h_split = sem("h_sum"), sem("h_ready"), sem("h_rounded"), sem("h_split")
        passed = sem("passed")
        y_sum, y_added, y_sent = sem("y_sum"), sem("y_added"), sem("y_sent")
        hbank = [X0, X1, S0, S1]
        ybank = [O0, O1]

        def slots(eng, step):
            def slot(g, par, front=True, middle=True, back=True):
                for m in range(HT):
                    if front and m == 1:
                        step("ln", 0, g + 2, par)
                    if front and m == 6:
                        step("x", 0, g + 2, par)
                    if middle:
                        step("h", m, g + 1, 1 - par)
                for t in range(GTT):
                    if back:
                        step("y", t, g, par)

            slot(-2, 0, middle=False, back=False)
            slot(-1, 1, back=False)
            slot(0, 0)
            slot(1, 1)
            with eng.Fori(1, (G - 2) // 2) as j:
                slot(j * 2, 0)
                slot(j * 2 + 1, 1)
            slot(G - 2, 0, front=False)
            slot(G - 1, 1, front=False, middle=False)

        block = ctx.enter_context(nc.Block())

        @block.vector
        def _(dve):
            def xtile(g, t):
                return xres[:, bass.ds(g * GTT + t, 1), :].rearrange("p o d -> p (o d)")

            def step(what, n, g, par):
                if what == "ln":
                    for t in range(GTT):
                        last = dve.bn_stats(bn[:, t, :], xtile(g, t))
                    last.then_inc(ln_bn, 1)
                    dve.wait_ge(ln_bn, g + 1)
                    dve.sem_inc(passed, 1)
                    for t in range(GTT):
                        last = dve.bn_aggr(mv[:, t, :], bn[:, t, :])
                    last.then_inc(ln_stats, 1)
                    dve.wait_ge(ln_rstd, g + 1)
                    for t in range(GTT):
                        last = dve.tensor_scalar(xn[:, t, :], xtile(g, t), mv[:, t, 0:1], rstd[:, t:t + 1],
                                                 ALU.subtract, ALU.mult)
                    last.then_inc(ln_xn, 1)
                elif what == "x":
                    for c in range(DC):
                        dve.wait_ge(xt_rounded, g * DC + c + 1)
                        dve.tensor_tensor(xt_lo[:, par, c, :], (T0, T1)[c][:, :],
                                          xt_hi[:, par, c, :].bitcast(F32), ALU.subtract).then_inc(xt_split, 1)
                elif what == "h":
                    dve.wait_ge(h_ready, g * HT + n + 1)
                    dve.tensor_copy(h_hi[:, par, n, :], h[:, n % 2, :]).then_inc(h_rounded, 1)
                    dve.wait_ge(h_rounded, g * HT + n + 1)
                    dve.tensor_tensor(h_lo[:, par, n, :], h[:, n % 2, :], h_hi[:, par, n, :].bitcast(F32),
                                      ALU.subtract).then_inc(h_split, 1)
                elif what == "y":
                    dve.wait_ge(y_sum, g * GTT + n + 1)
                    dve.wait_ge(biased, g + 1)
                    x = xtile(g, n)
                    dve.scalar_tensor_tensor(out=x, in0=ybank[n % 2][:, 0:D], scalar=tg[:, 0:1], in1=x,
                                             op0=ALU.mult, op1=ALU.add).then_inc(y_added, 1)

            slots(dve, step)

        @block.gpsimd
        def _(pool):
            with pool.Fori(0, G) as g:
                pool.wait_ge(ln_stats, g + 1)
                pool.tensor_tensor(var[:], mv[:, :, 1], eps[:], ALU.add).then_inc(ln_eps, 1)
                pool.wait_ge(ln_eps, g + 1)
                pool.tensor_tensor(rstd[:], var[:], minus_half[:], ALU.pow).then_inc(ln_rstd, 1)
                pool.wait_ge(ln_xn, g + 1)
                for t in range(GTT):
                    x = xres[:, bass.ds(g * GTT + t, 1), :].rearrange("p o d -> p (o d)")
                    last = pool.tensor_tensor(x, x, gb[:], ALU.add)
                last.then_inc(biased, 1)

        @block.scalar
        def _(act):
            def step(what, n, g, par):
                if what == "x":
                    for c in range(DC):
                        act.wait_ge(xt_ready, g * DC + c + 1)
                        act.activation(xt_hi[:, par, c, :], (T0, T1)[c][:, :], ACT.Copy).then_inc(xt_rounded, 1)
                elif what == "h":
                    act.wait_ge(h_sum, g * HT + n + 1)
                    if not (isinstance(g, int) and g == 0 and n < 2):
                        act.wait_ge(h_split, g * HT + n - 1)
                    act.activation(h[:, n % 2, :], hbank[n % 4][:, :], ACT.Gelu,
                                   bias=b1[:, n:n + 1]).then_inc(h_ready, 1)

            slots(act, step)

        @block.tensor
        def _(pe):
            def step(what, n, g, par):
                if what == "x":
                    pe.wait_ge(ln_xn, g + 1)
                    pe.wait_ge(xt_split, g * DC)
                    for c in range(DC):
                        for t in range(GTT):
                            last = pe.transpose((T0, T1)[c][:, t * P:(t + 1) * P], xn[:, t, c * P:(c + 1) * P],
                                                ident[:])
                        last.then_inc(xt_ready, 1)
                elif what == "h":
                    if n == 0:
                        pe.wait_ge(xt_split, (g + 1) * DC)
                    if not (isinstance(g, int) and g == 0 and n < 4):
                        pe.wait_ge(h_ready, g * HT + n - 3)
                    for c in range(DC):
                        last = three_passes(nc, hbank[n % 4][:, :], w1_hi[:, c, n * P:(n + 1) * P],
                                            w1_lo[:, c, n * P:(n + 1) * P], xt_hi[:, par, c, :],
                                            xt_lo[:, par, c, :], c == 0, c == DC - 1)
                    last.then_inc(h_sum, 1)
                elif what == "y":
                    if n == 0:
                        pe.wait_ge(h_split, (g + 1) * HT)
                    if not (isinstance(g, int) and g == 0 and n < 2):
                        pe.wait_ge(y_added, g * GTT + n - 1)
                    for m in range(HT):
                        last = three_passes(nc, ybank[n % 2][:, 0:D], h_hi[:, par, m, n * P:(n + 1) * P],
                                            h_lo[:, par, m, n * P:(n + 1) * P], w2_hi[:, m, :], w2_lo[:, m, :],
                                            m == 0, m == HT - 1)
                    last.then_inc(y_sum, 1)

            slots(pe, step)

        @block.sync
        def _(sp):
            with sp.Fori(0, G) as g:
                sp.wait_ge(y_added, (g + 1) * GTT)
                sp.dma_start(out[bass.ds(g * GT, GT), :].rearrange("(t p) d -> p t d", p=P),
                             xres[:, bass.ds(g * GTT, GTT), :]).then_inc(y_sent, 16)
            sp.wait_ge(y_sent, G * 16)


def build(nc, a, out):
    with ExitStack() as ctx:
        env = {"banks": [ctx.enter_context(nc.psum_tensor(f"bank{n}", [P, 512], F32)) for n in range(8)],
               "u_dram": nc.dram_tensor("u_spill", (P, HID0 // P, NT * P), F32, kind="Internal").ap()}
        butterfly = {name: a[name] for name in ("top_coef", "low_coef", "flips", "w_con", "w_exp_t")}
        butterfly["w1_dram"] = nc.dram_tensor("w1_spill", (P, HID1 // P, D + 1), F32, kind="Internal").ap()
        butterfly["w2_dram"] = nc.dram_tensor("w2_spill", (P, HID1 // P, D), F32, kind="Internal").ap()
        for name, shape in (("xres", [P, NT, D]), ("ident", [P, P]), ("mean_all", [P, NT]),
                            ("rstd_all", [P, NT]), ("amax_x", [P, B])):
            env[name] = ctx.enter_context(nc.sbuf_tensor(name, shape, F32))
        for layer in range(2):
            env[f"mask{layer}"], env[f"pick{layer}"] = a[f"mask{layer}"], a[f"pick{layer}"]
        ident_in = ctx.enter_context(nc.semaphore("ident_in"))
        with nc.Block() as block:
            @block.sync
            def _(sp):
                sp.dma_start(env["ident"][:], a["ident"]).then_inc(ident_in, 16)
                sp.wait_ge(ident_in, 16)

        attention(nc, env, 0, 16, 256, a["wqkv0"], a["wo0"], a["bq0"], a["bk0"], a["bv0"], a["bo0"],
                  a["gx0"], a["ctx_t"], a["x"])
        quantised_ffn(nc, env, a["w_up"], a["w_gate"], a["w_down"], a["gf0"], butterfly)
        attention(nc, env, 1, 8, 512, a["wqkv1"], a["wo1"], None, None, None, a["bo1"], a["gx1"],
                  a["ctx_t"], None)
        butterfly_ffn(nc, env, butterfly["w1_dram"], butterfly["w2_dram"], a["up_bias"], a["out_bias"],
                      a["gf1"], out)


def kernel(**inputs):
    import numpy as np
    import concourse.bacc as bacc
    from concourse.bass_utils import run_bass_kernel_spmd

    v = {k: np.asarray(x) for k, x in inputs.items()}

    def rows(vec):
        return np.ascontiguousarray(np.broadcast_to(vec.reshape(1, -1), (P, vec.size)))

    def columns(vec):
        return np.ascontiguousarray(vec.reshape(-1, P).T)

    def stage_coefs(w, transposed):
        n = np.arange(HID1)
        got = []
        for stage in range(w.shape[0]):
            s = 1 << stage
            pair, hi = (n // (2 * s)) * s + n % s, (n // s) % 2
            other = w[stage, pair, 1 - hi, hi] if transposed else w[stage, pair, hi, 1 - hi]
            got.append(np.stack([w[stage, pair, hi, hi], other]))
        return np.stack(got)

    LOW = P.bit_length() - 1
    up, up_t = (stage_coefs(v["L1_ffn_up_weights"], k) for k in (False, True))
    down, down_t = (stage_coefs(v["L1_ffn_down_weights"], k) for k in (False, True))
    low = np.stack([np.concatenate([up_t[LOW - 1:LOW], up[LOW - 2::-1]]),
                    np.concatenate([down[0:1], down_t[1:LOW]])])
    top = np.stack([up[LOW:], down_t[:LOW - 1:-1]])
    lows = np.stack([np.arange(LOW)[::-1], np.arange(LOW)])

    def per_tile(c):
        return np.ascontiguousarray(np.moveaxis(c.reshape(c.shape[:3] + (-1, P)), -1, 0))

    m = np.arange(P)
    flips = np.ascontiguousarray((m[:, None, None, None] == (m[None, None, None, :] ^ (1 << lows)[None, :, :, None])
                                  ).astype(np.float32))

    def mask(d):
        return np.ascontiguousarray((np.arange(P)[:, None] // d == np.arange(P // d)[None, :]).astype(np.float32))

    def pick(heads):
        m = np.zeros((P, heads, S + 1), np.float32)
        for h in range(heads):
            m[h, h, :] = -1.0
        return m

    t = np.transpose
    arrays = {
        "x": v["x"].reshape(NT * P, D),
        "ctx_t": np.ascontiguousarray(v["ctx_1024"].reshape(B * S, D).T),
        "ident": np.eye(P, dtype=np.float32),
        "mask0": mask(16), "mask1": mask(64), "pick0": pick(16), "pick1": pick(8),
        "wqkv0": np.ascontiguousarray(np.concatenate([t(v["L0_xattn_Wq"]), t(v["L0_xattn_Wk"]), t(v["L0_xattn_Wv"])], 1)),
        "wo0": np.ascontiguousarray(t(v["L0_xattn_Wo"])),
        "bq0": columns(v["L0_xattn_bq"]), "bk0": columns(v["L0_xattn_bk"]),
        "bv0": rows(v["L0_xattn_bv"]), "bo0": rows(v["L0_xattn_bo"]),
        "wqkv1": np.ascontiguousarray(np.concatenate([v["L1_xattn_Wq"], v["L1_xattn_Wk"], v["L1_xattn_Wv"]], 1)),
        "wo1": v["L1_xattn_Wo"], "bo1": rows(v["L1_xattn_bo"]),
        "gx0": rows(v["g_xattn"][0:1]), "gx1": rows(v["g_xattn"][1:2]),
        "gf0": rows(v["g_ffn"][0:1]), "gf1": rows(v["g_ffn"][1:2]),
        "w_up": v["L0_ffn_w_up"], "w_gate": v["L0_ffn_w_gate"], "w_down": v["L0_ffn_w_down"],
        "w_exp_t": np.ascontiguousarray(np.concatenate([t(v["L1_ffn_W_exp"]), v["L1_ffn_b_exp"][:, None]], 1)),
        "w_con": v["L1_ffn_W_con"], "up_bias": columns(v["L1_ffn_up_bias"]),
        "top_coef": per_tile(top), "low_coef": per_tile(low), "flips": flips,
        "out_bias": np.ascontiguousarray(np.stack([rows(v["L1_ffn_b_con"]), rows(v["L1_ffn_down_bias"])], 1)),
    }
    nc = bacc.Bacc("TRN2", target_bir_lowering=False, num_devices=1)
    feed, args = {}, {}
    for name, x in arrays.items():
        feed[f"in_{name}"] = np.ascontiguousarray(x)
        args[name] = nc.dram_tensor(f"in_{name}", x.shape, mybir.dt.from_np(x.dtype), kind="ExternalInput").ap()
    out = nc.dram_tensor("out_x", (NT * P, D), F32, kind="ExternalOutput").ap()
    build(nc, args, out)
    r = run_bass_kernel_spmd(nc, [feed], core_ids=[0])
    return r.results[0]["out_x"].reshape(B, T, D)
```

```python
from contextlib import ExitStack

import concourse.bass as bass
from concourse import mybir

F32 = mybir.dt.float32
F32R = mybir.dt.float32r
I16 = mybir.dt.int16
U16 = mybir.dt.uint16
ALU = mybir.AluOpType
ACT = mybir.ActivationFunctionType
AX = mybir.AxisListType
RMAX = bass.bass_isa.ReduceOp.max

P = 128
D = 256
DC = D // P
B = 16
T = 256
TT = T // P
S = 77
NT = B * TT
LN_EPS = 1e-5
BLOCK = 32
ACT_MAX = 32767.0
TINY = 1e-12
GT = 512
HID0 = 768
HID1 = 1024


def three_passes(nc, out, w_hi, w_lo, m_hi, m_lo, start, stop):
    nc.tensor.matmul(out, w_hi, m_hi, start=start, stop=False)
    nc.tensor.matmul(out, w_hi, m_lo, start=False, stop=False)
    return nc.tensor.matmul(out, w_lo, m_hi, start=False, stop=stop)


def free_semaphores(nc, sems):
    nc.clear_and_free_semaphores(sems)
    nc.all_engine_barrier()


def quantise_weights(dve, w, code, scale, i, k, step, done):
    n = code.shape[1]
    flat = w[:, bass.ds(i * n, n)].rearrange("p (n k) -> p n k", k=BLOCK)
    cv = code[:].rearrange("p (n k) -> p n k", k=BLOCK)

    def per_block(j):
        return scale[:, j, :].unsqueeze(2).to_broadcast([P, n // BLOCK, BLOCK])

    if k > 0:
        dve.wait_ge(step, 5 * i + k)
    if k == 0:
        dve.tensor_reduce(scale[:, 0, :], flat, AX.X, ALU.max, apply_absolute_value=True).then_inc(step, 1)
    elif k == 1:
        dve.tensor_scalar(scale[:, 1, :], scale[:, 0, :], 1.0 / 7.0, TINY, ALU.mult, ALU.max).then_inc(step, 1)
    elif k == 2:
        dve.reciprocal(scale[:, 2, :], scale[:, 1, :]).then_inc(step, 1)
    elif k == 3:
        dve.tensor_tensor(cv, flat, per_block(2), ALU.mult).then_inc(step, 1)
    elif k == 4:
        dve.tensor_scalar(code[:], code[:], -8.0, 7.0, ALU.max, ALU.min).then_inc(step, 1)
    else:
        dve.tensor_tensor(flat, cv, per_block(1), ALU.mult).then_inc(done, 1)


def attention(nc, env, layer, heads, inner, wqkv, wo, bq, bk, bv, gbias, gate, ctx_t, x_in):
    d = inner // heads
    C = inner // P
    HPC = P // d
    HP = heads // 2
    NP = C // 2
    NG = TT * heads // 4
    DV = d + 1
    SCALE = float(d) ** -0.5
    first = x_in is not None
    xres, banks, ident = env["xres"], env["banks"], env["ident"]
    T0, T1, X0, X1, S0, S1, O0, O1 = banks
    wide = heads * DV > 512
    mx_banks = [X0] if wide else [X0, X1]
    NMX = len(mx_banks)

    def out_of(t, h):
        if wide and h == heads - 1:
            return X1[:, t * DV:(t + 1) * DV]
        return (O0, O1)[t][:, h * DV:(h + 1) * DV]

    sems = []
    ctx = ExitStack()
    with ctx:
        def sb(name, shape, dt=F32):
            return ctx.enter_context(nc.sbuf_tensor(f"a{layer}_{name}", shape, dt))

        def sem(name):
            sems.append(nc.alloc_semaphore(f"a{layer}_{name}"))
            return sems[-1]

        w_hi = sb("w_hi", [P, DC, 3 * inner], F32R)
        w_lo = sb("w_lo", [P, DC, 3 * inner], F32R)
        wo_hi = sb("wo_hi", [P, C, D], F32R)
        wo_lo = sb("wo_lo", [P, C, D], F32R)
        k_hi = sb("k_hi", [P, C, B * S], F32R)
        k_lo = sb("k_lo", [P, C, B * S], F32R)
        values = sb("values", [P, B, heads, DV])
        bqk = sb("bqk", [P, 2, C])
        bv_all = sb("bv_all", [P, inner])
        gb = sb("gb", [P, D])
        tg = sb("tg", [P, 1])
        warm = sb("warm", [P, 1])
        minus_half = sb("minus_half", [P, TT])
        eps = sb("eps", [P, TT])
        head_mask = sb("head_mask", [P, HPC])
        pick = sb("pick", [P, heads, S + 1], F32R)

        x_loaded = [sem("x_loaded0"), sem("x_loaded1")]

        def load(sp, b, par):
            sp.dma_start(xres[:, bass.ds(b * TT, TT), :],
                         x_in[bass.ds(b * T, T), :].rearrange("(t p) d -> p t d", p=P)).then_inc(x_loaded[par], 16)

        mv = sb("mv", [P, TT, 2])
        bn = sb("bn", [P, TT, 6])
        var = sb("var", [P, TT])
        rstd = sb("rstd", [P, TT])
        xn = sb("xn", [P, TT, D])
        passed = sem("passed")
        ln_cleared, ln_bn, ln_stats, ln_eps, ln_rstd, ln_xn, biased = (sem(x) for x in (
            "ln_cleared", "ln_bn", "ln_stats", "ln_eps", "ln_rstd", "ln_xn", "biased"))

        def xtile(b, t):
            return xres[:, bass.ds(b * TT + t, 1), :].rearrange("p o d -> p (o d)")

        def ln_moments(dve, b, par):
            if first:
                if isinstance(b, int):
                    dve.wait_ge(x_loaded[par], 16 * (b // 2 + 1))
                else:
                    dve.wait_ge(x_loaded[par], (b - par) * 8 + 16)
                    dve.sem_inc(passed, 1)
            for t in range(TT):
                last = dve.bn_stats(bn[:, t, :], xtile(b, t))
            last.then_inc(ln_bn, 1)
            dve.wait_ge(ln_bn, b + 1)
            dve.sem_inc(passed, 1)
            for t in range(TT):
                last = dve.bn_aggr(mv[:, t, :], bn[:, t, :])
            last.then_inc(ln_stats, 1)

        def ln_inverse(pool, b):
            pool.wait_ge(ln_stats, b + 1)
            pool.tensor_tensor(var[:], mv[:, :, 1], eps[:], ALU.add).then_inc(ln_eps, 1)
            pool.wait_ge(ln_eps, b + 1)
            pool.tensor_tensor(rstd[:], var[:], minus_half[:], ALU.pow).then_inc(ln_rstd, 1)

        def ln_normalise(dve, b):
            dve.wait_ge(ln_rstd, b + 1)
            for t in range(TT):
                last = dve.tensor_scalar(xn[:, t, :], xtile(b, t), mv[:, t, 0:1], rstd[:, t:t + 1],
                                         ALU.subtract, ALU.mult)
            last.then_inc(ln_xn, 1)

        def add_bias(pool, b):
            pool.wait_ge(ln_xn, b + 1)
            for t in range(TT):
                last = pool.tensor_tensor(xtile(b, t), xtile(b, t), gb[:], ALU.add)
            last.then_inc(biased, 1)

        setup = ExitStack()
        with setup:
            def tmp(name, shape, dt=F32):
                return setup.enter_context(nc.sbuf_tensor(f"a{layer}_{name}", shape, dt))

            w_raw = tmp("w_raw", [P, DC, 3 * inner])
            wo_raw = tmp("wo_raw", [P, C, D])
            c_raw = tmp("c_raw", [P, DC, B * S])
            c_hi = tmp("c_hi", [P, DC, B * S], F32R)
            c_lo = tmp("c_lo", [P, DC, B * S], F32R)
            bo_raw = tmp("bo_raw", [P, D])
            gate_raw = tmp("gate_raw", [P, 1])
            pick_raw = tmp("pick_raw", [P, heads, S + 1])
            w_in, c_in = [sem(f"w_in{n}") for n in range(3)], [sem(f"c_in{n}") for n in range(3)]
            o_in, small_in = sem("o_in"), sem("small_in")
            w_rounded, c_rounded, o_rounded = sem("w_rounded"), sem("c_rounded"), sem("o_rounded")
            w_split, c_split = sem("w_split"), sem("c_split")
            k_sum, k_rounded, k_done = sem("k_sum"), sem("k_rounded"), sem("k_done")
            v_sum, v_cleared, v_done, g_done = sem("v_sum"), sem("v_cleared"), sem("v_done"), sem("g_done")
            KN = [(0, 412), (412, 410), (822, 410)]
            KJ = [(i, c, n0, n) for i, (n0, n) in enumerate(KN) for c in range(C)]
            k_banks = [T0, T1, X0, X1, O0, O1]
            NKB = len(k_banks)
            W_PARTS = [slice(inner, 2 * inner), slice(2 * inner, 3 * inner), slice(0, inner)]
            N_SMALL = 4 + (3 if first else 0)

            block = setup.enter_context(nc.Block())

            @block.sync
            def _(sp):
                for n, cols in enumerate(W_PARTS):
                    sp.dma_start(w_raw[:, :, cols], wqkv[:, cols].rearrange("(c p) n -> p c n", p=P),
                                 ).then_inc(w_in[n], 16)
                    if n == 0:
                        for i, (n0, nn) in enumerate(KN):
                            sp.dma_start(c_raw[:, :, n0:n0 + nn],
                                         ctx_t[:, n0:n0 + nn].rearrange("(c p) n -> p c n", p=P)).then_inc(c_in[i], 16)
                        if first:
                            load(sp, 0, 0)
                sp.dma_start(wo_raw[:], wo.rearrange("(c p) n -> p c n", p=P)).then_inc(o_in, 16)
                sp.dma_start(bo_raw[:], gbias).then_inc(small_in, 16)
                sp.dma_start(gate_raw[:], gate).then_inc(small_in, 16)
                sp.dma_start(head_mask[:], env[f"mask{layer}"]).then_inc(small_in, 16)
                sp.dma_start(pick_raw[:], env[f"pick{layer}"]).then_inc(small_in, 16)
                if first:
                    sp.dma_start(bqk[:, 0, :], bq).then_inc(small_in, 16)
                    sp.dma_start(bqk[:, 1, :], bk).then_inc(small_in, 16)
                    sp.dma_start(bv_all[:], bv).then_inc(small_in, 16)
                    load(sp, 1, 1)

            @block.gpsimd
            def _(pool):
                pool.memset(minus_half[:], -0.5).then_inc(ln_cleared, 1)
                pool.memset(eps[:], LN_EPS).then_inc(ln_cleared, 1)
                pool.wait_ge(ln_cleared, 2)
                if not first:
                    ln_inverse(pool, 0)
                pool.memset(values[:], 0.0).then_inc(v_cleared, 1)
                pool.wait_ge(v_cleared, 1)
                pool.memset(values[:, :, :, d:DV], 1.0).then_inc(v_cleared, 1)
                if first:
                    ln_inverse(pool, 0)

            @block.scalar
            def _(act):
                for n, cols in enumerate(W_PARTS):
                    act.wait_ge(w_in[n], 16)
                    act.activation(w_hi[:, :, cols], w_raw[:, :, cols], ACT.Copy).then_inc(w_rounded, 1)
                    if n == 0:
                        for i, (n0, nn) in enumerate(KN):
                            act.wait_ge(c_in[i], 16)
                            act.activation(c_hi[:, :, n0:n0 + nn], c_raw[:, :, n0:n0 + nn],
                                           ACT.Copy).then_inc(c_rounded, 1)
                act.wait_ge(o_in, 16)
                act.activation(wo_hi[:], wo_raw[:], ACT.Copy).then_inc(o_rounded, 1)
                act.wait_ge(small_in, 16 * N_SMALL)
                act.activation(tg[:], gate_raw[:], ACT.Tanh).then_inc(g_done, 1)
                act.activation(pick[:], pick_raw[:], ACT.Copy)
                for n, (_, c, n0, nn) in enumerate(KJ):
                    act.wait_ge(k_sum, n + 1)
                    bias = bqk[:, 1, c:c + 1] if first else 0.0
                    act.activation(k_hi[:, c, n0:n0 + nn], k_banks[n % NKB][:, 0:nn], ACT.Identity,
                                   bias=bias).then_inc(k_rounded, 1)
                act.activation(warm[:], gate_raw[:], ACT.Exp)

            @block.vector
            def _(dve):
                if not first:
                    ln_moments(dve, 0, 0)
                    ln_normalise(dve, 0)
                for n, cols in enumerate(W_PARTS):
                    if first and n == 1:
                        ln_moments(dve, 0, 0)
                    if first and n == 2:
                        ln_normalise(dve, 0)
                    dve.wait_ge(w_rounded, n + 1)
                    dve.tensor_tensor(w_lo[:, :, cols], w_raw[:, :, cols], w_hi[:, :, cols].bitcast(F32),
                                      ALU.subtract).then_inc(w_split, 1)
                    if n == 0:
                        for i, (n0, nn) in enumerate(KN):
                            dve.wait_ge(c_rounded, i + 1)
                            dve.tensor_tensor(c_lo[:, :, n0:n0 + nn], c_raw[:, :, n0:n0 + nn],
                                              c_hi[:, :, n0:n0 + nn].bitcast(F32), ALU.subtract).then_inc(c_split, 1)
                dve.wait_ge(o_rounded, 1)
                dve.tensor_tensor(wo_lo[:], wo_raw[:], wo_hi[:].bitcast(F32), ALU.subtract)
                dve.wait_ge(g_done, 1)
                dve.tensor_scalar(gb[:], bo_raw[:], tg[:, 0:1], None, ALU.mult)
                for n, (_, c, n0, nn) in enumerate(KJ):
                    dve.wait_ge(k_rounded, n + 1)
                    bias = bqk[:, 1, c:c + 1] if first else 0.0
                    dve.scalar_tensor_tensor(
                        out=k_lo[:, c, n0:n0 + nn], in0=k_banks[n % NKB][:, 0:nn], scalar=bias,
                        in1=k_hi[:, c, n0:n0 + nn].bitcast(F32), op0=ALU.add, op1=ALU.subtract,
                    ).then_inc(k_done, 1)
                dve.wait_ge(v_cleared, 2)
                for b in range(B):
                    dve.wait_ge(v_sum, b + 1)
                    src = (S0, S1)[b % 2][0:S, 0:inner].rearrange("p (h v) -> p h v", h=heads)
                    dst = values[0:S, b, :, 0:d]
                    if first:
                        dve.tensor_tensor(dst, src, bv_all[0:S, :].rearrange("p (h v) -> p h v", h=heads),
                                          ALU.add).then_inc(v_done, 1)
                    else:
                        dve.tensor_copy(dst, src).then_inc(v_done, 1)

            @block.tensor
            def _(pe):
                pe.wait_ge(w_split, 1)
                for n, (i, c, n0, nn) in enumerate(KJ):
                    pe.wait_ge(c_split, i + 1)
                    if n >= NKB:
                        pe.wait_ge(k_done, n + 1 - NKB)
                    for kc in range(DC):
                        cols = slice(inner + c * P, inner + (c + 1) * P)
                        last = three_passes(nc, k_banks[n % NKB][:, 0:nn], w_hi[:, kc, cols], w_lo[:, kc, cols],
                                            c_hi[:, kc, n0:n0 + nn], c_lo[:, kc, n0:n0 + nn],
                                            kc == 0, kc == DC - 1)
                    last.then_inc(k_sum, 1)
                pe.wait_ge(w_split, 2)
                for b in range(B):
                    if b >= 2:
                        pe.wait_ge(v_done, b - 1)
                    for kc in range(DC):
                        last = three_passes(nc, (S0, S1)[b % 2][0:S, 0:inner],
                                            c_hi[:, kc, b * S:(b + 1) * S], c_lo[:, kc, b * S:(b + 1) * S],
                                            w_hi[:, kc, 2 * inner:3 * inner], w_lo[:, kc, 2 * inner:3 * inner],
                                            kc == 0, kc == DC - 1)
                    last.then_inc(v_sum, 1)

        xt_hi = sb("xt_hi", [P, DC, T], F32R)
        xt_lo = sb("xt_lo", [P, DC, T], F32R)
        q_hi = sb("q_hi", [P, 2, C, T], F32R)
        q_lo = sb("q_lo", [P, 2, C, T], F32R)
        kb_hi = sb("kb_hi", [P, 2, C, HPC, S], F32R)
        kb_lo = sb("kb_lo", [P, 2, C, HPC, S], F32R)
        maxima = sb("maxima", [P, TT, heads])
        mt = sb("mt", [P, 2, T], F32R)
        prob = sb("prob", [P, 2, 2, T])
        rden = sb("rden", [P, TT, heads])
        att = sb("att", [P, TT, inner])
        at_hi = sb("at_hi", [P, C, T], F32R)
        at_lo = sb("at_lo", [P, C, T], F32R)
        mv2 = sb("mv2", [P, TT, 2])
        bn2 = sb("bn2", [P, TT, 6])
        var2 = sb("var2", [P, TT])
        xn2 = sb("xn2", [P, TT, D])

        if first:
            ffn = env["ffn_weights"]
            FW = ffn["quantised"].shape[2]
            FW_PIECES = B - 4
            fw = sb("fw", [P, 3 * FW])
            fw_code = sb("fw_code", [P, 3 * FW // FW_PIECES], I16)
            fw_scale = sb("fw_scale", [P, 3, 3 * FW // FW_PIECES // BLOCK])
            fw_in, fw_step, fw_done, fw_sent = sem("fw_in"), sem("fw_step"), sem("fw_done"), sem("fw_sent")
        cleared = sem("cleared")
        xt_ready, xt_rounded, xt_split = sem("xt_ready"), sem("xt_rounded"), sem("xt_split")
        q_ready, q_rounded, q_split = sem("q_ready"), sem("q_rounded"), sem("q_split")
        kb_ready, kb_lo_ready = sem("kb_ready"), sem("kb_lo_ready")
        mx_scores, mx_taken, mt_ready, mt_copied = (sem(x) for x in (
            "mx_scores", "mx_taken", "mt_ready", "mt_copied"))
        scores, probs, outs = sem("scores"), sem("probs"), sem("outs")
        den_ready, att_ready = sem("den_ready"), sem("att_ready")
        at_ready, at_rounded, at_split = sem("at_ready"), sem("at_rounded"), sem("at_split")
        proj_ready, x_updated = sem("proj_ready"), sem("x_updated")
        n_bn, n_stats, n_eps, n_rstd, n_xn, n_max = (sem(x) for x in (
            "n_bn", "n_stats", "n_eps", "n_rstd", "n_xn", "n_max"))

        if HP == 8:
            SLOT = ("s0 xt w0 kb w1 s1 p0 q0 w2 s2 p1 w3 at0 w4 s3 p2 mx0 mx1 w5 pr0 pr1 st1 s4 p3 mx2 mx3 ln s5 p4 "
                    "mx4 mx5 xn s6 p5 mx6 mx7 st2 s7 p6 mt p7 norm").split()
        else:
            SLOT = ("s0 s1 xt kb p0 q0 at0 q1 s2 p1 mx0 at1 s3 mx1 p2 mx2 p3 mx3 ln pr0 norm mt xn pr1").split()
        FRONT = {"kb", "xt", "mt"} | {f"q{n}" for n in range(NP)} | {f"mx{n}" for n in range(NG)}
        BACK = {"pr0", "pr1", "st1", "st2"} | {f"at{n}" for n in range(NP)}

        def slots(eng, step):
            def slot(b, par, pre=True, front=True, middle=True, back=True):
                for what in SLOT:
                    if what[0] == "w":
                        if not isinstance(b, int):
                            step(what, b, par)
                        continue
                    if what in ("ln", "xn"):
                        if pre:
                            step(what, b + 2, par)
                    elif what in FRONT:
                        if front:
                            step(what, b + 1, 1 - par)
                    elif what in BACK:
                        if back:
                            step(what, b - 1, 1 - par)
                    elif middle:
                        step(what, b, par)

            slot(-1, 1, middle=False, back=False)
            slot(0, 0, back=False)
            with eng.Fori(0, (B - 4) // 2) as j:
                slot(j * 2 + 1, 1)
                slot(j * 2 + 2, 0)
            slot(B - 3, 1)
            slot(B - 2, 0, pre=False)
            slot(B - 1, 1, pre=False, front=False)
            slot(B, 0, pre=False, front=False, middle=False)

        def masked_keys(eng, full, masked, b, par):
            for c in range(C):
                src = full[:, c, bass.ds(b * S, S)].bitcast(F32)
                last = eng.tensor_tensor(masked[:, par, c, :, :], src.unsqueeze(1).to_broadcast([P, HPC, S]),
                                         head_mask[:].unsqueeze(2).to_broadcast([P, HPC, S]), ALU.mult)
            return last

        block = ctx.enter_context(nc.Block())

        @block.sync
        def _(sp):
            if first:
                for par in range(2):
                    sp.wait_ge(x_loaded[par], 16)
                    load(sp, 2 + par, par)
                for n, w in enumerate(("w_gate", "w_up")):
                    sp.dma_start(fw[:, n * FW:(n + 1) * FW].rearrange("p (f d) -> p f d", d=D),
                                 ffn[w].rearrange("(f p) d -> p f d", p=P)).then_inc(fw_in, 16)
                sp.dma_start(fw[:, 2 * FW:3 * FW].rearrange("p (o f) -> p o f", o=DC),
                             ffn["w_down"].rearrange("(o p) f -> p o f", p=P)).then_inc(fw_in, 16)
                with sp.Fori(2, B // 2) as j:
                    for par in range(2):
                        sp.wait_ge(x_loaded[par], j * 16)
                        load(sp, j * 2 + par, par)
                for n in range(3):
                    sp.wait_ge(fw_done, (n + 1) * FW_PIECES // 3)
                    sp.dma_start(ffn["quantised"][:, n, :], fw[:, n * FW:(n + 1) * FW]).then_inc(fw_sent, 16)
                sp.wait_ge(fw_sent, 48)

        @block.gpsimd
        def _(pool):
            pool.memset(mt[:].bitcast(F32), 0.0).then_inc(cleared, 1)
            pool.memset(prob[:], 0.0).then_inc(cleared, 1)

            def step(what, b, par):
                if what == "kb":
                    if not (isinstance(b, int) and b < 2):
                        pool.wait_ge(outs, (b - 1) * HP)
                    masked_keys(pool, k_lo, kb_lo, b, par).then_inc(kb_lo_ready, 1)
                elif what == "ln":
                    ln_inverse(pool, b)
                    add_bias(pool, b)
                elif what == "st1" and first:
                    pool.wait_ge(n_stats, b + 1)
                    pool.tensor_tensor(var2[:], mv2[:, :, 1], eps[:], ALU.add).then_inc(n_eps, 1)
                    pool.wait_ge(n_eps, b + 1)
                    pool.tensor_tensor(env["rstd_all"][:, bass.ds(b * TT, TT)], var2[:], minus_half[:],
                                       ALU.pow).then_inc(n_rstd, 1)

            add_bias(pool, 0)
            slots(pool, step)

        @block.scalar
        def _(act):
            act.wait_ge(cleared, 2)

            def step(what, b, par):
                if what == "xt":
                    act.wait_ge(xt_ready, b + 1)
                    act.activation(xt_hi[:], T0[:, :], ACT.Copy).then_inc(xt_rounded, 1)
                elif what[0] == "q":
                    n = int(what[1])
                    act.wait_ge(q_ready, b * NP + n + 1)
                    src = (T0, X0)[n]
                    for c in range(2):
                        bias = bqk[:, 0, 2 * n + c:2 * n + c + 1] if first else 0.0
                        last = act.activation(q_hi[:, par, 2 * n + c, :], src[:, c * T:(c + 1) * T],
                                              ACT.Identity, bias=bias)
                    last.then_inc(q_rounded, 1)
                elif what == "mt":
                    act.wait_ge(mt_ready, b + 1)
                    act.activation(mt[0:heads, par, :], T0[0:heads, 0:T], ACT.Copy).then_inc(mt_copied, 1)
                elif what[0] == "s" and what[1] != "t":
                    n = int(what[1])
                    act.wait_ge(scores, b * HP + n + 1)
                    if not (isinstance(b, int) and b == 0 and n < 2):
                        act.wait_ge(outs, b * HP + n - 1)
                    act.activation(prob[0:S, n % 2, :, :].rearrange("p a b -> p (a b)"),
                                   (S0, S1)[n % 2][0:S, :], ACT.Exp, scale=SCALE).then_inc(probs, 1)
                elif what[:2] == "at":
                    n = int(what[2])
                    act.wait_ge(at_ready, b * NP + n + 1)
                    act.activation(at_hi[:, 2 * n:2 * n + 2, :].rearrange("p a b -> p (a b)"), T1[:, :],
                                   ACT.Copy).then_inc(at_rounded, 1)

            slots(act, step)

        @block.vector
        def _(dve):
            dve.sem_inc(x_updated, 1)

            def step(what, b, par):
                if what == "norm":
                    dve.wait_ge(outs, (b + 1) * HP)
                    for t in range(TT):
                        near = heads - 1 if wide else heads
                        o = (O0, O1)[t][:, 0:near * DV].rearrange("p (h v) -> p h v", v=DV)
                        last = dve.reciprocal(rden[:, t, 0:near], o[:, :, d])
                        if wide:
                            last = dve.reciprocal(rden[:, t, near:heads], out_of(t, near)[:, d:DV])
                    last.then_inc(den_ready, 1)
                    dve.wait_ge(den_ready, b + 1)
                    for t in range(TT):
                        near = heads - 1 if wide else heads
                        o = (O0, O1)[t][:, 0:near * DV].rearrange("p (h v) -> p h v", v=DV)
                        a = att[:, t, :].rearrange("p (h v) -> p h v", v=d)
                        last = dve.tensor_tensor(a[:, 0:near, :], o[:, :, 0:d],
                                                 rden[:, t, 0:near].unsqueeze(2).to_broadcast([P, near, d]),
                                                 ALU.mult)
                        if wide:
                            last = dve.tensor_scalar(a[:, near, :], out_of(t, near)[:, 0:d],
                                                     rden[:, t, near:heads], None, ALU.mult)
                    last.then_inc(att_ready, 1)
                elif what == "ln":
                    ln_moments(dve, b, par)
                elif what == "xn":
                    ln_normalise(dve, b)
                elif what == "kb":
                    masked_keys(dve, k_hi, kb_hi, b, par).then_inc(kb_ready, 1)
                elif what[0] == "w":
                    dve.wait_ge(fw_in, 48)
                    quantise_weights(dve, fw, fw_code, fw_scale, b - 1, int(what[1]), fw_step, fw_done)
                elif what == "xt":
                    dve.wait_ge(xt_rounded, b + 1)
                    dve.tensor_tensor(xt_lo[:].rearrange("p a b -> p (a b)"), T0[:, :],
                                      xt_hi[:].rearrange("p a b -> p (a b)").bitcast(F32),
                                      ALU.subtract).then_inc(xt_split, 1)
                elif what[0] == "q":
                    n = int(what[1])
                    dve.wait_ge(q_rounded, b * NP + n + 1)
                    src = (T0, X0)[n]
                    for c in range(2):
                        bias = bqk[:, 0, 2 * n + c:2 * n + c + 1] if first else 0.0
                        last = dve.scalar_tensor_tensor(
                            out=q_lo[:, par, 2 * n + c, :], in0=src[:, c * T:(c + 1) * T], scalar=bias,
                            in1=q_hi[:, par, 2 * n + c, :].bitcast(F32), op0=ALU.add, op1=ALU.subtract)
                    last.then_inc(q_split, 1)
                elif what[:2] == "mx":
                    g = int(what[2])
                    t, h0 = g // (NG // TT), 4 * (g % (NG // TT))
                    dve.wait_ge(mx_scores, b * NG + g + 1)
                    dve.tensor_reduce(maxima[:, t, h0:h0 + 4],
                                      mx_banks[g % NMX][:, 0:4 * S].rearrange("p (h s) -> p h s", s=S),
                                      AX.X, ALU.max).then_inc(mx_taken, 1)
                elif what[:2] == "at":
                    n = int(what[2])
                    dve.wait_ge(at_rounded, b * NP + n + 1)
                    dve.tensor_tensor(at_lo[:, 2 * n:2 * n + 2, :].rearrange("p a b -> p (a b)"), T1[:, :],
                                      at_hi[:, 2 * n:2 * n + 2, :].rearrange("p a b -> p (a b)").bitcast(F32),
                                      ALU.subtract).then_inc(at_split, 1)
                elif what == "pr1":
                    dve.wait_ge(proj_ready, b + 1)
                    dve.wait_ge(biased, b + 1)
                    for t in range(TT):
                        x = xtile(b, t)
                        last = dve.scalar_tensor_tensor(out=x, in0=T1[:, t * D:(t + 1) * D], scalar=tg[:, 0:1],
                                                        in1=x, op0=ALU.mult, op1=ALU.add)
                    last.then_inc(x_updated, 1)
                elif what == "st1" and first:
                    dve.wait_ge(x_updated, b + 2)
                    dve.sem_inc(passed, 1)
                    for t in range(TT):
                        last = dve.bn_stats(bn2[:, t, :], xtile(b, t))
                    last.then_inc(n_bn, 1)
                    dve.wait_ge(n_bn, b + 1)
                    dve.sem_inc(passed, 1)
                    for t in range(TT):
                        last = dve.bn_aggr(mv2[:, t, :], bn2[:, t, :])
                    last.then_inc(n_stats, 1)
                elif what == "st2" and first:
                    dve.wait_ge(n_rstd, b + 1)
                    dve.tensor_copy(env["mean_all"][:, bass.ds(b * TT, TT)], mv2[:, :, 0])
                    for t in range(TT):
                        last = dve.tensor_scalar(xn2[:, t, :], xtile(b, t), mv2[:, t, 0:1],
                                                 env["rstd_all"][:, bass.ds(b * TT + t, 1)],
                                                 ALU.subtract, ALU.mult)
                    last.then_inc(n_xn, 1)
                    dve.wait_ge(n_xn, b + 1)
                    dve.tensor_reduce(env["amax_x"][:, bass.ds(b, 1)],
                                      xn2[:].rearrange("p t d -> p (t d)"), AX.X, ALU.max,
                                      apply_absolute_value=True).then_inc(n_max, 1)

            slots(dve, step)

        @block.tensor
        def _(pe):
            def step(what, b, par):
                if what == "xt":
                    pe.wait_ge(ln_xn, b + 1)
                    pe.wait_ge(mt_copied, b)
                    for c in range(DC):
                        for t in range(TT):
                            last = pe.transpose(T0[:, c * T + t * P:c * T + (t + 1) * P],
                                                xn[:, t, c * P:(c + 1) * P], ident[:])
                    last.then_inc(xt_ready, 1)
                elif what[0] == "q":
                    n = int(what[1])
                    pe.wait_ge(xt_split, b + 1)
                    for c in range(2):
                        cols = slice((2 * n + c) * P, (2 * n + c + 1) * P)
                        for kc in range(DC):
                            last = three_passes(nc, (T0, X0)[n][:, c * T:(c + 1) * T],
                                                w_hi[:, kc, cols], w_lo[:, kc, cols],
                                                xt_hi[:, kc, :], xt_lo[:, kc, :], kc == 0, kc == DC - 1)
                    last.then_inc(q_ready, 1)
                elif what[:2] == "mx":
                    g = int(what[2])
                    t, h0 = g // (NG // TT), 4 * (g % (NG // TT))
                    if g == 0:
                        pe.wait_ge(kb_ready, b + 1)
                        pe.wait_ge(q_split, (b + 1) * NP)
                    if not (isinstance(b, int) and b == 0 and g < NMX):
                        pe.wait_ge(mx_taken, b * NG + g + 1 - NMX)
                    per = min(4, HPC)
                    for h in range(h0, h0 + 4, per):
                        c, r = h // HPC, h % HPC
                        last = pe.matmul(mx_banks[g % NMX][:, (h - h0) * S:(h - h0 + per) * S],
                                         q_hi[:, par, c, t * P:(t + 1) * P],
                                         kb_hi[:, par, c, r:r + per, :].rearrange("p a b -> p (a b)"),
                                         start=True, stop=True)
                    last.then_inc(mx_scores, 1)
                elif what == "mt":
                    pe.wait_ge(mx_taken, (b + 1) * NG)
                    for t in range(TT):
                        last = pe.transpose(T0[0:heads, t * P:(t + 1) * P], maxima[:, t, :], ident[:])
                    last.then_inc(mt_ready, 1)
                elif what[0] == "s" and what[1] != "t":
                    n = int(what[1])
                    if n == 0:
                        pe.wait_ge(mt_copied, b + 1)
                        pe.wait_ge(kb_lo_ready, b + 1)
                    if not (isinstance(b, int) and b == 0 and n < 2):
                        pe.wait_ge(probs, b * HP + n - 1)
                    for hh in range(2):
                        h = 2 * n + hh
                        c, r = h // HPC, h % HPC
                        out = (S0, S1)[n % 2][0:S, hh * T:(hh + 1) * T]
                        three_passes(nc, out, kb_hi[:, par, c, r, :], kb_lo[:, par, c, r, :],
                                     q_hi[:, par, c, :], q_lo[:, par, c, :], True, False)
                        last = pe.matmul(out, pick[:, h, 0:S], mt[:, par, :], start=False, stop=True)
                    last.then_inc(scores, 1)
                elif what[0] == "p" and what[1] != "r":
                    n = int(what[1])
                    pe.wait_ge(probs, b * HP + n + 1)
                    if n == 0:
                        pe.wait_ge(att_ready, b)
                    for hh in range(2):
                        h = 2 * n + hh
                        for t in range(TT):
                            v = values[:, bass.ds(b, 1), h, :].rearrange("p o v -> p (o v)")
                            last = pe.matmul(out_of(t, h), prob[:, n % 2, hh, t * P:(t + 1) * P], v,
                                             start=True, stop=True)
                    last.then_inc(outs, 1)
                elif what[:2] == "at":
                    n = int(what[2])
                    pe.wait_ge(att_ready, b + 1)
                    if n == 0:
                        pe.wait_ge(x_updated, b + 1)
                    else:
                        pe.wait_ge(at_split, b * NP + n)
                    for c in range(2):
                        for t in range(TT):
                            cols = slice((2 * n + c) * P, (2 * n + c + 1) * P)
                            last = pe.transpose(T1[:, c * T + t * P:c * T + (t + 1) * P], att[:, t, cols],
                                                ident[:])
                    last.then_inc(at_ready, 1)
                elif what[:2] == "pr":
                    t = int(what[2])
                    if t == 0:
                        pe.wait_ge(at_split, (b + 1) * NP)
                    for c in range(C):
                        last = three_passes(nc, T1[:, t * D:(t + 1) * D],
                                            at_hi[:, c, t * P:(t + 1) * P], at_lo[:, c, t * P:(t + 1) * P],
                                            wo_hi[:, c, :], wo_lo[:, c, :], c == 0, c == C - 1)
                    if t == TT - 1:
                        last.then_inc(proj_ready, 1)

            slots(pe, step)

    free_semaphores(nc, sems)


def quantised_ffn(nc, env, weights, gate, butterfly):
    bf = butterfly
    xres, banks, ident = env["xres"], env["banks"], env["ident"]
    T0, T1, X0, X1, S0, S1, O0, O1 = banks
    FT = HID0 // P
    G = NT * P // GT
    GTT = GT // P
    sems = []
    ctx = ExitStack()
    with ctx:
        def sb(name, shape, dt=F32):
            return ctx.enter_context(nc.sbuf_tensor(f"f0_{name}", shape, dt))

        def sem(name):
            sems.append(nc.alloc_semaphore(f"f0_{name}"))
            return sems[-1]

        scales = sb("scales", [P, 5])
        codes = sb("codes", [P, 5])
        small = sb("small", [P, 4])
        unit = sb("unit", [P, 5])
        tg = sb("tg", [P, 1])
        warm = sb("warm", [P, 1])
        amax = sb("amax", [P, 2, G, FT])
        SX, SG, SU, S2, SO = range(5)
        d_hi = sb("d_hi", [P, FT, D], F32R)
        d_lo = sb("d_lo", [P, FT, D], F32R)
        hid = sb("hid", [P, FT, NT * P])
        HT = HID1 // P
        TOP = HT.bit_length() - 1
        LOW = P.bit_length() - 1
        top_coef = sb("top_coef", [P, 2, TOP, 2, HT])
        low_coef = sb("low_coef", [P, 2, LOW, 2, HT])
        wide = ExitStack()
        w_hi = wide.enter_context(nc.sbuf_tensor("f0_w_hi", [P, 2, DC, HID0], F32R))
        w_lo = wide.enter_context(nc.sbuf_tensor("f0_w_lo", [P, 2, DC, HID0], F32R))

        def scale_steps(dve, k, done, at):
            dve.tensor_scalar(small[:, 2:3], small[:, 0:1], unit[:, k:k + 1], 1.0 / ACT_MAX,
                              ALU.mult, ALU.mult).then_inc(done, 1)
            dve.wait_ge(done, at + 1)
            dve.tensor_scalar(scales[:, k:k + 1], small[:, 2:3], TINY, None, ALU.max).then_inc(done, 1)
            dve.wait_ge(done, at + 2)
            dve.reciprocal(small[:, 3:4], scales[:, k:k + 1]).then_inc(done, 1)
            dve.wait_ge(done, at + 3)
            dve.tensor_tensor(codes[:, k:k + 1], small[:, 3:4], unit[:, k:k + 1], ALU.mult).then_inc(done, 1)
            dve.wait_ge(done, at + 4)

        def top_stage(pool, y, own, pair, net, i, multiplied, added, at):
            n = y.shape[2]
            r = 1 << i if net == 0 else HT >> (i + 1)
            pool.tensor_tensor(own, y, top_coef[:, net, i, 0, :].unsqueeze(2).to_broadcast([P, HT, n]), ALU.mult)
            yv, pv, cv = (x.rearrange("p (k two s) d -> p k two s d", two=2, s=r) for x in (
                y, pair, top_coef[:, net, i, 1, :].unsqueeze(2).to_broadcast([P, HT, n])))
            for half in range(2):
                for k in range(HT // (2 * r)):
                    last = pool.tensor_tensor(pv[:, k, half, :, :], yv[:, k, 1 - half, :, :], cv[:, k, half, :, :],
                                              ALU.mult)
            last.then_inc(multiplied, 1)
            pool.wait_ge(multiplied, at + 1)
            pool.tensor_tensor(y, own, pair, ALU.add).then_inc(added, 1)
            pool.wait_ge(added, at + 1)

        with ExitStack() as setup:
            wval = setup.enter_context(nc.sbuf_tensor("f0_wval", [P, 3 * FT, D], F32))
            w_in, g_in = [sem(f"w_in{n}") for n in range(3)], sem("g_in")
            turned, w_rounded, w_split = sem("turned"), sem("w_rounded"), sem("w_split")
            x_max, x_all, x_scale = sem("x_max"), sem("x_all"), sem("x_scale")
            turns = []
            for net in range(2):
                for c in range(DC):
                    for f0 in range(0, FT, 3):
                        turns.append(([(net * FT + f, c * P) for f in range(f0, f0 + 3)],
                                      (w_hi[:, net, c, f0 * P:(f0 + 3) * P], w_lo[:, net, c, f0 * P:(f0 + 3) * P])))
            for f in range(FT):
                turns.append(([(2 * FT + 3 * o + f // 2, (f % 2) * P) for o in range(DC)],
                              (d_hi[:, f, :], d_lo[:, f, :])))
            block = setup.enter_context(nc.Block())

            @block.sync
            def _(sp):
                for n in range(3):
                    sp.dma_start(wval[:, n * FT:(n + 1) * FT, :].rearrange("p f d -> p (f d)"),
                                 weights[:, n, :]).then_inc(w_in[n], 16)
                sp.dma_start(tg[:], gate).then_inc(g_in, 16)

            @block.vector
            def _(dve):
                dve.memset(unit[:, SX:SX + 1], 1.0)
                dve.tensor_reduce(small[:, 1:2], env["amax_x"][:], AX.X, ALU.max).then_inc(x_max, 1)
                dve.wait_ge(x_all, 1)
                scale_steps(dve, SX, x_scale, 0)
                for n, (pieces, (hi, lo)) in enumerate(turns):
                    dve.wait_ge(w_rounded, n + 1)
                    dve.tensor_tensor(lo, banks[n % 8][:, 0:len(pieces) * P], hi.bitcast(F32),
                                      ALU.subtract).then_inc(w_split, 1)

            @block.gpsimd
            def _(pool):
                pool.wait_ge(x_max, 1)
                pool.partition_all_reduce(small[:, 0:1], small[:, 1:2], P, RMAX).then_inc(x_all, 1)

            @block.tensor
            def _(pe):
                for n, (pieces, _) in enumerate(turns):
                    pe.wait_ge(w_in[pieces[0][0] // FT], 16)
                    if n >= 8:
                        pe.wait_ge(w_split, n - 7)
                    for i, (tile, col) in enumerate(pieces):
                        last = pe.transpose(banks[n % 8][:, i * P:(i + 1) * P], wval[:, tile, col:col + P],
                                            ident[:])
                    last.then_inc(turned, 1)

            @block.scalar
            def _(act):
                for n, (pieces, (hi, lo)) in enumerate(turns):
                    act.wait_ge(turned, n + 1)
                    act.activation(hi, banks[n % 8][:, 0:len(pieces) * P], ACT.Copy).then_inc(w_rounded, 1)
                act.wait_ge(g_in, 16)
                act.activation(tg[:], tg[:], ACT.Tanh)

        with wide, ExitStack() as ph:
            def tmp(name, shape, dt=F32):
                return ph.enter_context(nc.sbuf_tensor(f"f0_{name}", shape, dt))

            xn = tmp("xn", [P, GTT, D])
            xcode = tmp("xcode", [P, GTT, D], I16)
            xt_hi = tmp("xt_hi", [P, 2, DC, GT], F32R)
            xt_lo = tmp("xt_lo", [P, 2, DC, GT], F32R)
            NU = 3
            ubuf = tmp("ubuf", [P, NU, GT])
            x_normed, x_coded, x_float, xt_ready, xt_rounded, xt_split = (sem(x) for x in (
                "x_normed", "x_coded", "x_float", "xt_ready", "xt_rounded", "xt_split"))
            prods, stored, maxed = sem("prods"), sem("stored"), sem("maxed")
            u_sent = [sem(f"u_sent{n}") for n in range(NU)]
            mm = [X0, X1, S0, S1, O0, O1]
            M = 2 * FT
            HW = D // 2
            z = tmp("z", [P, HT, HW])
            z_own = tmp("z_own", [P, HT, HW])
            z_pair = tmp("z_pair", [P, HT, HW])
            coef_in, z_in, z_mul, z_add, z_sent = (sem(x) for x in ("coef_in", "z_in", "z_mul", "z_add", "z_sent"))
            block = ph.enter_context(nc.Block())

            def slots(eng, step):
                def slot(g, par, front=True, back=True):
                    for n in range(M):
                        if front and n == 1:
                            step("ln", 0, g + 1, 1 - par)
                        if front and n == 5:
                            step("x", 0, g + 1, 1 - par)
                        if back:
                            step("m", n, g, par)

                slot(-1, 1, back=False)
                slot(0, 0)
                with eng.Fori(0, (G - 2) // 2) as j:
                    slot(j * 2 + 1, 1)
                    slot(j * 2 + 2, 0)
                slot(G - 1, 1, front=False)

            @block.vector
            def _(dve):
                def step(what, n, g, par):
                    if what == "ln":
                        for t in range(GTT):
                            last = dve.tensor_scalar(
                                xn[:, t, :], xres[:, bass.ds(g * GTT + t, 1), :].rearrange("p o d -> p (o d)"),
                                env["mean_all"][:, bass.ds(g * GTT + t, 1)],
                                env["rstd_all"][:, bass.ds(g * GTT + t, 1)], ALU.subtract, ALU.mult)
                        last.then_inc(x_normed, 1)
                        dve.wait_ge(x_normed, g + 1)
                        dve.tensor_scalar(xcode[:], xn[:], codes[:, SX:SX + 1], None, ALU.mult).then_inc(x_coded, 1)
                        dve.wait_ge(x_coded, g + 1)
                        dve.tensor_copy(xn[:], xcode[:]).then_inc(x_float, 1)
                    elif what == "x":
                        for c in range(DC):
                            dve.wait_ge(xt_rounded, g * DC + c + 1)
                            dve.tensor_tensor(xt_lo[:, par, c, :], (T0, T1)[c][:, :],
                                              xt_hi[:, par, c, :].bitcast(F32), ALU.subtract).then_inc(xt_split, 1)
                    else:
                        dve.wait_ge(stored, g * M + n + 1)
                        dve.tensor_reduce(amax[:, n % 2, bass.ds(g, 1), n // 2], mm[n % 6][:, :], AX.X, ALU.max,
                                          apply_absolute_value=True).then_inc(maxed, 1)

                slots(dve, step)

            @block.tensor
            def _(pe):
                def step(what, n, g, par):
                    if what == "x":
                        pe.wait_ge(x_float, g + 1)
                        for c in range(DC):
                            pe.wait_ge(xt_split, g * DC)
                            for t in range(GTT):
                                last = pe.transpose((T0, T1)[c][:, t * P:(t + 1) * P],
                                                    xn[:, t, c * P:(c + 1) * P], ident[:])
                            last.then_inc(xt_ready, 1)
                    elif what == "m":
                        if n == 0:
                            pe.wait_ge(xt_split, (g + 1) * DC)
                        if not (isinstance(g, int) and g == 0 and n < 6):
                            pe.wait_ge(maxed, g * M + n - 5)
                        f = n // 2
                        for c in range(DC):
                            last = three_passes(nc, mm[n % 6][:, :],
                                                w_hi[:, n % 2, c, f * P:(f + 1) * P],
                                                w_lo[:, n % 2, c, f * P:(f + 1) * P],
                                                xt_hi[:, par, c, :], xt_lo[:, par, c, :], c == 0, c == DC - 1)
                        last.then_inc(prods, 1)

                slots(pe, step)

            @block.scalar
            def _(act):
                def step(what, n, g, par):
                    if what == "x":
                        for c in range(DC):
                            act.wait_ge(xt_ready, g * DC + c + 1)
                            act.activation(xt_hi[:, par, c, :], (T0, T1)[c][:, :], ACT.Copy).then_inc(xt_rounded, 1)
                    if what != "m":
                        return
                    act.wait_ge(prods, g * M + n + 1)
                    f = n // 2
                    if n % 2 == 0:
                        act.activation(hid[:, f, bass.ds(g * GT, GT)], mm[n % 6][:, :], ACT.Copy).then_inc(stored, 1)
                    else:
                        if not (isinstance(g, int) and g == 0 and f < NU):
                            act.wait_ge(u_sent[f % NU], g * 32 + (f // NU) * 16)
                        act.activation(ubuf[:, f % NU, :], mm[n % 6][:, :], ACT.Copy).then_inc(stored, 1)

                slots(act, step)

            @block.sync
            def _(sp):
                with sp.Fori(0, G) as g:
                    for f in range(FT):
                        sp.wait_ge(stored, g * M + 2 * f + 2)
                        sp.dma_start(env["u_dram"][:, f, bass.ds(g * GT, GT)],
                                     ubuf[:, f % NU, :]).then_inc(u_sent[f % NU], 16)
                for k in range(NU):
                    sp.wait_ge(u_sent[k], G * 32)

            @block.gpsimd
            def _(pool):
                pool.dma_start(top_coef[:], bf["top_coef"]).then_inc(coef_in, 16)
                pool.dma_start(low_coef[:], bf["low_coef"]).then_inc(coef_in, 16)
                pool.wait_ge(coef_in, 32)
                for half in range(2):
                    cols = slice(half * HW, (half + 1) * HW)
                    if half:
                        pool.wait_ge(z_sent, 16)
                    pool.dma_start(z[:], bf["w_con"][:, cols].rearrange("(t p) d -> p t d", p=P)).then_inc(z_in, 16)
                    pool.wait_ge(z_in, 16 * (half + 1))
                    for i in range(TOP):
                        top_stage(pool, z[:], z_own[:], z_pair[:], 1, i, z_mul, z_add, half * TOP + i)
                    pool.dma_start(bf["w2_dram"][:, :, cols], z[:]).then_inc(z_sent, 16)
                pool.wait_ge(z_sent, 32)

        NCH = 12
        CW = FT * NT * P // NCH
        flat = hid[:].rearrange("p f t -> p (f t)")
        u_flat = env["u_dram"].rearrange("p f t -> p (f t)")
        cmax = amax[:].rearrange("p n g f -> p (n g f)")

        blocks = sb("blocks", [P, 2, HT, P])
        NR = 3
        u_back = [sem(f"u_back{n}") for n in range(NR)]
        first_u = sb("first_u", [P, CW])

        with ExitStack() as ph:
            b_own = ph.enter_context(nc.sbuf_tensor("f0_b_own", [P, 2, HT, P], F32))
            b_cross = ph.enter_context(nc.sbuf_tensor("f0_b_cross", [P, 2, HT, P], F32))
            flip = ph.enter_context(nc.sbuf_tensor("f0_flip", [P, 2, P], F32))
            b_cleared = [sem("b_cleared0"), sem("b_cleared1")]
            flip_in = [sem(f"flip_in{net}") for net in range(2)]
            b_scaled, b_summed, b_ready = ([sem(f"{x}{net}") for net in range(2)] for x in (
                "b_scaled", "b_summed", "b_ready"))
            bank_of = [[X0, X1], [S0, S1]]

            def per_row(net, i, k):
                return low_coef[:, net, bass.ds(i, 1), k, :].rearrange("p o t -> p (o t)").unsqueeze(
                    2).to_broadcast([P, HT, P])

            def first_step(eng, net):
                eng.wait_ge(flip_in[net], 16)
                eng.tensor_tensor(b_own[:, net], ident[:].unsqueeze(1).to_broadcast([P, HT, P]),
                                  per_row(net, 0, 0), ALU.mult)
                eng.tensor_tensor(b_cross[:, net], flip[:, net, :].unsqueeze(1).to_broadcast([P, HT, P]),
                                  per_row(net, 0, 1), ALU.mult).then_inc(b_cleared[net], 1)
                eng.wait_ge(b_cleared[net], 1)
                eng.tensor_tensor(blocks[:, net], b_own[:, net], b_cross[:, net], ALU.add).then_inc(b_ready[net], 1)

            gcode = ph.enter_context(nc.sbuf_tensor("f0_gcode", [P, 2, CW], I16))
            sig = ph.enter_context(nc.sbuf_tensor("f0_sig", [P, 2, CW], F32))
            scode = ph.enter_context(nc.sbuf_tensor("f0_scode", [P, 2, CW], U16))
            t_max, t_all, t_scale = sem("t_max"), sem("t_all"), sem("t_scale")
            gcoded, sig_ready, scoded, gated, c_maxed = (sem(x) for x in (
                "gcoded", "sig_ready", "scoded", "gated", "c_maxed"))
            block = ph.enter_context(nc.Block())

            @block.gpsimd
            def _(pool):
                for n in range(2):
                    pool.wait_ge(t_max, n + 1)
                    pool.partition_all_reduce(small[:, 0:1], small[:, 1:2], P, RMAX).then_inc(t_all, 1)

                first_step(pool, 0)
                with pool.Fori(1, LOW) as i:
                    for net in range(2):
                        pool.wait_ge(b_ready[net], i)
                        pool.tensor_tensor(b_own[:, net], blocks[:, net], per_row(net, i, 0), ALU.mult)
                        pool.tensor_tensor(b_cross[:, net], blocks[:, net], per_row(net, i, 1),
                                           ALU.mult).then_inc(b_scaled[net], 1)

            @block.sync
            def _(sp):
                sp.dma_start(first_u[:], u_flat[:, 0:CW]).then_inc(u_back[0], 16)
                for i in range(2):
                    for net in range(2):
                        if i == 1:
                            sp.wait_ge(b_cleared[net], 1)
                        sp.dma_start(flip[:, net, :], bf["flips"][:, net, i, :]).then_inc(flip_in[net], 16)
                with sp.Fori(2, LOW) as i:
                    for net in range(2):
                        sp.wait_ge(b_summed[net], i - 1)
                        sp.dma_start(flip[:, net, :], bf["flips"][:, net, bass.ds(i, 1), :].rearrange(
                            "p o m -> p (o m)")).then_inc(flip_in[net], 16)

            @block.tensor
            def _(pe):
                with pe.Fori(1, LOW) as i:
                    for net in range(2):
                        pe.wait_ge(b_scaled[net], i)
                        pe.wait_ge(flip_in[net], i * 16 + 16)
                        for k in range(2):
                            tiles = slice(k * HT // 2, (k + 1) * HT // 2)
                            pe.matmul(bank_of[net][k][:, :], ident[:],
                                      b_own[:, net, tiles, :].rearrange("p t m -> p (t m)"), start=True, stop=False)
                            last = pe.matmul(bank_of[net][k][:, :],
                                             flip[:, net, :],
                                             b_cross[:, net, tiles, :].rearrange("p t m -> p (t m)"),
                                             start=False, stop=True)
                        last.then_inc(b_summed[net], 1)

            @block.vector
            def _(dve):
                for n, k in enumerate((SG, SU)):
                    dve.tensor_copy(unit[:, k:k + 1], scales[:, SX:SX + 1])
                    dve.tensor_reduce(small[:, 1:2], amax[:, n, :, :].rearrange("p g f -> p (g f)"), AX.X,
                                      ALU.max).then_inc(t_max, 1)
                    dve.wait_ge(t_all, n + 1)
                    scale_steps(dve, k, t_scale, 4 * n)
                dve.tensor_scalar(unit[:, S2:S2 + 1], scales[:, SG:SG + 1], 1.0 / 65536, None, ALU.mult)
                first_step(dve, 1)

                def sig_code(i, par):
                    dve.wait_ge(sig_ready, i + 1)
                    dve.tensor_scalar(scode[:, par, :], sig[:, par, :], 65536.0, None, ALU.mult).then_inc(scoded, 1)

                def product(i, par, following):
                    part = flat[:, bass.ds(i * CW, CW)]
                    dve.wait_ge(scoded, i + 1)
                    dve.tensor_tensor(part, gcode[:, par, :], scode[:, par, :], ALU.mult).then_inc(gated, 1)
                    if following:
                        sig_code(i + 1, 1 - par)
                    dve.wait_ge(gated, i + 1)
                    dve.tensor_reduce(cmax[:, bass.ds(i, 1)], part, AX.X, ALU.max,
                                      apply_absolute_value=True).then_inc(c_maxed, 1)

                sig_code(0, 0)
                with dve.Fori(0, NCH // 2 - 1) as j:
                    product(j * 2, 0, True)
                    product(j * 2 + 1, 1, True)
                product(NCH - 2, 0, True)
                product(NCH - 1, 1, False)

            @block.scalar
            def _(act):
                act.activation(warm[:], tg[:], ACT.Sigmoid)
                act.wait_ge(t_scale, 4)

                def chunk(i, par, again):
                    if again:
                        act.wait_ge(gated, i - 1)
                    act.activation(gcode[:, par, :], flat[:, bass.ds(i * CW, CW)], ACT.Identity,
                                   scale=codes[:, SG:SG + 1]).then_inc(gcoded, 1)
                    act.wait_ge(gcoded, i + 1)
                    act.activation(sig[:, par, :], gcode[:, par, :], ACT.Sigmoid,
                                   scale=scales[:, SG:SG + 1]).then_inc(sig_ready, 1)

                def composed(i, net):
                    act.wait_ge(b_summed[net], i)
                    for k in range(2):
                        last = act.activation(
                            blocks[:, net, k * HT // 2:(k + 1) * HT // 2, :].rearrange("p t m -> p (t m)"),
                            bank_of[net][k][:, :], ACT.Copy)
                    last.then_inc(b_ready[net], 1)

                chunk(0, 0, False)
                chunk(1, 1, False)
                with act.Fori(1, NCH // 2) as j:
                    chunk(j * 2, 0, True)
                    composed(j, 0)
                    chunk(j * 2 + 1, 1, True)
                    composed(j, 1)
                composed(LOW - 1, 0)
                composed(LOW - 1, 1)

        with ExitStack() as ph:
            ubuf = [first_u] + [ph.enter_context(nc.sbuf_tensor(f"f0_uback{n}", [P, CW], F32)) for n in range(1, NR)]
            ucode = ph.enter_context(nc.sbuf_tensor("f0_ucode", [P, 2, CW], I16))
            gcode = ph.enter_context(nc.sbuf_tensor("f0_g2code", [P, 2, CW], I16))
            d_max, d_all, d_scale = sem("d_max"), sem("d_all"), sem("d_scale")
            ucoded, g2coded, multiplied, d_maxed = (sem(x) for x in ("ucoded", "g2coded", "multiplied", "d_maxed"))
            y = ph.enter_context(nc.sbuf_tensor("f0_y", [P, HT, D + 1], F32))
            z = ph.enter_context(nc.sbuf_tensor("f0_z2", [P, HT * (D + 1)], F32))
            z_tiles = z[:, 0:HT * D].rearrange("p (t d) -> p t d", d=D)
            y_own = z[:].rearrange("p (t d) -> p t d", d=D + 1)
            HWB = D // 2 + 1
            y_pair = blocks[:].rearrange("p n t m -> p (n t m)")[:, 0:HT * HWB].rearrange("p (t d) -> p t d", d=HWB)
            y_in, z_back, y_prod, z_prod, bias_prod, y_out, z_out, bias_out, z_stored, y_mul, y_add, y_stored = (
                sem(x) for x in ("y_in", "z_back", "y_prod", "z_prod", "bias_prod", "y_out", "z_out", "bias_out",
                                 "z_stored", "y_mul", "y_add", "y_stored"))
            y_banks, z_banks = [X0, X1, S0, S1], [O0, O1, T0, T1]
            block = ph.enter_context(nc.Block())

            @block.sync
            def _(sp):
                def load(j, k):
                    sp.dma_start(ubuf[k][:], u_flat[:, bass.ds((j * NR + k) * CW, CW)]).then_inc(u_back[k], 16)

                load(0, 1)
                sp.dma_start(z_tiles, bf["w2_dram"]).then_inc(z_back, 16)
                sp.dma_start(y[:], bf["w_exp_t"].rearrange("(t p) d -> p t d", p=P)).then_inc(y_in, 16)
                load(0, 2)
                for k in range(NR):
                    sp.wait_ge(ucoded, k + 1)
                    load(1, k)
                    if k == 1:
                        sp.wait_ge(z_out, 1)
                        sp.dma_start(bf["w2_dram"], z_tiles).then_inc(z_stored, 16)
                with sp.Fori(2, NCH // NR) as j:
                    for k in range(NR):
                        sp.wait_ge(ucoded, (j - 1) * NR + k + 1)
                        load(j, k)
                sp.wait_ge(y_add, 2 * TOP)
                sp.dma_start(bf["w1_dram"], y[:]).then_inc(y_stored, 16)
                sp.wait_ge(y_stored, 16)
                sp.wait_ge(z_stored, 16)

            @block.tensor
            def _(pe):
                pe.wait_ge(z_back, 16)
                for t in range(HT):
                    last = pe.matmul(z_banks[t // 2][:, (t % 2) * D:(t % 2 + 1) * D], blocks[:, 1, t, :],
                                     z_tiles[:, t, :], start=True, stop=True)
                last.then_inc(z_prod, 1)
                pe.wait_ge(y_in, 16)
                for t in range(HT):
                    last = pe.matmul(y_banks[t // 2][:, (t % 2) * D:(t % 2 + 1) * D], blocks[:, 0, t, :],
                                     y[:, t, 0:D], start=True, stop=True)
                last.then_inc(y_prod, 1)
                pe.wait_ge(z_out, 1)
                for t in range(HT):
                    last = pe.matmul(T0[:, t:t + 1], blocks[:, 0, t, :], y[:, t, D:D + 1], start=True, stop=True)
                last.then_inc(bias_prod, 1)

            @block.scalar
            def _(act):
                def chunk(j, k, n):
                    i = j * 6 + n
                    act.wait_ge(u_back[k], (j * 2 + n // NR + 1) * 16)
                    if not (isinstance(j, int) and j == 0 and n < 2):
                        act.wait_ge(multiplied, i - 1)
                    act.activation(ucode[:, n % 2, :], ubuf[k][:], ACT.Identity,
                                   scale=codes[:, SU:SU + 1]).then_inc(ucoded, 1)
                    act.activation(gcode[:, n % 2, :], flat[:, bass.ds(i * CW, CW)], ACT.Identity,
                                   scale=codes[:, S2:S2 + 1]).then_inc(g2coded, 1)

                def tiles_out(banks_, dst, done):
                    for k, bank in enumerate(banks_):
                        last = act.activation(dst[:, 2 * k:2 * k + 2, :],
                                              bank[:, :].rearrange("p (t d) -> p t d", d=D), ACT.Copy)
                    last.then_inc(done, 1)

                act.wait_ge(d_scale, 5)
                chunk(0, 0, 0)
                chunk(0, 1, 1)
                act.wait_ge(z_prod, 1)
                tiles_out(z_banks, z_tiles, z_out)
                chunk(0, 2, 2)
                act.wait_ge(y_prod, 1)
                tiles_out(y_banks, y[:, :, 0:D], y_out)
                act.wait_ge(bias_prod, 1)
                act.activation(y[:, :, D], T0[:, 0:HT], ACT.Copy).then_inc(bias_out, 1)
                for n in range(3, 6):
                    chunk(0, n % NR, n)
                with act.Fori(1, NCH // 6) as j:
                    for n in range(6):
                        chunk(j, n % NR, n)

            @block.gpsimd
            def _(pool):
                pool.wait_ge(d_max, 1)
                pool.partition_all_reduce(small[:, 0:1], small[:, 1:2], P, RMAX).then_inc(d_all, 1)
                pool.wait_ge(bias_out, 1)
                pool.wait_ge(z_stored, 16)
                for n, (c0, c1) in enumerate(((0, D // 2), (D // 2, D + 1))):
                    for i in range(TOP):
                        top_stage(pool, y[:, :, c0:c1], y_own[:, :, c0:c1], y_pair[:, :, 0:c1 - c0], 0, i,
                                  y_mul, y_add, n * TOP + i)

            @block.vector
            def _(dve):
                dve.tensor_reduce(small[:, 1:2], cmax[:, 0:NCH], AX.X, ALU.max).then_inc(d_max, 1)
                dve.wait_ge(d_all, 1)
                scale_steps(dve, S2, d_scale, 0)
                dve.tensor_tensor(unit[:, SO:SO + 1], scales[:, S2:S2 + 1], scales[:, SU:SU + 1],
                                  ALU.mult).then_inc(d_scale, 1)

                def product(i, par):
                    part = flat[:, bass.ds(i * CW, CW)]
                    dve.wait_ge(g2coded, i + 1)
                    dve.tensor_tensor(part, gcode[:, par, :], ucode[:, par, :], ALU.mult).then_inc(multiplied, 1)

                def maximum(i):
                    dve.wait_ge(multiplied, i + 1)
                    dve.tensor_reduce(cmax[:, bass.ds(i, 1)], flat[:, bass.ds(i * CW, CW)], AX.X, ALU.max,
                                      apply_absolute_value=True).then_inc(d_maxed, 1)

                product(0, 0)
                with dve.Fori(0, NCH // 2 - 1) as j:
                    product(j * 2 + 1, 1)
                    maximum(j * 2)
                    product(j * 2 + 2, 0)
                    maximum(j * 2 + 1)
                product(NCH - 1, 1)
                maximum(NCH - 2)
                maximum(NCH - 1)

        with ExitStack() as ph:
            ocode = ph.enter_context(nc.sbuf_tensor("f0_ocode", [P, 2, FT, T], I16))
            o_hi = ph.enter_context(nc.sbuf_tensor("f0_o_hi", [P, 2, FT, T], F32R))
            o_lo = ph.enter_context(nc.sbuf_tensor("f0_o_lo", [P, 2, FT, T], F32R))
            back = ph.enter_context(nc.sbuf_tensor("f0_back", [P, 1], F32))
            e_max, e_all, e_scale = sem("e_max"), sem("e_all"), sem("e_scale")
            ocoded, o_rounded, o_split, down, e_added = (sem(x) for x in (
                "ocoded", "o_rounded", "o_split", "down", "e_added"))
            block = ph.enter_context(nc.Block())
            ybank = [X0, X1, S0, S1]

            @block.gpsimd
            def _(pool):
                pool.wait_ge(e_max, 1)
                pool.partition_all_reduce(small[:, 0:1], small[:, 1:2], P, RMAX).then_inc(e_all, 1)

            @block.vector
            def _(dve):
                dve.tensor_reduce(small[:, 1:2], cmax[:, 0:NCH], AX.X, ALU.max).then_inc(e_max, 1)
                dve.wait_ge(e_all, 1)
                scale_steps(dve, SO, e_scale, 0)
                dve.tensor_tensor(back[:], scales[:, SO:SO + 1], tg[:, 0:1], ALU.mult).then_inc(e_scale, 1)
                dve.wait_ge(e_scale, 5)

                def code(b, par, again):
                    if again:
                        dve.wait_ge(o_split, b - 1)
                    dve.tensor_scalar(ocode[:, par, :, :], hid[:, :, bass.ds(b * T, T)], codes[:, SO:SO + 1], None,
                                      ALU.mult).then_inc(ocoded, 1)

                def split(b, par):
                    dve.wait_ge(o_rounded, b + 1)
                    dve.tensor_tensor(o_lo[:, par, :, :], ocode[:, par, :, :], o_hi[:, par, :, :].bitcast(F32),
                                      ALU.subtract).then_inc(o_split, 1)

                def add(b, par):
                    dve.wait_ge(down, b + 1)
                    for t in range(TT):
                        x = xres[:, bass.ds(b * TT + t, 1), :].rearrange("p o d -> p (o d)")
                        last = dve.scalar_tensor_tensor(out=x, in0=ybank[2 * par + t][:, 0:D], scalar=back[:, 0:1],
                                                        in1=x, op0=ALU.mult, op1=ALU.add)
                    last.then_inc(e_added, 1)

                code(0, 0, False)
                code(1, 1, False)
                split(0, 0)
                code(2, 0, True)
                split(1, 1)
                code(3, 1, True)
                with dve.Fori(0, B // 2 - 2) as j:
                    add(j * 2, 0)
                    split(j * 2 + 2, 0)
                    code(j * 2 + 4, 0, True)
                    add(j * 2 + 1, 1)
                    split(j * 2 + 3, 1)
                    code(j * 2 + 5, 1, True)
                for b in range(B - 4, B):
                    add(b, b % 2)
                    if b < B - 2:
                        split(b + 2, b % 2)

            @block.scalar
            def _(act):
                def hi(b, par, again):
                    act.wait_ge(ocoded, b + 1)
                    if again:
                        act.wait_ge(down, b - 1)
                    act.activation(o_hi[:, par, :, :], ocode[:, par, :, :], ACT.Copy).then_inc(o_rounded, 1)

                hi(0, 0, False)
                hi(1, 1, False)
                with act.Fori(1, B // 2) as j:
                    hi(j * 2, 0, True)
                    hi(j * 2 + 1, 1, True)

            @block.tensor
            def _(pe):
                def prod(b, par, again):
                    pe.wait_ge(o_split, b + 1)
                    if again:
                        pe.wait_ge(e_added, b - 1)
                    for t in range(TT):
                        for f in range(FT):
                            last = three_passes(nc, ybank[2 * par + t][:, 0:D],
                                                o_hi[:, par, f, t * P:(t + 1) * P],
                                                o_lo[:, par, f, t * P:(t + 1) * P],
                                                d_hi[:, f, :], d_lo[:, f, :], f == 0, f == FT - 1)
                    last.then_inc(down, 1)

                prod(0, 0, False)
                prod(1, 1, False)
                with pe.Fori(1, B // 2) as j:
                    prod(j * 2, 0, True)
                    prod(j * 2 + 1, 1, True)

    free_semaphores(nc, sems)


def butterfly_ffn(nc, env, w1_dram, w2_dram, up_bias, out_bias, gate, out):
    xres, banks, ident = env["xres"], env["banks"], env["ident"]
    T0, T1, X0, X1, S0, S1, O0, O1 = banks
    HT = HID1 // P
    G = NT * P // GT
    GTT = GT // P
    sems = []
    ctx = ExitStack()
    with ctx:
        def sb(name, shape, dt=F32):
            return ctx.enter_context(nc.sbuf_tensor(f"f1_{name}", shape, dt))

        def sem(name):
            sems.append(nc.alloc_semaphore(f"f1_{name}"))
            return sems[-1]

        w1_hi = sb("w1_hi", [P, DC, HID1], F32R)
        w1_lo = sb("w1_lo", [P, DC, HID1], F32R)
        w2_hi = sb("w2_hi", [P, HT, D], F32R)
        w2_lo = sb("w2_lo", [P, HT, D], F32R)
        b1 = sb("b1", [P, HT])
        gb = sb("gb", [P, D])
        tg = sb("tg", [P, 1])
        minus_half = sb("minus_half", [P, GTT])
        eps = sb("eps", [P, GTT])

        u = sb("u", [P, HT, D + 1])
        v = sb("v", [P, HT, D])
        ub = sb("ub", [P, HT])
        ob = sb("ob", [P, 2, D])
        u_in, v_in, small_in, turned, w1_rounded, w1_ready, v_rounded, w2_ready, g_done, ob_sum, gb_ready = (
            sem(x) for x in ("u_in", "v_in", "small_in", "turned", "w1_rounded", "w1_ready", "v_rounded", "w2_ready",
                             "g_done", "ob_sum", "gb_ready"))
        TURNS = [(c, t0) for c in range(DC) for t0 in range(0, HT, 4)]
        turn_banks = [X0, X1, S0, S1]

        mv = sb("mv", [P, GTT, 2])
        bn = sb("bn", [P, GTT, 6])
        var = sb("var", [P, GTT])
        rstd = sb("rstd", [P, GTT])
        xn = sb("xn", [P, GTT, D])
        xt_hi = sb("xt_hi", [P, 2, DC, GT], F32R)
        xt_lo = sb("xt_lo", [P, 2, DC, GT], F32R)
        h = sb("h", [P, 2, GT])
        h_hi = sb("h_hi", [P, 2, HT, GT], F32R)
        h_lo = sb("h_lo", [P, 2, HT, GT], F32R)
        ln_bn, ln_stats, ln_eps, ln_rstd, ln_xn, biased = (sem(x) for x in (
            "ln_bn", "ln_stats", "ln_eps", "ln_rstd", "ln_xn", "biased"))
        xt_ready, xt_rounded, xt_split = sem("xt_ready"), sem("xt_rounded"), sem("xt_split")
        h_sum, h_ready, h_rounded, h_split = sem("h_sum"), sem("h_ready"), sem("h_rounded"), sem("h_split")
        passed = sem("passed")
        cleared = sem("cleared")
        y_sum, y_added, y_sent = sem("y_sum"), sem("y_added"), sem("y_sent")
        hbank = [X0, X1, S0, S1]
        ybank = [O0, O1]

        def slots(eng, step):
            def slot(g, par, front=True, middle=True, back=True):
                for m in range(HT):
                    if isinstance(g, int) and g == -1 and m == 0:
                        step("w2", 0, 0, 0)
                    if front and m == 1:
                        step("ln", 0, g + 2, par)
                        if isinstance(g, int) and g == -2:
                            step("weights", 0, 0, 0)
                    if front and m == 6:
                        step("x", 0, g + 2, par)
                    if middle:
                        step("h", m, g + 1, 1 - par)
                for t in range(GTT):
                    if back:
                        step("y", t, g, par)

            slot(-2, 0, middle=False, back=False)
            slot(-1, 1, back=False)
            slot(0, 0)
            slot(1, 1)
            with eng.Fori(1, (G - 2) // 2) as j:
                slot(j * 2, 0)
                slot(j * 2 + 1, 1)
            slot(G - 2, 0, front=False)
            slot(G - 1, 1, front=False, middle=False)

        block = ctx.enter_context(nc.Block())

        @block.vector
        def _(dve):
            def xtile(g, t):
                return xres[:, bass.ds(g * GTT + t, 1), :].rearrange("p o d -> p (o d)")

            def step(what, n, g, par):
                if what == "ln":
                    for t in range(GTT):
                        last = dve.bn_stats(bn[:, t, :], xtile(g, t))
                    last.then_inc(ln_bn, 1)
                    dve.wait_ge(ln_bn, g + 1)
                    dve.sem_inc(passed, 1)
                    for t in range(GTT):
                        last = dve.bn_aggr(mv[:, t, :], bn[:, t, :])
                    last.then_inc(ln_stats, 1)
                    dve.wait_ge(ln_rstd, g + 1)
                    for t in range(GTT):
                        last = dve.tensor_scalar(xn[:, t, :], xtile(g, t), mv[:, t, 0:1], rstd[:, t:t + 1],
                                                 ALU.subtract, ALU.mult)
                    last.then_inc(ln_xn, 1)
                elif what == "weights":
                    for n, (c, t0) in enumerate(TURNS):
                        dve.wait_ge(w1_rounded, n + 1)
                        cols = slice(t0 * P, (t0 + 4) * P)
                        last = dve.tensor_tensor(w1_lo[:, c, cols], turn_banks[n][:, :],
                                                 w1_hi[:, c, cols].bitcast(F32), ALU.subtract)
                    dve.wait_ge(small_in, 48)
                    dve.tensor_tensor(b1[:], u[:, :, D], ub[:], ALU.add).then_inc(w1_ready, 1)
                elif what == "w2":
                    dve.tensor_tensor(gb[:], ob[:, 0, :], ob[:, 1, :], ALU.add).then_inc(ob_sum, 1)
                    dve.wait_ge(g_done, 1)
                    dve.wait_ge(ob_sum, 1)
                    dve.tensor_scalar(gb[:], gb[:], tg[:, 0:1], None, ALU.mult).then_inc(gb_ready, 1)
                    dve.wait_ge(v_rounded, 1)
                    dve.tensor_tensor(w2_lo[:], v[:], w2_hi[:].bitcast(F32), ALU.subtract).then_inc(w2_ready, 1)
                elif what == "x":
                    for c in range(DC):
                        dve.wait_ge(xt_rounded, g * DC + c + 1)
                        dve.tensor_tensor(xt_lo[:, par, c, :], (T0, T1)[c][:, :],
                                          xt_hi[:, par, c, :].bitcast(F32), ALU.subtract).then_inc(xt_split, 1)
                elif what == "h":
                    dve.wait_ge(h_ready, g * HT + n + 1)
                    dve.tensor_copy(h_hi[:, par, n, :], h[:, n % 2, :]).then_inc(h_rounded, 1)
                    dve.wait_ge(h_rounded, g * HT + n + 1)
                    dve.tensor_tensor(h_lo[:, par, n, :], h[:, n % 2, :], h_hi[:, par, n, :].bitcast(F32),
                                      ALU.subtract).then_inc(h_split, 1)
                elif what == "y":
                    dve.wait_ge(y_sum, g * GTT + n + 1)
                    dve.wait_ge(biased, g + 1)
                    x = xtile(g, n)
                    dve.scalar_tensor_tensor(out=x, in0=ybank[n % 2][:, 0:D], scalar=tg[:, 0:1], in1=x,
                                             op0=ALU.mult, op1=ALU.add).then_inc(y_added, 1)

            slots(dve, step)

        @block.gpsimd
        def _(pool):
            pool.memset(minus_half[:], -0.5).then_inc(cleared, 1)
            pool.memset(eps[:], LN_EPS).then_inc(cleared, 1)
            pool.wait_ge(cleared, 2)
            with pool.Fori(0, G) as g:
                pool.wait_ge(ln_stats, g + 1)
                pool.tensor_tensor(var[:], mv[:, :, 1], eps[:], ALU.add).then_inc(ln_eps, 1)
                pool.wait_ge(ln_eps, g + 1)
                pool.tensor_tensor(rstd[:], var[:], minus_half[:], ALU.pow).then_inc(ln_rstd, 1)
                pool.wait_ge(gb_ready, 1)
                pool.wait_ge(ln_xn, g + 1)
                for t in range(GTT):
                    x = xres[:, bass.ds(g * GTT + t, 1), :].rearrange("p o d -> p (o d)")
                    last = pool.tensor_tensor(x, x, gb[:], ALU.add)
                last.then_inc(biased, 1)

        @block.scalar
        def _(act):
            def step(what, n, g, par):
                if what == "x":
                    for c in range(DC):
                        act.wait_ge(xt_ready, g * DC + c + 1)
                        act.activation(xt_hi[:, par, c, :], (T0, T1)[c][:, :], ACT.Copy).then_inc(xt_rounded, 1)
                elif what == "weights":
                    for n, (c, t0) in enumerate(TURNS):
                        act.wait_ge(turned, n + 1)
                        act.activation(w1_hi[:, c, t0 * P:(t0 + 4) * P], turn_banks[n][:, :],
                                       ACT.Copy).then_inc(w1_rounded, 1)
                elif what == "w2":
                    act.wait_ge(small_in, 48)
                    act.activation(tg[:], tg[:], ACT.Tanh).then_inc(g_done, 1)
                    act.wait_ge(v_in, 16)
                    act.activation(w2_hi[:], v[:], ACT.Copy).then_inc(v_rounded, 1)
                elif what == "h":
                    if isinstance(g, int) and g == 0 and n == 0:
                        act.wait_ge(w1_ready, 1)
                    act.wait_ge(h_sum, g * HT + n + 1)
                    if not (isinstance(g, int) and g == 0 and n < 2):
                        act.wait_ge(h_split, g * HT + n - 1)
                    act.activation(h[:, n % 2, :], hbank[n % 4][:, :], ACT.Gelu,
                                   bias=b1[:, n:n + 1]).then_inc(h_ready, 1)

            slots(act, step)

        @block.tensor
        def _(pe):
            def step(what, n, g, par):
                if what == "weights":
                    pe.wait_ge(u_in, 16)
                    for n, (c, t0) in enumerate(TURNS):
                        for k in range(4):
                            last = pe.transpose(turn_banks[n][:, k * P:(k + 1) * P],
                                                u[:, t0 + k, c * P:(c + 1) * P], ident[:])
                        last.then_inc(turned, 1)
                elif what == "x":
                    pe.wait_ge(ln_xn, g + 1)
                    pe.wait_ge(xt_split, g * DC)
                    for c in range(DC):
                        for t in range(GTT):
                            last = pe.transpose((T0, T1)[c][:, t * P:(t + 1) * P], xn[:, t, c * P:(c + 1) * P],
                                                ident[:])
                        last.then_inc(xt_ready, 1)
                elif what == "h":
                    if isinstance(g, int) and g == 0 and n == 0:
                        pe.wait_ge(w1_ready, 1)
                    if n == 0:
                        pe.wait_ge(xt_split, (g + 1) * DC)
                    if not (isinstance(g, int) and g == 0 and n < 4):
                        pe.wait_ge(h_ready, g * HT + n - 3)
                    for c in range(DC):
                        last = three_passes(nc, hbank[n % 4][:, :], w1_hi[:, c, n * P:(n + 1) * P],
                                            w1_lo[:, c, n * P:(n + 1) * P], xt_hi[:, par, c, :],
                                            xt_lo[:, par, c, :], c == 0, c == DC - 1)
                    last.then_inc(h_sum, 1)
                elif what == "y":
                    if isinstance(g, int) and g == 0 and n == 0:
                        pe.wait_ge(w2_ready, 1)
                    if n == 0:
                        pe.wait_ge(h_split, (g + 1) * HT)
                    if not (isinstance(g, int) and g == 0 and n < 2):
                        pe.wait_ge(y_added, g * GTT + n - 1)
                    for m in range(HT):
                        last = three_passes(nc, ybank[n % 2][:, 0:D], h_hi[:, par, m, n * P:(n + 1) * P],
                                            h_lo[:, par, m, n * P:(n + 1) * P], w2_hi[:, m, :], w2_lo[:, m, :],
                                            m == 0, m == HT - 1)
                    last.then_inc(y_sum, 1)

            slots(pe, step)

        @block.sync
        def _(sp):
            sp.dma_start(u[:], w1_dram).then_inc(u_in, 16)
            sp.dma_start(ub[:], up_bias).then_inc(small_in, 16)
            sp.dma_start(ob[:], out_bias).then_inc(small_in, 16)
            sp.dma_start(tg[:], gate).then_inc(small_in, 16)
            sp.dma_start(v[:], w2_dram).then_inc(v_in, 16)
            with sp.Fori(0, G) as g:
                sp.wait_ge(y_added, (g + 1) * GTT)
                sp.dma_start(out[bass.ds(g * GT, GT), :].rearrange("(t p) d -> p t d", p=P),
                             xres[:, bass.ds(g * GTT, GTT), :]).then_inc(y_sent, 16)
            sp.wait_ge(y_sent, G * 16)


def build(nc, a, out):
    with ExitStack() as ctx:
        env = {"banks": [ctx.enter_context(nc.psum_tensor(f"bank{n}", [P, 512], F32)) for n in range(8)],
               "u_dram": nc.dram_tensor("u_spill", (P, HID0 // P, NT * P), F32, kind="Internal").ap()}
        env["ffn_weights"] = {name: a[name] for name in ("w_gate", "w_up", "w_down")}
        env["ffn_weights"]["quantised"] = nc.dram_tensor("w_quantised", (P, 3, HID0 * D // P), F32,
                                                         kind="Internal").ap()
        butterfly = {name: a[name] for name in ("top_coef", "low_coef", "flips", "w_con", "w_exp_t")}
        butterfly["w1_dram"] = nc.dram_tensor("w1_spill", (P, HID1 // P, D + 1), F32, kind="Internal").ap()
        butterfly["w2_dram"] = nc.dram_tensor("w2_spill", (P, HID1 // P, D), F32, kind="Internal").ap()
        for name, shape in (("xres", [P, NT, D]), ("ident", [P, P]), ("mean_all", [P, NT]),
                            ("rstd_all", [P, NT]), ("amax_x", [P, B])):
            env[name] = ctx.enter_context(nc.sbuf_tensor(name, shape, F32))
        for layer in range(2):
            env[f"mask{layer}"], env[f"pick{layer}"] = a[f"mask{layer}"], a[f"pick{layer}"]
        ident_in = ctx.enter_context(nc.semaphore("ident_in"))
        with nc.Block() as block:
            @block.sync
            def _(sp):
                sp.dma_start(env["ident"][:], a["ident"]).then_inc(ident_in, 16)
                sp.wait_ge(ident_in, 16)

        attention(nc, env, 0, 16, 256, a["wqkv0"], a["wo0"], a["bq0"], a["bk0"], a["bv0"], a["bo0"],
                  a["gx0"], a["ctx_t"], a["x"])
        quantised_ffn(nc, env, env["ffn_weights"]["quantised"], a["gf0"], butterfly)
        attention(nc, env, 1, 8, 512, a["wqkv1"], a["wo1"], None, None, None, a["bo1"], a["gx1"],
                  a["ctx_t"], None)
        butterfly_ffn(nc, env, butterfly["w1_dram"], butterfly["w2_dram"], a["up_bias"], a["out_bias"],
                      a["gf1"], out)


def kernel(**inputs):
    import numpy as np
    import concourse.bacc as bacc
    from concourse.bass_utils import run_bass_kernel_spmd

    v = {k: np.asarray(x) for k, x in inputs.items()}

    def rows(vec):
        return np.ascontiguousarray(np.broadcast_to(vec.reshape(1, -1), (P, vec.size)))

    def columns(vec):
        return np.ascontiguousarray(vec.reshape(-1, P).T)

    def stage_coefs(w, transposed):
        n = np.arange(HID1)
        got = []
        for stage in range(w.shape[0]):
            s = 1 << stage
            pair, hi = (n // (2 * s)) * s + n % s, (n // s) % 2
            other = w[stage, pair, 1 - hi, hi] if transposed else w[stage, pair, hi, 1 - hi]
            got.append(np.stack([w[stage, pair, hi, hi], other]))
        return np.stack(got)

    LOW = P.bit_length() - 1
    up, up_t = (stage_coefs(v["L1_ffn_up_weights"], k) for k in (False, True))
    down, down_t = (stage_coefs(v["L1_ffn_down_weights"], k) for k in (False, True))
    low = np.stack([np.concatenate([up_t[LOW - 1:LOW], up[LOW - 2::-1]]),
                    np.concatenate([down[0:1], down_t[1:LOW]])])
    top = np.stack([up[LOW:], down_t[:LOW - 1:-1]])
    lows = np.stack([np.arange(LOW)[::-1], np.arange(LOW)])

    def per_tile(c):
        return np.ascontiguousarray(np.moveaxis(c.reshape(c.shape[:3] + (-1, P)), -1, 0))

    m = np.arange(P)
    flips = np.ascontiguousarray((m[:, None, None, None] == (m[None, None, None, :] ^ (1 << lows)[None, :, :, None])
                                  ).astype(np.float32))

    def mask(d):
        return np.ascontiguousarray((np.arange(P)[:, None] // d == np.arange(P // d)[None, :]).astype(np.float32))

    def pick(heads):
        m = np.zeros((P, heads, S + 1), np.float32)
        for h in range(heads):
            m[h, h, :] = -1.0
        return m

    t = np.transpose
    arrays = {
        "x": v["x"].reshape(NT * P, D),
        "ctx_t": np.ascontiguousarray(v["ctx_1024"].reshape(B * S, D).T),
        "ident": np.eye(P, dtype=np.float32),
        "mask0": mask(16), "mask1": mask(64), "pick0": pick(16), "pick1": pick(8),
        "wqkv0": np.ascontiguousarray(np.concatenate([t(v["L0_xattn_Wq"]), t(v["L0_xattn_Wk"]), t(v["L0_xattn_Wv"])], 1)),
        "wo0": np.ascontiguousarray(t(v["L0_xattn_Wo"])),
        "bq0": columns(v["L0_xattn_bq"]), "bk0": columns(v["L0_xattn_bk"]),
        "bv0": rows(v["L0_xattn_bv"]), "bo0": rows(v["L0_xattn_bo"]),
        "wqkv1": np.ascontiguousarray(np.concatenate([v["L1_xattn_Wq"], v["L1_xattn_Wk"], v["L1_xattn_Wv"]], 1)),
        "wo1": v["L1_xattn_Wo"], "bo1": rows(v["L1_xattn_bo"]),
        "gx0": rows(v["g_xattn"][0:1]), "gx1": rows(v["g_xattn"][1:2]),
        "gf0": rows(v["g_ffn"][0:1]), "gf1": rows(v["g_ffn"][1:2]),
        "w_up": v["L0_ffn_w_up"], "w_gate": v["L0_ffn_w_gate"], "w_down": v["L0_ffn_w_down"],
        "w_exp_t": np.ascontiguousarray(np.concatenate([t(v["L1_ffn_W_exp"]), v["L1_ffn_b_exp"][:, None]], 1)),
        "w_con": v["L1_ffn_W_con"], "up_bias": columns(v["L1_ffn_up_bias"]),
        "top_coef": per_tile(top), "low_coef": per_tile(low), "flips": flips,
        "out_bias": np.ascontiguousarray(np.stack([rows(v["L1_ffn_b_con"]), rows(v["L1_ffn_down_bias"])], 1)),
    }
    nc = bacc.Bacc("TRN2", target_bir_lowering=False, num_devices=1)
    feed, args = {}, {}
    for name, x in arrays.items():
        feed[f"in_{name}"] = np.ascontiguousarray(x)
        args[name] = nc.dram_tensor(f"in_{name}", x.shape, mybir.dt.from_np(x.dtype), kind="ExternalInput").ap()
    out = nc.dram_tensor("out_x", (NT * P, D), F32, kind="ExternalOutput").ap()
    build(nc, args, out)
    r = run_bass_kernel_spmd(nc, [feed], core_ids=[0])
    return r.results[0]["out_x"].reshape(B, T, D)
```
